# Optimizing a Trainium2 kernel written in Bass

```python
import numpy as np
import jax
import jax.numpy as jnp

def _softmax(x, axis=-1):
    return jax.nn.softmax(x, axis=axis)

def _gelu(x):
    return jax.nn.gelu(x, approximate=True)

def _silu(x):
    return jax.nn.silu(x)

def _sigmoid(x):
    return jax.nn.sigmoid(x)

def _layernorm(x, axis=-1, eps=1e-05):
    m = jnp.mean(x, axis=axis, keepdims=True)
    v = jnp.var(x, axis=axis, keepdims=True)
    return (x - m) / jnp.sqrt(v + eps)

def _scatter_add(tgt, idx, src, axis=0):
    return tgt.at[idx].add(src)

def _segment_sum(src, seg, n):
    return jax.ops.segment_sum(src, seg, n)
kernel_name = 'mk_decoder_preln_d4_seqx_r8_60c2d7'

def setup_inputs(seed: int=0):
    np.random.seed(seed)
    _w = jnp.asarray

    def _rec_inputs():
        import jax
        import jax.numpy as jnp
        _rk = jax.random.key(seed)
        x = 7.22e-05 + 1 * jax.random.normal(jax.random.fold_in(_rk, 1), (8, 256, 128), jnp.float32)
        _lenS = 256 - jax.random.randint(jax.random.fold_in(_rk, 7), (8,), 0, max(1, 256 // 4) + 1, jnp.int32)
        _lenS2 = 64 - jax.random.randint(jax.random.fold_in(_rk, 8), (8,), 0, max(1, 64 // 4) + 1, jnp.int32)
        _ctx_1024P = jax.random.normal(jax.random.fold_in(_rk, 11), (8, 16, 128), jnp.float32)
        _ctx_1024c = jax.random.dirichlet(jax.random.fold_in(_rk, 511), 0.3 * jnp.ones((16,), jnp.float32), (8, 64))
        _ctx_1024t = jnp.einsum('bsk,bkd->bsd', _ctx_1024c, _ctx_1024P)
        _ctx_1024t = _ctx_1024t * jax.lax.rsqrt(jnp.mean(jnp.square(_ctx_1024t)) + 1e-12) * 0.953939
        ctx_1024 = 4.13588e-05 + 0.999923 * (_ctx_1024t + 0.3 * jax.random.normal(jax.random.fold_in(_rk, 611), (8, 64, 128), jnp.float32))
        _validS = jnp.arange(256)[None, :] < _lenS[:, None]
        _validS2 = jnp.arange(64)[None, :] < _lenS2[:, None]
        _causal = jnp.tril(jnp.ones((256, 256), dtype=bool))
        mask_SxS2_bk1 = jnp.broadcast_to(_validS2[0:1, :], (256, 64))
        mask_BxS2_bk0 = jnp.logical_not(jnp.broadcast_to(_validS2[:, :], (8, 64)))
        mask_BxS2_bf1 = jnp.ones((8, 64), dtype=bool)
        return (x, ctx_1024, mask_SxS2_bk1, mask_BxS2_bk0, mask_BxS2_bf1)
    x, ctx_1024, mask_SxS2_bk1, mask_BxS2_bk0, mask_BxS2_bf1 = _rec_inputs()

    def _L0_attn_setup():
        import math
        import jax, jax.numpy as jnp
        import numpy as np
        B, S, DIM, HEADS = (1, 256, 128, 16)
        HEAD_DIM = DIM // HEADS
        key = jax.random.key(seed)
        ks = jax.random.split(key, 6)
        scale = DIM ** (-0.5)
        x = jax.random.normal(ks[0], (B, S, DIM), jnp.float32)
        wq = jax.random.normal(ks[1], (DIM, DIM), jnp.float32) * scale
        wk = jax.random.normal(ks[2], (DIM, DIM), jnp.float32) * scale
        wv = jax.random.normal(ks[3], (DIM, DIM), jnp.float32) * scale
        wo = jax.random.normal(ks[4], (DIM, DIM), jnp.float32) * scale
        pope_bias = -jax.random.uniform(ks[5], (HEADS, HEAD_DIM), jnp.float32) * 3.0
        return {'x': x, 'wq': wq, 'wk': wk, 'wv': wv, 'wo': wo, 'pope_bias': pope_bias}
    _L0_attn_all = _L0_attn_setup()
    _L0_attn_in = {k: v for k, v in _L0_attn_all.items() if k in ('wq', 'wk', 'wv', 'wo', 'pope_bias')}
    del _L0_attn_all

    def _L0_xattn_setup():
        import jax, jax.numpy as jnp
        import numpy as np
        B, S, D = (4, 256, 128)
        key = jax.random.key(seed)
        ks = jax.random.split(key, 9)
        inp = {'encodings_q': jax.random.normal(ks[0], (B, S, D), dtype=jnp.float32), 'encodings_k': jax.random.normal(ks[1], (B, S, D), dtype=jnp.float32), 'encodings_v': jax.random.normal(ks[2], (B, S, D), dtype=jnp.float32), 'mask': jnp.triu(jnp.ones((S, S), dtype=bool), k=1), 'W_q': jax.random.normal(ks[3], (D, D), dtype=jnp.float32) / np.sqrt(D), 'b_q': jax.random.normal(ks[4], (D,), dtype=jnp.float32) * 0.01, 'W_k': jax.random.normal(ks[5], (D, D), dtype=jnp.float32) / np.sqrt(D), 'b_k': jax.random.normal(ks[6], (D,), dtype=jnp.float32) * 0.01, 'W_v': jax.random.normal(ks[7], (D, D), dtype=jnp.float32) / np.sqrt(D), 'b_v': jax.random.normal(ks[8], (D,), dtype=jnp.float32) * 0.01}
        return inp
    _L0_xattn_all = _L0_xattn_setup()
    _L0_xattn_in = {k: v for k, v in _L0_xattn_all.items() if k in ('W_q', 'b_q', 'W_k', 'b_k', 'W_v', 'b_v')}
    del _L0_xattn_all

    def _L0_ffn_setup():
        import jax, jax.numpy as jnp
        import numpy as np
        B, S, H, F, E, K = (2, 256, 128, 512, 8, 2)

        def _ln(x, g, b, eps=1e-05):
            m = jnp.mean(x, axis=-1, keepdims=True)
            v = jnp.var(x, axis=-1, keepdims=True)
            return (x - m) / jnp.sqrt(v + eps) * g + b

        def _gelu(x):
            return jax.nn.gelu(x, approximate=False)
        key = jax.random.key(seed)
        ks = jax.random.split(key, 12)
        F2 = F // 2
        return {'hidden_states': jax.random.normal(ks[0], (B, S, H), jnp.float32), 'ln_g': jnp.ones((H,), jnp.float32), 'ln_b': jnp.zeros((H,), jnp.float32), 'router_w': jax.random.normal(ks[1], (H, E), jnp.float32) * 0.01, 'up_W': jax.random.normal(ks[2], (E, H, F), jnp.float32) * 0.02, 'up_b': jnp.zeros((E, F), jnp.float32), 'down_W': jax.random.normal(ks[3], (E, F, H), jnp.float32) * 0.02, 'down_b': jnp.zeros((E, H), jnp.float32), 'spec0_W': jax.random.normal(ks[4], (2, F, F), jnp.float32) * 0.02, 'spec0_b': jnp.zeros((2, F), jnp.float32), 'ln0_g': jnp.ones((2, F), jnp.float32), 'ln0_b': jnp.zeros((2, F), jnp.float32), 'spec1a_W': jax.random.normal(ks[5], (2, F, F2), jnp.float32) * 0.02, 'spec1a_b': jnp.zeros((2, F2), jnp.float32), 'spec1b_W': jax.random.normal(ks[6], (2, F2, F), jnp.float32) * 0.02, 'spec1b_b': jnp.zeros((2, F), jnp.float32), 'ln1_g': jnp.ones((2, F), jnp.float32), 'ln1_b': jnp.zeros((2, F), jnp.float32), 'spec2_W': jax.random.normal(ks[7], (2, F, F), jnp.float32) * 0.02, 'spec2_b': jnp.zeros((2, F), jnp.float32)}
    _L0_ffn_all = _L0_ffn_setup()
    _L0_ffn_in = {k: v for k, v in _L0_ffn_all.items() if k in ('ln_g', 'ln_b', 'router_w', 'up_W', 'up_b', 'down_W', 'down_b', 'spec0_W', 'spec0_b', 'ln0_g', 'ln0_b', 'spec1a_W', 'spec1a_b', 'spec1b_W', 'spec1b_b', 'ln1_g', 'ln1_b', 'spec2_W', 'spec2_b')}
    del _L0_ffn_all

    def _L1_attn_setup():
        import jax, jax.numpy as jnp
        import numpy as np
        D_MODEL = 128
        D_STATE = 16
        DT_MIN = 0.001
        DT_MAX = 0.02
        key = jax.random.key(seed)
        ks = jax.random.split(key, 5)
        B, L = (2, 256)
        u = jax.random.normal(ks[0], (B, L, D_MODEL), dtype=jnp.float32)
        A_log = jnp.log(jnp.broadcast_to(jnp.arange(1, D_STATE + 1, dtype=jnp.float32), (D_MODEL, D_STATE)))
        B_p = jax.random.normal(ks[1], (D_MODEL, D_STATE), dtype=jnp.float32) * 0.01
        C_p = jax.random.normal(ks[2], (D_MODEL, D_STATE), dtype=jnp.float32) * 0.01
        D_p = jnp.ones((D_MODEL,), dtype=jnp.float32)
        W_dt = jax.random.normal(ks[3], (D_MODEL, D_MODEL), dtype=jnp.float32) * (1.0 / np.sqrt(D_MODEL))
        b_dt = jax.random.normal(ks[4], (D_MODEL,), dtype=jnp.float32) * 0.01
        return {'u': u, 'A_log': A_log, 'B_p': B_p, 'C_p': C_p, 'D_p': D_p, 'W_dt': W_dt, 'b_dt': b_dt}
    _L1_attn_all = _L1_attn_setup()
    _L1_attn_in = {k: v for k, v in _L1_attn_all.items() if k in ('A_log', 'B_p', 'C_p', 'D_p', 'W_dt', 'b_dt')}
    del _L1_attn_all

    def _L1_xattn_setup():
        import jax, jax.numpy as jnp
        import numpy as np
        DIM = 128
        HEADS = 16
        HEAD_DIM = DIM // HEADS
        SCALE = HEAD_DIM ** (-0.5)
        B, N_TGT, N_SRC = (4, 128, 256)
        key = jax.random.key(seed)
        ks = jax.random.split(key, 8)
        s = 0.02
        tgt = jax.random.normal(ks[0], (B, N_TGT, DIM), dtype=jnp.float32)
        src = jax.random.normal(ks[1], (B, N_SRC, DIM), dtype=jnp.float32)
        src_padded_mask = jnp.broadcast_to(jnp.arange(N_SRC) >= N_SRC - 64, (B, N_SRC))
        q_w = jax.random.normal(ks[2], (DIM, DIM), dtype=jnp.float32) * s
        q_b = jnp.zeros((DIM,), dtype=jnp.float32)
        kv_w = jax.random.normal(ks[3], (2 * DIM, DIM), dtype=jnp.float32) * s
        kv_b = jnp.zeros((2 * DIM,), dtype=jnp.float32)
        proj_w = jax.random.normal(ks[4], (DIM, DIM), dtype=jnp.float32) * s
        proj_b = jnp.zeros((DIM,), dtype=jnp.float32)
        return {'tgt': tgt, 'src': src, 'src_padded_mask': src_padded_mask, 'q_w': q_w, 'q_b': q_b, 'kv_w': kv_w, 'kv_b': kv_b, 'proj_w': proj_w, 'proj_b': proj_b}
    _L1_xattn_all = _L1_xattn_setup()
    _L1_xattn_in = {k: v for k, v in _L1_xattn_all.items() if k in ('q_w', 'q_b', 'kv_w', 'kv_b', 'proj_w', 'proj_b')}
    del _L1_xattn_all

    def _L1_ffn_setup():
        import jax, jax.numpy as jnp
        import numpy as np
        HIDDEN = 128
        INNER = 512

        def _weight_quant(w):
            scale = 1.0 / jnp.clip(jnp.mean(jnp.abs(w)), 1e-05)
            wq = jnp.clip(jnp.round(w * scale), -1.0, 1.0) / scale
            return w + jax.lax.stop_gradient(wq - w)

        def _act_quant(x):
            scale = 127.0 / jnp.clip(jnp.max(jnp.abs(x), axis=-1, keepdims=True), 1e-05)
            xq = jnp.clip(jnp.round(x * scale), -128.0, 127.0) / scale
            return x + jax.lax.stop_gradient(xq - x)

        def _bitlinear(x, w):
            return jnp.einsum('bsi,oi->bso', _act_quant(x), _weight_quant(w))
        key = jax.random.key(seed)
        k0, k1, k2, k3 = jax.random.split(key, 4)
        x = jax.random.normal(k0, (4, 256, HIDDEN), dtype=jnp.float32)
        w_gate = jax.random.normal(k1, (INNER, HIDDEN), dtype=jnp.float32) / np.sqrt(HIDDEN)
        w_up = jax.random.normal(k2, (INNER, HIDDEN), dtype=jnp.float32) / np.sqrt(HIDDEN)
        w_down = jax.random.normal(k3, (HIDDEN, INNER), dtype=jnp.float32) / np.sqrt(INNER)
        return {'x': x, 'w_gate': w_gate, 'w_up': w_up, 'w_down': w_down}
    _L1_ffn_all = _L1_ffn_setup()
    _L1_ffn_in = {k: v for k, v in _L1_ffn_all.items() if k in ('w_gate', 'w_up', 'w_down')}
    del _L1_ffn_all

    def _L2_attn_setup():
        import jax, jax.numpy as jnp
        import numpy as np
        NH = 16
        NKV = 4
        D = 64
        BLK = 64
        KSEL = 16
        THETA = 10000.0

        def _rotate_half(x):
            x1, x2 = jnp.split(x, 2, axis=-1)
            return jnp.concatenate([-x2, x1], axis=-1)
        key = jax.random.key(seed)
        ks = jax.random.split(key, 8)
        B, S, Hm = (2, 256, 128)
        s = 0.02
        return {'hidden_states': jax.random.normal(ks[0], (B, S, Hm), jnp.float32), 'Wq': jax.random.normal(ks[1], (NH * D, Hm), jnp.float32) * s, 'Wk': jax.random.normal(ks[2], (NKV * D, Hm), jnp.float32) * s, 'Wv': jax.random.normal(ks[3], (NKV * D, Hm), jnp.float32) * s, 'Wo': jax.random.normal(ks[4], (Hm, NH * D), jnp.float32) * s, 'Wkc': jax.random.normal(ks[5], (D // 4, D), jnp.float32) * s, 'Wg_slc': jax.random.normal(ks[6], (NH, Hm), jnp.float32) * s, 'Wg_swa': jax.random.normal(ks[7], (NH, Hm), jnp.float32) * s}
    _L2_attn_all = _L2_attn_setup()
    _L2_attn_in = {k: v for k, v in _L2_attn_all.items() if k in ('Wq', 'Wk', 'Wv', 'Wo', 'Wkc', 'Wg_slc', 'Wg_swa')}
    del _L2_attn_all

    def _L2_xattn_setup():
        import jax, jax.numpy as jnp
        import numpy as np
        import math
        B, S, D, H = (1, 256, 128, 16)
        DK = D // H
        DH = 64
        LOG_T_MIN = math.log(0.1)
        LOG_T_MAX = math.log(10.0)

        def _linear(x, W, b):
            return x @ W.T + b
        key = jax.random.key(seed)
        ks = jax.random.split(key, 20)
        p = 0.02
        return {'query': jax.random.normal(ks[0], (B, S, D), jnp.float32), 'key': jax.random.normal(ks[1], (B, S, D), jnp.float32), 'value': jax.random.normal(ks[2], (B, S, D), jnp.float32), 'Wq': jax.random.normal(ks[3], (D, D), jnp.float32) * p, 'bq': jax.random.normal(ks[4], (D,), jnp.float32) * p, 'Wk': jax.random.normal(ks[5], (D, D), jnp.float32) * p, 'bk': jax.random.normal(ks[6], (D,), jnp.float32) * p, 'Wv': jax.random.normal(ks[7], (D, D), jnp.float32) * p, 'bv': jax.random.normal(ks[8], (D,), jnp.float32) * p, 'Wo': jax.random.normal(ks[9], (D, D), jnp.float32) * p, 'bo': jax.random.normal(ks[10], (D,), jnp.float32) * p, 'w1': jax.random.normal(ks[11], (DH, 3), jnp.float32) * 0.3, 'b1': jax.random.normal(ks[12], (DH,), jnp.float32) * 0.1, 'w2': jax.random.normal(ks[13], (DH, DH), jnp.float32) * 0.1, 'b2': jax.random.normal(ks[14], (DH,), jnp.float32) * 0.1, 'w3': jax.random.normal(ks[15], (1, DH), jnp.float32) * 0.1, 'b3': jnp.full((1,), (LOG_T_MIN + LOG_T_MAX) / 2, jnp.float32)}
    _L2_xattn_all = _L2_xattn_setup()
    _L2_xattn_in = {k: v for k, v in _L2_xattn_all.items() if k in ('Wq', 'bq', 'Wk', 'bk', 'Wv', 'bv', 'Wo', 'bo', 'w1', 'b1', 'w2', 'b2', 'w3', 'b3')}
    del _L2_xattn_all

    def _L2_ffn_setup():
        import jax, jax.numpy as jnp
        import numpy as np
        CAPACITY_FACTOR = 0.5
        NUM_HEADS = 16
        key = jax.random.key(seed)
        ks = jax.random.split(key, 6)
        B, N, D = (4, 512, 128)
        s = 1.0 / np.sqrt(D)
        return {'token_inputs': jax.random.normal(ks[0], (B, N, D), jnp.float32), 'Wg': jax.random.normal(ks[1], (D, 1), jnp.float32) * s, 'Wq': jax.random.normal(ks[2], (D, D), jnp.float32) * s, 'Wk': jax.random.normal(ks[3], (D, D), jnp.float32) * s, 'Wv': jax.random.normal(ks[4], (D, D), jnp.float32) * s, 'Wo': jax.random.normal(ks[5], (D, D), jnp.float32) * s}
    _L2_ffn_all = _L2_ffn_setup()
    _L2_ffn_in = {k: v for k, v in _L2_ffn_all.items() if k in ('Wg', 'Wq', 'Wk', 'Wv', 'Wo')}
    del _L2_ffn_all

    def _L3_attn_setup():
        import jax, jax.numpy as jnp
        import numpy as np
        B, S, D = (2, 256, 128)
        N_HEADS, N_KV_HEADS = (16, 4)
        HEAD_DIM = D // N_HEADS
        KV_GROUPS = N_HEADS // N_KV_HEADS
        ROPE_BASE = 10000.0

        def _apply_rope(t, cos, sin):
            t1, t2 = jnp.split(t, 2, axis=-1)
            return jnp.concatenate([t1 * cos - t2 * sin, t1 * sin + t2 * cos], axis=-1)
        key = jax.random.key(seed)
        ks = jax.random.split(key, 5)
        s = 0.02
        return {'x': jax.random.normal(ks[0], (B, S, D), dtype=jnp.float32), 'wq': jax.random.normal(ks[1], (D, D), dtype=jnp.float32) * s, 'wk': jax.random.normal(ks[2], (D, N_KV_HEADS * HEAD_DIM), dtype=jnp.float32) * s, 'wv': jax.random.normal(ks[3], (D, N_KV_HEADS * HEAD_DIM), dtype=jnp.float32) * s, 'wo': jax.random.normal(ks[4], (D, D), dtype=jnp.float32) * s}
    _L3_attn_all = _L3_attn_setup()
    _L3_attn_in = {k: v for k, v in _L3_attn_all.items() if k in ('wq', 'wk', 'wv', 'wo')}
    del _L3_attn_all

    def _L3_xattn_setup():
        import jax, jax.numpy as jnp
        import numpy as np
        DIM = 128
        HEADS = 16
        DIM_HEAD = 64
        INNER = HEADS * DIM_HEAD
        EPS = 1e-05

        def layer_norm(x, gamma, beta):
            mu = jnp.mean(x, axis=-1, keepdims=True)
            var = jnp.var(x, axis=-1, keepdims=True)
            return (x - mu) * jax.lax.rsqrt(var + EPS) * gamma + beta
        key = jax.random.key(seed)
        ks = jax.random.split(key, 8)
        b, n, ctx = (2, 256, 256)
        x = jax.random.normal(ks[0], (b, n, DIM), dtype=jnp.float32)
        context = jax.random.normal(ks[1], (b, ctx, DIM), dtype=jnp.float32)
        context_mask = jnp.ones((b, ctx), dtype=bool)
        g1 = jnp.ones((DIM,), jnp.float32)
        b1 = jnp.zeros((DIM,), jnp.float32)
        g2 = jnp.ones((DIM,), jnp.float32)
        b2 = jnp.zeros((DIM,), jnp.float32)
        s = 1.0 / np.sqrt(DIM)
        Wq = jax.random.normal(ks[2], (DIM, INNER), jnp.float32) * s
        Wkv = jax.random.normal(ks[3], (DIM, 2 * INNER), jnp.float32) * s
        Wo = jax.random.normal(ks[4], (INNER, DIM), jnp.float32) * (1.0 / np.sqrt(INNER))
        bo = jnp.zeros((DIM,), jnp.float32)
        return dict(x=x, context=context, context_mask=context_mask, g1=g1, b1=b1, g2=g2, b2=b2, Wq=Wq, Wkv=Wkv, Wo=Wo, bo=bo)
    _L3_xattn_all = _L3_xattn_setup()
    _L3_xattn_in = {k: v for k, v in _L3_xattn_all.items() if k in ('g1', 'b1', 'g2', 'b2', 'Wq', 'Wkv', 'Wo', 'bo')}
    del _L3_xattn_all

    def _L3_ffn_setup():
        import math
        import jax, jax.numpy as jnp
        import numpy as np
        B, S, D, F, E = (8, 256, 128, 512, 8)
        CAPACITY_FACTOR = 1.0
        key = jax.random.key(seed)
        k1, k2, k3, k4 = jax.random.split(key, 4)
        x = jax.random.normal(k1, (B, S, D), dtype=jnp.float32)
        Wr = jax.random.normal(k2, (D, E), dtype=jnp.float32) * (1.0 / math.sqrt(D))
        W1 = jax.random.normal(k3, (E, D, F), dtype=jnp.float32) * (1.0 / math.sqrt(D))
        W2 = jax.random.normal(k4, (E, F, D), dtype=jnp.float32) * (1.0 / math.sqrt(F))
        return {'x': x, 'Wr': Wr, 'W1': W1, 'W2': W2}
    _L3_ffn_all = _L3_ffn_setup()
    _L3_ffn_in = {k: v for k, v in _L3_ffn_all.items() if k in ('Wr', 'W1', 'W2')}
    del _L3_ffn_all
    return {'x': x, 'ctx_1024': ctx_1024, 'mask_SxS2_bk1': mask_SxS2_bk1, 'mask_BxS2_bk0': mask_BxS2_bk0, 'mask_BxS2_bf1': mask_BxS2_bf1, 'L0_attn_wq': _L0_attn_in['wq'], 'L0_attn_wk': _L0_attn_in['wk'], 'L0_attn_wv': _L0_attn_in['wv'], 'L0_attn_wo': _L0_attn_in['wo'], 'L0_attn_pope_bias': _L0_attn_in['pope_bias'], 'L0_xattn_W_q': _L0_xattn_in['W_q'], 'L0_xattn_b_q': _L0_xattn_in['b_q'], 'L0_xattn_W_k': _L0_xattn_in['W_k'], 'L0_xattn_b_k': _L0_xattn_in['b_k'], 'L0_xattn_W_v': _L0_xattn_in['W_v'], 'L0_xattn_b_v': _L0_xattn_in['b_v'], 'L0_ffn_ln_g': _L0_ffn_in['ln_g'], 'L0_ffn_ln_b': _L0_ffn_in['ln_b'], 'L0_ffn_router_w': _L0_ffn_in['router_w'], 'L0_ffn_up_W': _L0_ffn_in['up_W'], 'L0_ffn_up_b': _L0_ffn_in['up_b'], 'L0_ffn_down_W': _L0_ffn_in['down_W'], 'L0_ffn_down_b': _L0_ffn_in['down_b'], 'L0_ffn_spec0_W': _L0_ffn_in['spec0_W'], 'L0_ffn_spec0_b': _L0_ffn_in['spec0_b'], 'L0_ffn_ln0_g': _L0_ffn_in['ln0_g'], 'L0_ffn_ln0_b': _L0_ffn_in['ln0_b'], 'L0_ffn_spec1a_W': _L0_ffn_in['spec1a_W'], 'L0_ffn_spec1a_b': _L0_ffn_in['spec1a_b'], 'L0_ffn_spec1b_W': _L0_ffn_in['spec1b_W'], 'L0_ffn_spec1b_b': _L0_ffn_in['spec1b_b'], 'L0_ffn_ln1_g': _L0_ffn_in['ln1_g'], 'L0_ffn_ln1_b': _L0_ffn_in['ln1_b'], 'L0_ffn_spec2_W': _L0_ffn_in['spec2_W'], 'L0_ffn_spec2_b': _L0_ffn_in['spec2_b'], 'L1_attn_A_log': _L1_attn_in['A_log'], 'L1_attn_B_p': _L1_attn_in['B_p'], 'L1_attn_C_p': _L1_attn_in['C_p'], 'L1_attn_D_p': _L1_attn_in['D_p'], 'L1_attn_W_dt': _L1_attn_in['W_dt'], 'L1_attn_b_dt': _L1_attn_in['b_dt'], 'L1_xattn_q_w': _L1_xattn_in['q_w'], 'L1_xattn_q_b': _L1_xattn_in['q_b'], 'L1_xattn_kv_w': _L1_xattn_in['kv_w'], 'L1_xattn_kv_b': _L1_xattn_in['kv_b'], 'L1_xattn_proj_w': _L1_xattn_in['proj_w'], 'L1_xattn_proj_b': _L1_xattn_in['proj_b'], 'L1_ffn_w_gate': _L1_ffn_in['w_gate'], 'L1_ffn_w_up': _L1_ffn_in['w_up'], 'L1_ffn_w_down': _L1_ffn_in['w_down'], 'L2_attn_Wq': _L2_attn_in['Wq'], 'L2_attn_Wk': _L2_attn_in['Wk'], 'L2_attn_Wv': _L2_attn_in['Wv'], 'L2_attn_Wo': _L2_attn_in['Wo'], 'L2_attn_Wkc': _L2_attn_in['Wkc'], 'L2_attn_Wg_slc': _L2_attn_in['Wg_slc'], 'L2_attn_Wg_swa': _L2_attn_in['Wg_swa'], 'L2_xattn_Wq': _L2_xattn_in['Wq'], 'L2_xattn_bq': _L2_xattn_in['bq'], 'L2_xattn_Wk': _L2_xattn_in['Wk'], 'L2_xattn_bk': _L2_xattn_in['bk'], 'L2_xattn_Wv': _L2_xattn_in['Wv'], 'L2_xattn_bv': _L2_xattn_in['bv'], 'L2_xattn_Wo': _L2_xattn_in['Wo'], 'L2_xattn_bo': _L2_xattn_in['bo'], 'L2_xattn_w1': _L2_xattn_in['w1'], 'L2_xattn_b1': _L2_xattn_in['b1'], 'L2_xattn_w2': _L2_xattn_in['w2'], 'L2_xattn_b2': _L2_xattn_in['b2'], 'L2_xattn_w3': _L2_xattn_in['w3'], 'L2_xattn_b3': _L2_xattn_in['b3'], 'L2_ffn_Wg': _L2_ffn_in['Wg'], 'L2_ffn_Wq': _L2_ffn_in['Wq'], 'L2_ffn_Wk': _L2_ffn_in['Wk'], 'L2_ffn_Wv': _L2_ffn_in['Wv'], 'L2_ffn_Wo': _L2_ffn_in['Wo'], 'L3_attn_wq': _L3_attn_in['wq'], 'L3_attn_wk': _L3_attn_in['wk'], 'L3_attn_wv': _L3_attn_in['wv'], 'L3_attn_wo': _L3_attn_in['wo'], 'L3_xattn_g1': _L3_xattn_in['g1'], 'L3_xattn_b1': _L3_xattn_in['b1'], 'L3_xattn_g2': _L3_xattn_in['g2'], 'L3_xattn_b2': _L3_xattn_in['b2'], 'L3_xattn_Wq': _L3_xattn_in['Wq'], 'L3_xattn_Wkv': _L3_xattn_in['Wkv'], 'L3_xattn_Wo': _L3_xattn_in['Wo'], 'L3_xattn_bo': _L3_xattn_in['bo'], 'L3_ffn_Wr': _L3_ffn_in['Wr'], 'L3_ffn_W1': _L3_ffn_in['W1'], 'L3_ffn_W2': _L3_ffn_in['W2']}

def reference(x, ctx_1024, mask_SxS2_bk1, mask_BxS2_bk0, mask_BxS2_bf1, L0_attn_wq, L0_attn_wk, L0_attn_wv, L0_attn_wo, L0_attn_pope_bias, L0_xattn_W_q, L0_xattn_b_q, L0_xattn_W_k, L0_xattn_b_k, L0_xattn_W_v, L0_xattn_b_v, L0_ffn_ln_g, L0_ffn_ln_b, L0_ffn_router_w, L0_ffn_up_W, L0_ffn_up_b, L0_ffn_down_W, L0_ffn_down_b, L0_ffn_spec0_W, L0_ffn_spec0_b, L0_ffn_ln0_g, L0_ffn_ln0_b, L0_ffn_spec1a_W, L0_ffn_spec1a_b, L0_ffn_spec1b_W, L0_ffn_spec1b_b, L0_ffn_ln1_g, L0_ffn_ln1_b, L0_ffn_spec2_W, L0_ffn_spec2_b, L1_attn_A_log, L1_attn_B_p, L1_attn_C_p, L1_attn_D_p, L1_attn_W_dt, L1_attn_b_dt, L1_xattn_q_w, L1_xattn_q_b, L1_xattn_kv_w, L1_xattn_kv_b, L1_xattn_proj_w, L1_xattn_proj_b, L1_ffn_w_gate, L1_ffn_w_up, L1_ffn_w_down, L2_attn_Wq, L2_attn_Wk, L2_attn_Wv, L2_attn_Wo, L2_attn_Wkc, L2_attn_Wg_slc, L2_attn_Wg_swa, L2_xattn_Wq, L2_xattn_bq, L2_xattn_Wk, L2_xattn_bk, L2_xattn_Wv, L2_xattn_bv, L2_xattn_Wo, L2_xattn_bo, L2_xattn_w1, L2_xattn_b1, L2_xattn_w2, L2_xattn_b2, L2_xattn_w3, L2_xattn_b3, L2_ffn_Wg, L2_ffn_Wq, L2_ffn_Wk, L2_ffn_Wv, L2_ffn_Wo, L3_attn_wq, L3_attn_wk, L3_attn_wv, L3_attn_wo, L3_xattn_g1, L3_xattn_b1, L3_xattn_g2, L3_xattn_b2, L3_xattn_Wq, L3_xattn_Wkv, L3_xattn_Wo, L3_xattn_bo, L3_ffn_Wr, L3_ffn_W1, L3_ffn_W2):
    import jax
    import jax.numpy as jnp

    def _L0_attn_ref(x, wq, wk, wv, wo, pope_bias):
        import math
        import jax, jax.numpy as jnp
        import numpy as np
        B, S, DIM, HEADS = (1, 256, 128, 16)
        HEAD_DIM = DIM // HEADS
        B_, S_, C = x.shape
        H = HEADS
        D = C // H
        q = jnp.einsum('bsc,oc->bso', x, wq).reshape(B_, S_, H, D).transpose(0, 2, 1, 3)
        k = jnp.einsum('bsc,oc->bso', x, wk).reshape(B_, S_, H, D).transpose(0, 2, 1, 3)
        v = jnp.einsum('bsc,oc->bso', x, wv).reshape(B_, S_, H, D).transpose(0, 2, 1, 3)
        inv_freqs = 10000.0 ** (-(jnp.arange(D, dtype=jnp.float32) / D))
        pos = jnp.arange(S_, dtype=jnp.float32)
        freqs = pos[:, None] * inv_freqs[None, :]
        bias = jnp.clip(pope_bias, -2.0 * math.pi, 0.0)
        freqs_with_bias = freqs[None, :, :] + bias[:, None, :]
        q_mag = jax.nn.softplus(q)
        k_mag = jax.nn.softplus(k)
        qp = freqs[None, None, :, :]
        kp = freqs_with_bias[None, :, :, :]
        q_embed = jnp.stack([q_mag * jnp.cos(qp), q_mag * jnp.sin(qp)], axis=-1).reshape(B_, H, S_, 2 * D)
        k_embed = jnp.stack([k_mag * jnp.cos(kp), k_mag * jnp.sin(kp)], axis=-1).reshape(B_, H, S_, 2 * D)
        scores = jnp.einsum('bhsd,bhtd->bhst', q_embed, k_embed) / D ** 0.5
        attn = jax.nn.softmax(scores, axis=-1)
        out = jnp.einsum('bhst,bhtd->bhsd', attn, v)
        out = out.transpose(0, 2, 1, 3).reshape(B_, S_, C)
        return jnp.einsum('bsc,oc->bso', out, wo)

    def _L0_xattn_ref(encodings_q, encodings_k, encodings_v, mask, W_q, b_q, W_k, b_k, W_v, b_v):
        import jax, jax.numpy as jnp
        import numpy as np
        B, S, D = (4, 256, 128)
        q = jnp.einsum('bsd,ed->bse', encodings_q, W_q) + b_q
        k = jnp.einsum('bsd,ed->bse', encodings_k, W_k) + b_k
        v = jnp.einsum('bsd,ed->bse', encodings_v, W_v) + b_v
        scores = jnp.einsum('bqd,bkd->bqk', q, k) / jnp.sqrt(jnp.asarray(q.shape[2], q.dtype))
        scores = jnp.where(mask[None, :, :], jnp.asarray(-1000000000.0, scores.dtype), scores)
        attn = jax.nn.softmax(scores, axis=-1)
        return jnp.einsum('bqk,bkd->bqd', attn, v)

    def _L0_ffn_ref(hidden_states, ln_g, ln_b, router_w, up_W, up_b, down_W, down_b, spec0_W, spec0_b, ln0_g, ln0_b, spec1a_W, spec1a_b, spec1b_W, spec1b_b, ln1_g, ln1_b, spec2_W, spec2_b):
        import jax, jax.numpy as jnp
        import numpy as np
        B, S, H, F, E, K = (2, 256, 128, 512, 8, 2)

        def _ln(x, g, b, eps=1e-05):
            m = jnp.mean(x, axis=-1, keepdims=True)
            v = jnp.var(x, axis=-1, keepdims=True)
            return (x - m) / jnp.sqrt(v + eps) * g + b

        def _gelu(x):
            return jax.nn.gelu(x, approximate=False)
        b, s, h = hidden_states.shape
        x = hidden_states.reshape(-1, h)
        nx = _ln(x, ln_g, ln_b)
        logits = nx @ router_w
        probs = jax.nn.softmax(logits, axis=-1)
        _, idx = jax.lax.top_k(probs, K)
        mask = jnp.sum(jax.nn.one_hot(idx, probs.shape[-1], dtype=probs.dtype), axis=1)
        w = probs * mask
        w = w / jnp.sum(w, axis=-1, keepdims=True)
        h1 = _gelu(jnp.einsum('th,ehf->etf', nx, up_W) + up_b[:, None, :])
        i0 = jnp.array([0, 4])
        i1 = jnp.array([1, 5])
        i2 = jnp.array([2, 6])
        s0 = _gelu(_ln(jnp.einsum('etf,efg->etg', h1[i0], spec0_W) + spec0_b[:, None, :], ln0_g[:, None, :], ln0_b[:, None, :]))
        t1 = _gelu(jnp.einsum('etf,efg->etg', h1[i1], spec1a_W) + spec1a_b[:, None, :])
        s1 = _ln(jnp.einsum('etg,egf->etf', t1, spec1b_W) + spec1b_b[:, None, :], ln1_g[:, None, :], ln1_b[:, None, :])
        s2 = _gelu(jnp.einsum('etf,efg->etg', h1[i2], spec2_W) + spec2_b[:, None, :])
        h2 = h1.at[i0].set(s0).at[i1].set(s1).at[i2].set(s2)
        out_e = jnp.einsum('etf,efh->eth', h2, down_W) + down_b[:, None, :]
        y = jnp.einsum('eth,te->th', out_e, w) + x
        return y.reshape(hidden_states.shape)

    def _L1_attn_ref(u, A_log, B_p, C_p, D_p, W_dt, b_dt):
        import jax, jax.numpy as jnp
        import numpy as np
        D_MODEL = 128
        D_STATE = 16
        DT_MIN = 0.001
        DT_MAX = 0.02
        log_dt = jnp.einsum('blh,gh->blg', u, W_dt) + b_dt
        dt = jnp.clip(jnp.exp(log_dt), DT_MIN, DT_MAX)
        A = -jnp.exp(A_log)
        Z = jnp.einsum('blh,hn->blhn', dt, A)
        A_bar = jnp.exp(Z)
        coef = jnp.expm1(Z) / A
        Bu = coef * B_p * u[..., None]
        Bsz, L, H = u.shape
        x0 = jnp.zeros((Bsz, H, D_STATE), dtype=u.dtype)

        def step(x, inputs):
            a_t, bu_t, u_t = inputs
            x = x * a_t + bu_t
            y = jnp.einsum('bhn,hn->bh', x, C_p) + D_p * u_t
            return (x, y)
        xs = (jnp.moveaxis(A_bar, 1, 0), jnp.moveaxis(Bu, 1, 0), jnp.moveaxis(u, 1, 0))
        _, ys = jax.lax.scan(step, x0, xs)
        return jnp.moveaxis(ys, 0, 1)

    def _L1_xattn_ref(tgt, src, src_padded_mask, q_w, q_b, kv_w, kv_b, proj_w, proj_b):
        import jax, jax.numpy as jnp
        import numpy as np
        DIM = 128
        HEADS = 16
        HEAD_DIM = DIM // HEADS
        SCALE = HEAD_DIM ** (-0.5)
        B, N_TGT, N_SRC = (4, 128, 256)
        Bb, Ns, C = src.shape
        Nt = tgt.shape[1]
        kv = (src @ kv_w.T + kv_b).reshape(Bb, Ns, 2, HEADS, HEAD_DIM)
        kv = jnp.transpose(kv, (2, 0, 3, 1, 4))
        k, v = (kv[0], kv[1])
        q = (tgt @ q_w.T + q_b).reshape(Bb, Nt, HEADS, HEAD_DIM).transpose(0, 2, 1, 3)
        attn = jnp.einsum('bhqd,bhkd->bhqk', q, k) * SCALE
        attn = jnp.where(src_padded_mask[:, None, None, :], -jnp.inf, attn)
        attn = jax.nn.softmax(attn, axis=-1)
        out = jnp.einsum('bhqk,bhkd->bhqd', attn, v)
        out = out.transpose(0, 2, 1, 3).reshape(Bb, Nt, C)
        out = out @ proj_w.T + proj_b
        return out

    def _L1_ffn_ref(x, w_gate, w_up, w_down):
        import jax, jax.numpy as jnp
        import numpy as np
        HIDDEN = 128
        INNER = 512

        def _weight_quant(w):
            scale = 1.0 / jnp.clip(jnp.mean(jnp.abs(w)), 1e-05)
            wq = jnp.clip(jnp.round(w * scale), -1.0, 1.0) / scale
            return w + jax.lax.stop_gradient(wq - w)

        def _act_quant(x):
            scale = 127.0 / jnp.clip(jnp.max(jnp.abs(x), axis=-1, keepdims=True), 1e-05)
            xq = jnp.clip(jnp.round(x * scale), -128.0, 127.0) / scale
            return x + jax.lax.stop_gradient(xq - x)

        def _bitlinear(x, w):
            return jnp.einsum('bsi,oi->bso', _act_quant(x), _weight_quant(w))
        gate = jax.nn.silu(_bitlinear(x, w_gate))
        up = _bitlinear(x, w_up)
        return _bitlinear(gate * up, w_down)

    def _L2_attn_ref(hidden_states, Wq, Wk, Wv, Wo, Wkc, Wg_slc, Wg_swa):
        import jax, jax.numpy as jnp
        import numpy as np
        NH = 16
        NKV = 4
        D = 64
        BLK = 64
        KSEL = 16
        THETA = 10000.0

        def _rotate_half(x):
            x1, x2 = jnp.split(x, 2, axis=-1)
            return jnp.concatenate([-x2, x1], axis=-1)
        B, S, Hm = hidden_states.shape
        g_slc = jax.nn.sigmoid(hidden_states @ Wg_slc.T)
        g_swa = jax.nn.sigmoid(hidden_states @ Wg_swa.T)
        q = (hidden_states @ Wq.T).reshape(B, S, NH, D)
        k = (hidden_states @ Wk.T).reshape(B, S, NKV, D)
        v = (hidden_states @ Wv.T).reshape(B, S, NKV, D)
        inv_freq = 1.0 / THETA ** (jnp.arange(0, D, 2, dtype=jnp.float32) / D)
        freqs = jnp.arange(S, dtype=jnp.float32)[:, None] * inv_freq
        emb = jnp.concatenate([freqs, freqs], axis=-1)
        cos = jnp.cos(emb)[None, :, None, :]
        sin = jnp.sin(emb)[None, :, None, :]
        q = q * cos + _rotate_half(q) * sin
        k = k * cos + _rotate_half(k) * sin
        groups = NH // NKV
        k = jnp.repeat(k, groups, axis=2)
        v = jnp.repeat(v, groups, axis=2)
        nb = S // BLK
        kc = k @ Wkc.T
        k_block_mean = kc.reshape(B, nb, BLK, NH, D // 4).mean(axis=2)
        qc = q @ Wkc.T
        block_scores = jnp.einsum('bshd,bnhd->bhsn', qc, k_block_mean)
        block_scores = block_scores / jnp.sqrt(jnp.float32(D // 4))
        pos_blocks = jnp.arange(S) // BLK
        bmask = jnp.arange(nb)[None, :] <= pos_blocks[:, None]
        block_scores = jnp.where(bmask[None, None], block_scores, -jnp.inf)
        _, top_idx = jax.lax.top_k(block_scores, min(KSEL, nb))
        top_idx = jnp.sort(top_idx, axis=-1)
        del top_idx
        scale = 1.0 / jnp.sqrt(jnp.float32(D))
        scores = jnp.einsum('bqhd,bkhd->bhqk', q, k) * scale
        cmask = jnp.tril(jnp.ones((S, S), dtype=bool))
        scores = jnp.where(cmask[None, None], scores, -jnp.inf)
        p = jax.nn.softmax(scores, axis=-1)
        attn = jnp.einsum('bhqk,bkhd->bqhd', p, v)
        out = attn * (g_slc + g_swa)[..., None]
        out = out.reshape(B, S, NH * D)
        return out @ Wo.T

    def _L2_xattn_ref(query, key, value, Wq, bq, Wk, bk, Wv, bv, Wo, bo, w1, b1, w2, b2, w3, b3):
        import jax, jax.numpy as jnp
        import numpy as np
        import math
        B, S, D, H = (1, 256, 128, 16)
        DK = D // H
        DH = 64
        LOG_T_MIN = math.log(0.1)
        LOG_T_MAX = math.log(10.0)

        def _linear(x, W, b):
            return x @ W.T + b
        b, sq, d = query.shape
        sk = key.shape[1]
        h, dk = (H, DK)
        Q = _linear(query, Wq, bq).reshape(b, sq, h, dk).transpose(0, 2, 1, 3)
        K = _linear(key, Wk, bk).reshape(b, sk, h, dk).transpose(0, 2, 1, 3)
        V = _linear(value, Wv, bv).reshape(b, sk, h, dk).transpose(0, 2, 1, 3)
        qk = jnp.einsum('bhqd,bhkd->bhqk', Q, K)
        scores = qk / math.sqrt(dk)
        mean_sim = scores.mean(axis=(-2, -1))
        max_sim = scores.max(axis=-1).mean(axis=-1)
        probs = jax.nn.softmax(scores, axis=-1)
        entropy_proxy = jnp.var(probs, axis=-1, ddof=1).mean(axis=-1)
        feats = jnp.stack([mean_sim, max_sim, entropy_proxy], axis=-1)
        hidden = jax.nn.gelu(_linear(feats, w1, b1), approximate=False)
        hidden = jax.nn.gelu(_linear(hidden, w2, b2), approximate=False)
        log_t = jnp.clip(_linear(hidden, w3, b3), LOG_T_MIN, LOG_T_MAX)
        t = jnp.exp(log_t)[..., None]
        attn_scores = qk / (2.0 * t)
        attn = jax.nn.softmax(attn_scores, axis=-1)
        attn = jnp.nan_to_num(attn, nan=0.0)
        out = jnp.einsum('bhqk,bhkd->bhqd', attn, V)
        out = out.transpose(0, 2, 1, 3).reshape(b, sq, d)
        return _linear(out, Wo, bo)

    def _L2_ffn_ref(token_inputs, Wg, Wq, Wk, Wv, Wo):
        import jax, jax.numpy as jnp
        import numpy as np
        CAPACITY_FACTOR = 0.5
        NUM_HEADS = 16
        B, N, D = token_inputs.shape
        C = int(N * CAPACITY_FACTOR)
        H = NUM_HEADS
        dh = D // H
        gate = jax.nn.sigmoid((token_inputs @ Wg)[..., 0])
        _, idx = jax.lax.top_k(gate, C)
        attn_in = jnp.take_along_axis(token_inputs, idx[..., None], axis=1)
        q = (attn_in @ Wq).reshape(B, C, H, dh)
        k = (attn_in @ Wk).reshape(B, C, H, dh)
        v = (attn_in @ Wv).reshape(B, C, H, dh)
        scores = jnp.einsum('bqhd,bkhd->bhqk', q, k) / jnp.sqrt(jnp.float32(dh))
        attn = jax.nn.softmax(scores, axis=-1)
        o = jnp.einsum('bhqk,bkhd->bqhd', attn, v).reshape(B, C, D) @ Wo
        gate_sel = jnp.take_along_axis(gate, idx, axis=1)
        out = jnp.zeros_like(token_inputs)
        out = out.at[jnp.arange(B)[:, None], idx].set(o * gate_sel[..., None])
        return out

    def _L3_attn_ref(x, wq, wk, wv, wo):
        import jax, jax.numpy as jnp
        import numpy as np
        B, S, D = (2, 256, 128)
        N_HEADS, N_KV_HEADS = (16, 4)
        HEAD_DIM = D // N_HEADS
        KV_GROUPS = N_HEADS // N_KV_HEADS
        ROPE_BASE = 10000.0

        def _apply_rope(t, cos, sin):
            t1, t2 = jnp.split(t, 2, axis=-1)
            return jnp.concatenate([t1 * cos - t2 * sin, t1 * sin + t2 * cos], axis=-1)
        Bx, Sx, Dx = x.shape
        q = (x @ wq).reshape(Bx, Sx, N_HEADS, HEAD_DIM)
        k = (x @ wk).reshape(Bx, Sx, N_KV_HEADS, HEAD_DIM)
        v = (x @ wv).reshape(Bx, Sx, N_KV_HEADS, HEAD_DIM)
        half = HEAD_DIM // 2
        inv_freq = 1.0 / ROPE_BASE ** (jnp.arange(0, half, dtype=jnp.float32) / half)
        pos = jnp.arange(Sx, dtype=jnp.float32)
        ang = pos[:, None] * inv_freq[None, :]
        cos = jnp.cos(ang)[:, None, :]
        sin = jnp.sin(ang)[:, None, :]
        q = _apply_rope(q, cos, sin)
        k = _apply_rope(k, cos, sin)
        k = jnp.broadcast_to(k[:, :, None, :, :], (Bx, Sx, KV_GROUPS, N_KV_HEADS, HEAD_DIM)).reshape(Bx, Sx, N_HEADS, HEAD_DIM)
        v = jnp.broadcast_to(v[:, :, None, :, :], (Bx, Sx, KV_GROUPS, N_KV_HEADS, HEAD_DIM)).reshape(Bx, Sx, N_HEADS, HEAD_DIM)
        scale = 1.0 / jnp.sqrt(jnp.float32(HEAD_DIM))
        scores = jnp.einsum('bshd,bthd->bhst', q, k) * scale
        causal = jnp.tril(jnp.ones((Sx, Sx), dtype=bool))
        scores = jnp.where(causal[None, None, :, :], scores, jnp.float32(-jnp.inf))
        attn = jax.nn.softmax(scores, axis=-1)
        out = jnp.einsum('bhst,bthd->bshd', attn, v).reshape(Bx, Sx, Dx)
        return out @ wo

    def _L3_xattn_ref(x, context, context_mask, g1, b1, g2, b2, Wq, Wkv, Wo, bo):
        import jax, jax.numpy as jnp
        import numpy as np
        DIM = 128
        HEADS = 16
        DIM_HEAD = 64
        INNER = HEADS * DIM_HEAD
        EPS = 1e-05

        def layer_norm(x, gamma, beta):
            mu = jnp.mean(x, axis=-1, keepdims=True)
            var = jnp.var(x, axis=-1, keepdims=True)
            return (x - mu) * jax.lax.rsqrt(var + EPS) * gamma + beta
        scale = DIM_HEAD ** (-0.5)
        xn = layer_norm(x, g1, b1)
        cn = layer_norm(context, g2, b2)
        q = xn @ Wq
        kv_x = xn @ Wkv
        kv_c = cn @ Wkv
        k_in, v_in = jnp.split(kv_x, 2, axis=-1)
        k_c, v_c = jnp.split(kv_c, 2, axis=-1)
        k = jnp.concatenate([k_c, k_in], axis=1)
        v = jnp.concatenate([v_c, v_in], axis=1)

        def split_heads(t):
            b_, n_, _ = t.shape
            return t.reshape(b_, n_, HEADS, DIM_HEAD).transpose(0, 2, 1, 3)
        q, k, v = map(split_heads, (q, k, v))
        q = q * scale
        i, j = (q.shape[2], k.shape[2])
        mask_value = -jnp.finfo(q.dtype).max
        sim = jnp.einsum('bhid,bhjd->bhij', q, k)
        cm = jnp.pad(context_mask, ((0, 0), (0, j - context_mask.shape[-1])), constant_values=True)
        sim = jnp.where(cm[:, None, None, :], sim, mask_value)
        causal = jnp.triu(jnp.ones((i, j), dtype=bool), k=j - i + 1)
        sim = jnp.where(causal[None, None], mask_value, sim)
        attn = jax.nn.softmax(sim, axis=-1)
        out = jnp.einsum('bhij,bhjd->bhid', attn, v)
        out = out.transpose(0, 2, 1, 3).reshape(x.shape[0], i, INNER)
        return out @ Wo + bo

    def _L3_ffn_ref(x, Wr, W1, W2):
        import math
        import jax, jax.numpy as jnp
        import numpy as np
        B, S, D, F, E = (8, 256, 128, 512, 8)
        CAPACITY_FACTOR = 1.0
        b, s, d = x.shape
        t = b * s
        cap = max(math.ceil(t * CAPACITY_FACTOR / E), 1)
        xf = x.reshape(t, d)
        probs = jax.nn.softmax(xf.astype(jnp.float32) @ Wr, axis=-1)
        eidx = jnp.argmax(probs, axis=-1)
        p_tok = jnp.take_along_axis(probs, eidx[:, None], axis=1)[:, 0]
        onehot = jax.nn.one_hot(eidx, E, dtype=jnp.int32)
        rank_all = jnp.cumsum(onehot, axis=0) - onehot
        rank = jnp.take_along_axis(rank_all, eidx[:, None], axis=1)[:, 0]
        keep = rank < cap
        slot = jnp.where(keep, rank, cap)
        dispatch = jnp.zeros((E, cap + 1), dtype=jnp.int32).at[eidx, slot].set(jnp.arange(t, dtype=jnp.int32))
        valid = jnp.zeros((E, cap + 1), dtype=bool).at[eidx, slot].set(keep)
        dispatch = dispatch[:, :cap]
        valid = valid[:, :cap]
        xe = xf[dispatch]
        h = jnp.maximum(jnp.einsum('ecd,edf->ecf', xe, W1), 0.0)
        ye = jnp.einsum('ecf,efd->ecd', h, W2)
        pe = p_tok[dispatch]
        ye = ye * (pe * valid.astype(ye.dtype))[:, :, None]
        y = jnp.zeros((t, d), dtype=x.dtype).at[dispatch.reshape(-1)].add(ye.reshape(E * cap, d).astype(x.dtype))
        return y.reshape(b, s, d)
    x = x + _L0_attn_ref(_layernorm(x, axis=-1), L0_attn_wq, L0_attn_wk, L0_attn_wv, L0_attn_wo, L0_attn_pope_bias)
    x = x + _L0_xattn_ref(_layernorm(x, axis=-1), ctx_1024, ctx_1024, mask_SxS2_bk1, L0_xattn_W_q, L0_xattn_b_q, L0_xattn_W_k, L0_xattn_b_k, L0_xattn_W_v, L0_xattn_b_v)
    x = x + _L0_ffn_ref(_layernorm(x, axis=-1), L0_ffn_ln_g, L0_ffn_ln_b, L0_ffn_router_w, L0_ffn_up_W, L0_ffn_up_b, L0_ffn_down_W, L0_ffn_down_b, L0_ffn_spec0_W, L0_ffn_spec0_b, L0_ffn_ln0_g, L0_ffn_ln0_b, L0_ffn_spec1a_W, L0_ffn_spec1a_b, L0_ffn_spec1b_W, L0_ffn_spec1b_b, L0_ffn_ln1_g, L0_ffn_ln1_b, L0_ffn_spec2_W, L0_ffn_spec2_b)
    x = x + _L1_attn_ref(_layernorm(x, axis=-1), L1_attn_A_log, L1_attn_B_p, L1_attn_C_p, L1_attn_D_p, L1_attn_W_dt, L1_attn_b_dt)
    x = x + _L1_xattn_ref(_layernorm(x, axis=-1), ctx_1024, mask_BxS2_bk0, L1_xattn_q_w, L1_xattn_q_b, L1_xattn_kv_w, L1_xattn_kv_b, L1_xattn_proj_w, L1_xattn_proj_b)
    x = x + _L1_ffn_ref(_layernorm(x, axis=-1), L1_ffn_w_gate, L1_ffn_w_up, L1_ffn_w_down)
    x = x + _L2_attn_ref(_layernorm(x, axis=-1), L2_attn_Wq, L2_attn_Wk, L2_attn_Wv, L2_attn_Wo, L2_attn_Wkc, L2_attn_Wg_slc, L2_attn_Wg_swa)
    x = x + _L2_xattn_ref(_layernorm(x, axis=-1), ctx_1024, ctx_1024, L2_xattn_Wq, L2_xattn_bq, L2_xattn_Wk, L2_xattn_bk, L2_xattn_Wv, L2_xattn_bv, L2_xattn_Wo, L2_xattn_bo, L2_xattn_w1, L2_xattn_b1, L2_xattn_w2, L2_xattn_b2, L2_xattn_w3, L2_xattn_b3)
    x = x + _L2_ffn_ref(_layernorm(x, axis=-1), L2_ffn_Wg, L2_ffn_Wq, L2_ffn_Wk, L2_ffn_Wv, L2_ffn_Wo)
    x = x + _L3_attn_ref(_layernorm(x, axis=-1), L3_attn_wq, L3_attn_wk, L3_attn_wv, L3_attn_wo)
    x = x + _L3_xattn_ref(_layernorm(x, axis=-1), ctx_1024, mask_BxS2_bf1, L3_xattn_g1, L3_xattn_b1, L3_xattn_g2, L3_xattn_b2, L3_xattn_Wq, L3_xattn_Wkv, L3_xattn_Wo, L3_xattn_bo)
    x = x + _L3_ffn_ref(_layernorm(x, axis=-1), L3_ffn_Wr, L3_ffn_W1, L3_ffn_W2)
    return x

_drawn_inputs = setup_inputs


def setup_inputs(seed=0):
    import zlib

    import numpy as np

    out = dict(_drawn_inputs(seed))
    spreads = {'L0_ffn_ln_g': (1.0, 0.2),
     'L0_ffn_ln_b': (0.0, 0.1),
     'L0_ffn_up_b': (0.0, 0.573),
     'L0_ffn_down_b': (0.0, 0.1),
     'L0_ffn_spec0_b': (0.0, 0.1),
     'L0_ffn_ln0_g': (1.0, 0.6),
     'L0_ffn_ln0_b': (0.0, 0.8),
     'L0_ffn_spec1a_b': (0.0, 0.539),
     'L0_ffn_spec1b_b': (0.0, 0.1),
     'L0_ffn_ln1_g': (1.0, 0.6),
     'L0_ffn_ln1_b': (0.0, 0.728),
     'L0_ffn_spec2_b': (0.0, 0.8),
     'L1_attn_D_p': (1.0, 0.2),
     'L1_xattn_q_b': (0.0, 0.8),
     'L1_xattn_kv_b': (0.0, 0.663),
     'L1_xattn_proj_b': (0.0, 0.1),
     'L3_xattn_g1': (1.0, 0.6),
     'L3_xattn_b1': (0.0, 0.376),
     'L3_xattn_g2': (1.0, 0.6),
     'L3_xattn_b2': (0.0, 0.448),
     'L3_xattn_bo': (0.0, 0.281)}
    factors = {'L0_xattn_b_q': 8.0,
     'L0_xattn_b_k': 64.0,
     'L0_xattn_b_v': 4.068,
     'L0_ffn_spec1a_W': 5.565,
     'L0_ffn_spec1b_W': 3.652,
     'L0_ffn_spec2_W': 8.0,
     'L1_attn_A_log': 64.0,
     'L1_attn_B_p': 64.0,
     'L1_attn_C_p': 50.07,
     'L1_attn_W_dt': 64.0,
     'L1_attn_b_dt': 64.0,
     'L1_xattn_q_w': 8.0,
     'L1_xattn_kv_w': 4.496,
     'L1_xattn_proj_w': 3.688,
     'L2_attn_Wq': 8.0,
     'L2_attn_Wk': 8.0,
     'L2_attn_Wg_slc': 8.0,
     'L2_attn_Wg_swa': 8.0,
     'L2_xattn_Wq': 8.0,
     'L2_xattn_bq': 8.0,
     'L2_xattn_Wk': 8.0,
     'L2_xattn_bk': 8.0,
     'L2_xattn_Wv': 5.03,
     'L2_xattn_bv': 8.0,
     'L2_xattn_Wo': 5.055,
     'L2_xattn_bo': 5.252,
     'L2_xattn_w1': 8.0,
     'L2_xattn_b1': 8.0,
     'L2_xattn_w2': 8.0,
     'L2_xattn_b2': 8.0,
     'L2_xattn_w3': 8.0,
     'L2_ffn_Wq': 2.936,
     'L2_ffn_Wk': 2.998,
     'L3_attn_wq': 8.0,
     'L3_attn_wk': 8.0,
     'L3_attn_wv': 4.657,
     'L3_attn_wo': 4.978}
    for name, (base, spread) in spreads.items():
        noise = np.random.default_rng([zlib.crc32(name.encode()), seed]).standard_normal(out[name].shape)
        drawn = base * np.exp(spread * noise) if base else spread * noise
        out[name] = jnp.asarray(drawn.astype(out[name].dtype))
    for name, factor in factors.items():
        out[name] = (out[name] * factor).astype(out[name].dtype)
    return out
```

```python
from contextlib import ExitStack
from itertools import zip_longest

import numpy as np

import concourse.bass as bass
from concourse import mybir

F32 = mybir.dt.float32
BF16 = mybir.dt.bfloat16
U8 = mybir.dt.uint8
U32 = mybir.dt.uint32
I32 = mybir.dt.int32
ALU = mybir.AluOpType
ACT = mybir.ActivationFunctionType
AX = mybir.AxisListType

B, S, D, SC = 8, 256, 128, 64
QT = S // 128
NT = B * QT
H = 16
EPS = 1e-5
MAX_LANES = 4
MASKED = -1e30


class Weights:

    def __init__(self, nc, name, dram, at):
        self.nc, self.dram, self.at = nc, dram, at
        self.stack = ExitStack()
        self.sb = self.stack.enter_context(nc.sbuf_tensor(f"{name}_weights", [128, dram.shape[1]], F32))
        self.loaded = nc.alloc_semaphore(f"{name}_weights_loaded")

    def of(self, key):
        a, n = self.at[key]
        return self.sb[:, a:a + n]

    def fetch(self, sp):
        sp.dma_start(self.sb[:, :], self.dram).then_inc(self.loaded, 16)

    def close(self):
        self.stack.close()
        self.nc.clear_and_free_semaphores([self.loaded])
        self.nc.all_engine_barrier()


class Stage:

    def __init__(self, nc, name):
        self.nc, self.name = nc, name
        self.stack = ExitStack()
        self.sems = []

    def sb(self, name, shape, dt=F32):
        return self.stack.enter_context(self.nc.sbuf_tensor(f"{self.name}_{name}", shape, dt))

    def ps(self, name, shape=(128, 512), dt=F32):
        return self.stack.enter_context(self.nc.psum_tensor(f"{self.name}_{name}", list(shape), dt))

    def sem(self, name):
        s = self.nc.alloc_semaphore(f"{self.name}_{name}")
        self.sems.append(s)
        return s

    def close(self):
        self.stack.close()
        self.nc.clear_and_free_semaphores(self.sems)
        self.nc.all_engine_barrier()


class Ring:

    def __init__(self, st, name, banks, uses):
        self.banks = [st.ps(f"{name}{i}") for i in range(banks)]
        self.filled = [st.sem(f"{name}{i}_filled") for i in range(banks)]
        self.freed = [st.sem(f"{name}{i}_freed") for i in range(banks)]
        self.n = banks
        self.per = [(uses - i + banks - 1) // banks for i in range(banks)]

    def bank(self, k):
        return self.banks[k % self.n]

    def full(self, k):
        return self.filled[k % self.n]

    def free(self, k):
        return self.freed[k % self.n]

    def credit(self, eng):
        for f in self.freed:
            eng.sem_inc(f, 1)

    def wait_free(self, eng, b, k):
        eng.wait_ge(self.free(k), b * self.per[k % self.n] + k // self.n + 1)

    def wait_filled(self, eng, b, k):
        eng.wait_ge(self.full(k), b * self.per[k % self.n] + k // self.n + 1)

    def wait_emptied(self, eng, b, k):
        eng.wait_ge(self.free(k), b * self.per[k % self.n] + k // self.n + 2)


    def wait_for(self, eng, b, emptied, k):
        last = {}
        for j in [*emptied, k - self.n]:
            last[j % self.n] = max(last.get(j % self.n, j), j)
        for j in last.values():
            eng.wait_ge(self.free(j), b * self.per[j % self.n] + j // self.n + 2)


class Lane:

    def __init__(self, st, lane=0, lanes=1, tag=None):
        tag = f"lane{lane}_" if tag is None else tag
        self.nc, self.lane, self.lanes = st.nc, lane, lanes
        self.sb = lambda name, *a: st.sb(tag + name, *a)
        self.ps = lambda name, *a: st.ps(tag + name, *a)
        self.sem = lambda name: st.sem(tag + name)

    def batch(self, i):
        return self.lanes * i + self.lane


def in_turn(*programs):
    for _ in zip_longest(*programs):
        pass


class Norm:

    def __init__(self, st, x, of=None):
        self.x, self.nc, self.of = x, st.nc, of
        self.batch = st.batch if isinstance(st, Lane) else lambda i: i
        if of:
            st = Lane(st, tag="again_")
        self.stats = st.sb("stats", [128, QT, 6])
        self.mv = st.sb("mv", [128, QT, 2])
        self.veps = st.sb("veps", [128, QT])
        self.rstd = st.sb("rstd", [128, QT])
        self.neghalf = st.sb("neghalf", [128, QT])
        self.xn = st.sb("xn", [128, QT, D])
        self.mv_done = st.sem("mv_done")
        self.veps_done = st.sem("veps_done")
        self.rstd_done = st.sem("rstd_done")
        self.xn_done = st.sem("xn_done")
        self.half_set = st.sem("half_set")

    def pool_setup(self, eng):
        eng.memset(self.neghalf[:, :], -0.5).then_inc(self.half_set, 1)
        eng.wait_ge(self.half_set, 1)

    def source(self, i, t):
        return self.of.xn[:, t, :] if self.of else self.x[:, QT * self.batch(i) + t, :]

    def take_moments(self, eng, i):
        if self.of:
            self.of.wait(eng, i)
        for t in range(QT):
            eng.bn_stats(self.stats[:, t, :], self.source(i, t))
        eng.drain()
        for t in range(QT):
            eng.bn_aggr(self.mv[:, t, :], self.stats[:, t, :]).then_inc(self.mv_done, 1)
        eng.wait_ge(self.mv_done, QT * i + QT)
        eng.tensor_scalar(self.veps[:, :], self.mv[:, :, 1], EPS, None, ALU.add).then_inc(self.veps_done, 1)

    def norm_rows(self, eng, i):
        eng.wait_ge(self.rstd_done, i + 1)
        for t in range(QT):
            eng.tensor_scalar(self.xn[:, t, :], self.source(i, t), self.mv[:, t, 0:1],
                              self.rstd[:, t:t + 1], ALU.subtract, ALU.mult).then_inc(self.xn_done, 1)

    def vector(self, eng, i):
        self.take_moments(eng, i)
        self.norm_rows(eng, i)

    def pool(self, eng, i):
        eng.wait_ge(self.veps_done, i + 1)
        eng.tensor_tensor(self.rstd[:, :], self.veps[:, :], self.neghalf[:, :], ALU.pow).then_inc(self.rstd_done, 1)

    def wait(self, eng, i):
        eng.wait_ge(self.xn_done, QT * i + QT)


class SelfLane:
    LAG, PR = 2, 3
    SR = 2

    def __init__(self, st, lane, lanes, g, w, ktab, spec):
        self.g, self.w, self.ktab, self.spec = g, w, ktab, spec
        self.d, self.NG, self.causal = spec["d"], spec["groups"], spec["causal"]
        self.nq, self.nk, self.kreps = spec["qchunks"], spec["kchunks"], spec["heads_of_kchunk"]
        self.gates, self.rope = spec["gates"], spec["rope"]
        self.NP = H // 2
        self.NI = self.NP * QT
        self.per_group = self.NP // self.NG
        self.MW = 128 * self.NG // H
        self.nv = spec["kvheads"] * self.d
        self.NB = 2 * self.per_group
        self.CH = self.nq + self.nk
        self.v_uses = QT if self.nv > 128 else 1
        self.V_USE = 1 + self.CH
        self.G_USE = self.V_USE + self.v_uses
        self.FIRST = self.G_USE + self.gates
        self.OUT = self.FIRST + self.NI + self.NG
        self.share = self.nk * self.kreps == H
        self.act_tile = 1 if self.causal else 0
        st = Lane(st, lane, lanes)
        self.batch = st.batch
        self.T = Ring(st, "t", 2, self.OUT + 1)
        self.scores = [st.ps(f"s{i}") for i in range(self.SR)]
        self.nrm = Norm(st, g["x"])
        self.xnT = st.sb("xnT", [128, S])
        self.q_sb = st.sb("q", [128, self.nq, S])
        self.k_sb = st.sb("k", [128, self.nk, S])
        self.tmp = st.sb("tmp", [128, 2 if self.rope else self.CH, 2, S])
        self.kbd = st.sb("kbd", [128, self.nk * self.kreps, S])
        self.v_sb = st.sb("v", [128, QT, self.nv // self.d, self.MW])
        self.P = [st.sb(f"p{i}", [128, 2, S]) for i in range(self.PR)]
        self.PT = [st.sb(f"pt{i}", [128, 2, QT, S]) for i in range(self.NB)]
        self.OT = st.sb("ot", [128, self.NG, S])
        self.nmax = st.sb("nmax", [128, self.PR, 2])
        self.sums = st.sb("sums", [128, self.PR, 2])
        self.rec = st.sb("rec", [128, self.PR, 2])
        self.weight = st.sb("weight", [128, self.PR, 2])
        self.gate = st.sb("gate", [128, QT, 2, H])
        self.gsum = st.sb("gsum", [128, QT, H])
        self.parts, self.joined = st.sem("parts"), st.sem("joined")
        self.soft_abs, self.soft_exp, self.soft_ln = st.sem("soft_abs"), st.sem("soft_exp"), st.sem("soft_ln")
        self.soft_sum = st.sem("soft_sum")
        self.kbd_pool, self.kbd_vector, self.v_set = st.sem("kbd_pool"), st.sem("kbd_vector"), st.sem("v_set")
        self.s_filled, self.max_done, self.exp_done = st.sem("s_filled"), st.sem("max_done"), st.sem("exp_done")
        self.rec_done, self.weight_done, self.p_done = st.sem("rec_done"), st.sem("weight_done"), st.sem("p_done")
        self.gate_step = st.sem("gate_step")

    def keys_of(self, qt):
        return 128 * (qt + 1) if self.causal else S

    def khead(self, h):
        return h if self.nk * self.kreps == H else 2 * (h // 4) + h % 2

    def chunk(self, k):
        return self.q_sb[:, k - 1, :] if k <= self.nq else self.k_sb[:, k - 1 - self.nq, :]

    def item_use(self, j):
        return self.FIRST + j + j // (QT * self.per_group)

    def group_use(self, gr):
        return self.item_use((gr + 1) * QT * self.per_group - 1) + 1

    def ended_group(self, j):
        n = QT * self.per_group
        return j // n if 0 <= j < self.NI and j % n == n - 1 else None

    def sync_setup(self, sp):
        self.T.credit(sp)
        sp.sem_inc(self.exp_done, self.SR)

    def pool_setup(self, pool):
        self.nrm.pool_setup(pool)
        pool.memset(self.v_sb[:, :, :, :], 0.0).then_inc(self.v_set, 1)

    def pool(self, pool, b):
        yield
        for k in range(1, self.CH + 1):
            if self.rope:
                part = self.tmp[:, (k - 1) % 2, :, :]
                pool.wait_ge(self.parts, b * self.CH + k)
                pool.tensor_tensor(self.chunk(k), part[:, 0, :], part[:, 1, :], ALU.add).then_inc(self.joined, 1)
                if k > self.nq:
                    self.lone_keys(pool, b, k - 1 - self.nq)
            yield
        yield
        if not self.rope:
            yield
            for c in range(self.nk):
                self.lone_keys(pool, b, c)
            yield
        for s in range(self.NI + self.LAG + 1):
            i = s - 1
            if 0 <= i < self.NI:
                n = self.keys_of(i % QT)
                pool.wait_ge(self.weight_done if self.gates else self.rec_done, b * self.NI + i + 1)
                by = self.weight if self.gates else self.rec
                P = self.P[i % self.PR]
                pool.tensor_tensor(P[:, :, 0:n], P[:, :, 0:n],
                                   by[:, i % self.PR, :].unsqueeze(2).to_broadcast([128, 2, n]),
                                   ALU.mult).then_inc(self.p_done, 1)
            if s == self.NI:
                self.nrm.pool(pool, b + 1)
            yield

    def lone_keys(self, pool, b, c):
        kreps = self.kreps
        pool.wait_ge(self.joined, b * self.CH + self.nq + c + 1)
        for j in range(0, kreps, 2):
            if self.share and (c * kreps + j) // 2 % 2 == 0:
                continue
            pool.tensor_tensor(self.kbd[:, c * kreps + j:c * kreps + j + 2, :],
                               self.k_sb[:, c, :].unsqueeze(1).to_broadcast([128, 2, S]),
                               self.w("kmask")[:, j:j + 2].unsqueeze(2).to_broadcast([128, 2, S]),
                               ALU.mult).then_inc(self.kbd_pool, 1)

    def lone_keys_vector(self, v, b, c):
        kreps = self.kreps
        v.wait_ge(self.joined, b * self.CH + self.nq + c + 1)
        for j in range(kreps):
            h = c * kreps + j
            if h // 2 % 2 == 0:
                one = v.tensor_scalar(self.kbd[:, h, :], self.k_sb[:, c, :], self.w("kmask")[:, j:j + 1], None, ALU.mult)
                if h % 2:
                    one.then_inc(self.kbd_vector, 1)

    def tensor(self, pe, b):
        T, w, g, nv, xnT, NI, LAG = self.T, self.w, self.g, self.nv, self.xnT, self.NI, self.LAG
        self.nrm.wait(pe, b)
        T.wait_free(pe, b, 0)
        for t in range(QT):
            mm = pe.transpose(T.bank(0)[:, t * 128:t * 128 + 128], self.nrm.xn[:, t, :], g["ident"][:, :])
        mm.then_inc(T.full(0), 1)
        yield
        for k in range(1, self.CH + 1):
            if k == 1:
                T.wait_emptied(pe, b, 0)
            key, c = ("q", k - 1) if k <= self.nq else ("k", k - 1 - self.nq)
            T.wait_free(pe, b, k)
            for r in range(2 if self.rope else 1):
                mm = pe.matmul(T.bank(k)[:, r * S:(r + 1) * S], w(key + "r" * r)[:, c * 128:c * 128 + 128],
                               xnT[:, :], start=True, stop=True)
            mm.then_inc(T.full(k), 1)
            yield
        k = self.V_USE
        for t0 in range(0, QT, QT // self.v_uses):
            T.wait_free(pe, b, k)
            for t in range(t0, t0 + QT // self.v_uses):
                mm = pe.matmul(T.bank(k)[:, (t - t0) * nv:(t - t0 + 1) * nv],
                               xnT[:, t * 128:t * 128 + 128], w("v"), start=True, stop=True)
            mm.then_inc(T.full(k), 1)
            k += 1
        if self.gates:
            T.wait_free(pe, b, k)
            for t in range(QT):
                mm = pe.matmul(T.bank(k)[:, t * 2 * H:(t + 1) * 2 * H], xnT[:, t * 128:t * 128 + 128],
                               w("g"), start=True, stop=True)
            mm.then_inc(T.full(k), 1)
        yield
        if not self.rope:
            yield
            yield
        for i in range(NI + LAG + 1):
            if i == 0:
                pe.wait_ge(self.joined, b * self.CH + self.nq)
            if i < NI:
                u, qt = divmod(i, QT)
                n = self.keys_of(qt)
                kh = self.khead(2 * u)
                if self.share:
                    pe.wait_ge(self.kbd_pool if kh // 2 % 2 else self.kbd_vector, b * (H // 4) + kh // 4 + 1)
                else:
                    pe.wait_ge(self.kbd_pool, b * (self.nk * self.kreps // 2) + kh // 2 + 1)
                pe.wait_ge(self.exp_done, b * NI + max(i + 1, self.SR))
                so = self.scores[i % self.SR][:, :].rearrange("p (j k) -> p j k", j=2)[:, :, 0:n]
                mm = pe.matmul(so, self.q_sb[:, u * self.nq // self.NP, qt * 128:qt * 128 + 128],
                               self.kbd[:, kh:kh + 2, 0:n], start=True, stop=not self.causal)
                if self.causal:
                    mm = pe.matmul(so[:, :, n - 128:n], g["identb"][:, :],
                                   g["tri"][:, :].unsqueeze(1).to_broadcast([128, 2, 128]),
                                   start=False, stop=True)
                mm.then_inc(self.s_filled, 1)
            gr = self.ended_group(i - LAG - 1)
            if gr is not None:
                self.products(pe, b, gr)
            j = i - LAG
            if 0 <= j < NI:
                nb = self.keys_of(j % QT) // 128
                k = self.item_use(j)
                pe.wait_ge(self.p_done, b * NI + j + 1)
                T.wait_free(pe, b, k)
                for hh in range(2):
                    for kt in range(nb):
                        at = (hh * nb + kt) * 128
                        mm = pe.transpose(T.bank(k)[:, at:at + 128],
                                          self.P[j % self.PR][:, hh, kt * 128:kt * 128 + 128], g["ident"][:, :])
                mm.then_inc(T.full(k), 1)
            yield
        k = self.OUT
        T.wait_emptied(pe, b, self.group_use(self.NG - 1))
        T.wait_free(pe, b, k)
        for t in range(QT):
            for gr in range(self.NG):
                mm = pe.matmul(T.bank(k)[:, t * 128:t * 128 + 128], self.OT[:, gr, t * 128:t * 128 + 128],
                               w("o")[:, gr * 128:gr * 128 + 128], start=(gr == 0), stop=(gr == self.NG - 1))
        mm.then_inc(T.full(k), 1)
        yield

    def products(self, pe, b, gr):
        T, MW, k = self.T, self.MW, self.group_use(gr)
        T.wait_emptied(pe, b, k - 2)
        T.wait_emptied(pe, b, k - 1)
        T.wait_free(pe, b, k)
        for u in range(gr * self.per_group, (gr + 1) * self.per_group):
            for hh in range(2):
                h = 2 * u + hh
                row = MW * (h % (128 // MW))
                for kt in range(QT):
                    q0 = 128 * kt if self.causal else 0
                    mm = pe.matmul(T.bank(k)[row:row + MW, q0:S], self.v_sb[:, kt, h * (self.nv // self.d) // H, :],
                                   self.PT[u % self.NB][:, hh, kt, q0:S], start=(kt == 0), stop=(kt == QT - 1),
                                   tile_position=(0, row))
        mm.then_inc(T.full(k), 1)

    def pt_copy(self, copy, eng, b, j):
        T = self.T
        u, qt = divmod(j, QT)
        nb = self.keys_of(qt) // 128
        k = self.item_use(j)
        T.wait_filled(eng, b, k)
        gr = u // self.per_group
        if gr >= 2:
            T.wait_filled(eng, b, self.group_use(gr - 2))
        copy(self.PT[u % self.NB][:, :, 0:nb, qt * 128:qt * 128 + 128],
             T.bank(k)[:, 0:2 * nb * 128].rearrange("p (j t q) -> p j t q", j=2, t=nb)).then_inc(T.free(k), 1)

    def ot_copy(self, copy, eng, b, gr):
        k = self.group_use(gr)
        self.T.wait_filled(eng, b, k)
        copy(self.OT[:, gr, :], self.T.bank(k)[:, 0:S]).then_inc(self.T.free(k), 1)

    def scalar(self, act, b):
        T, NI, LAG, CH = self.T, self.NI, self.LAG, self.CH

        def copy(dst, src):
            return act.activation(dst, src, ACT.Copy)

        T.wait_filled(act, b, 0)
        copy(self.xnT[:, :], T.bank(0)[:, 0:S]).then_inc(T.free(0), 1)
        yield
        for k in range(1, CH + 1):
            if not self.rope:
                T.wait_filled(act, b, k)
                act.activation(self.tmp[:, k - 1, 0, :], T.bank(k)[:, 0:S], ACT.Abs).then_inc(self.soft_abs, 1)
            yield
        if self.gates:
            T.wait_filled(act, b, self.G_USE)
            act.activation(self.gate[:, :, :, :], T.bank(self.G_USE)[:, 0:QT * 2 * H]
                           .rearrange("p (t g h) -> p t g h", t=QT, g=2), ACT.Exp, scale=-1.0)\
                .then_inc(T.free(self.G_USE), 1)
        yield
        if not self.rope:
            a = self.tmp[:, :, 0, :]
            act.wait_ge(self.soft_abs, b * CH + CH)
            act.activation(a, a, ACT.Exp, scale=-1.0).then_inc(self.soft_exp, 1)
            yield
            act.wait_ge(self.soft_exp, b + 1)
            act.activation(a, a, ACT.Ln, bias=1.0).then_inc(self.soft_ln, 1)
            yield
        for i in range(NI + LAG + 1):
            gr = self.ended_group(i - LAG - 1)
            if gr is not None and self.causal:
                self.ot_copy(copy, act, b, gr)
            if i < NI:
                n = self.keys_of(i % QT)
                act.wait_ge(self.max_done, b * NI + i + 1)
                if i >= self.PR:
                    T.wait_filled(act, b, self.item_use(i - self.PR))
                m = i % self.PR
                for hh in range(2):
                    e = act.activation(self.P[m][:, hh, 0:n], self.scores[i % self.SR][:, hh * S:hh * S + n], ACT.Exp,
                                       bias=self.nmax[:, m, hh:hh + 1], accum_out=self.sums[:, m, hh:hh + 1])
                e.then_inc(self.exp_done, 1)
            j = i - LAG
            if 0 <= j < NI and j % QT == self.act_tile:
                self.pt_copy(copy, act, b, j)
            yield
        yield

    def vector(self, v, b):
        T, NI, LAG, CH, w, x = self.T, self.NI, self.LAG, self.CH, self.w, self.g["x"]
        SCALE = self.d ** -0.5
        yield
        for k in range(1, CH + 1):
            T.wait_filled(v, b, k)
            if self.rope:
                part = self.tmp[:, (k - 1) % 2, :, :]
                scale = SCALE if k <= self.nq else 1.0
                if k > 2:
                    v.wait_ge(self.joined, b * CH + k - 2)
                v.scalar_tensor_tensor(part[:, 0, :], T.bank(k)[:, 0:S], scale, w("cos"), ALU.mult, ALU.mult)
                v.scalar_tensor_tensor(part[:, 1, :], T.bank(k)[:, S:2 * S], scale, w("sin"), ALU.mult, ALU.mult)\
                    .then_inc(self.parts, 1)
                v.wait_ge(self.parts, b * CH + k)
                v.sem_inc(T.free(k), 1)
            else:
                v.wait_ge(self.soft_abs, b * CH + k)
                v.tensor_scalar(self.tmp[:, k - 1, 1, :], T.bank(k)[:, 0:S], 0.0, None, ALU.max).then_inc(T.free(k), 1)
            yield
        if self.rope and self.share:
            for c in range(self.nk):
                self.lone_keys_vector(v, b, c)
        for n in range(self.v_uses):
            k = self.V_USE + n
            T.wait_filled(v, b, k)
            t = QT // self.v_uses
            v.tensor_copy(self.v_sb[:, n * t:(n + 1) * t, :, 0:self.d],
                          T.bank(k)[:, 0:t * self.nv].rearrange("p (t h d) -> p t h d", t=t, d=self.d))\
                .then_inc(T.free(k), 1)
        if self.gates:
            gate, step = self.gate, self.gate_step
            T.wait_emptied(v, b, self.G_USE)
            v.tensor_scalar(gate[:, :, :, :], gate[:, :, :, :], 1.0, None, ALU.add).then_inc(step, 1)
            v.wait_ge(step, 3 * b + 1)
            v.reciprocal(gate[:, :, :, :], gate[:, :, :, :]).then_inc(step, 1)
            v.wait_ge(step, 3 * b + 2)
            v.tensor_tensor(self.gsum[:, :, :], gate[:, :, 0, :], gate[:, :, 1, :], ALU.add).then_inc(step, 1)
            v.wait_ge(step, 3 * b + 3)
        yield
        if not self.rope:
            yield
            v.wait_ge(self.soft_ln, b + 1)
            T.wait_emptied(v, b, CH)
            v.tensor_tensor(self.tmp[:, :, 1, :], self.tmp[:, :, 1, :], self.tmp[:, :, 0, :], ALU.add)\
                .then_inc(self.soft_sum, 1)
            v.wait_ge(self.soft_sum, b + 1)
            for k in range(1, CH + 1):
                isk = k > self.nq
                v.scalar_tensor_tensor(self.chunk(k), self.tmp[:, k - 1, 1, :], 1.0 if isk else SCALE,
                                       self.ktab[:, k - 1 - self.nq, :] if isk else w("cos"),
                                       ALU.mult, ALU.mult).then_inc(self.joined, 1)
            for c in range(self.nk):
                self.lone_keys_vector(v, b, c)
            yield
        for i in range(NI + LAG + 1):
            gr = self.ended_group(i - LAG - 1)
            if gr is not None and not self.causal:
                self.ot_copy(v.tensor_copy, v, b, gr)
            if i < NI:
                n = self.keys_of(i % QT)
                v.wait_ge(self.s_filled, b * NI + i + 1)
                v.tensor_reduce(self.nmax[:, i % self.PR, :],
                                self.scores[i % self.SR][:, :].rearrange("p (j k) -> p j k", j=2)[:, :, 0:n],
                                AX.X, ALU.max, negate=True).then_inc(self.max_done, 1)
            j = i - 1
            if 0 <= j < NI:
                m = j % self.PR
                v.wait_ge(self.exp_done, b * NI + j + 1 + self.SR)
                v.reciprocal(self.rec[:, m, :], self.sums[:, m, :]).then_inc(self.rec_done, 1)
                if self.gates:
                    u, qt = divmod(j, QT)
                    v.wait_ge(self.rec_done, b * NI + j + 1)
                    v.tensor_tensor(self.weight[:, m, :], self.rec[:, m, :], self.gsum[:, qt, 2 * u:2 * u + 2],
                                    ALU.mult).then_inc(self.weight_done, 1)
            j = i - LAG
            if 0 <= j < NI and j % QT != self.act_tile:
                self.pt_copy(v.tensor_copy, v, b, j)
            if i == NI:
                self.nrm.take_moments(v, b + 1)
            if i == NI + 1:
                self.nrm.norm_rows(v, b + 1)
            yield
        k, c = self.OUT, self.batch(b)
        T.wait_filled(v, b, k)
        v.tensor_tensor(x[:, bass.ds(QT * c, QT), :], x[:, bass.ds(QT * c, QT), :],
                        T.bank(k)[:, 0:QT * 128].rearrange("p (t f) -> p t f", t=QT),
                        ALU.add).then_inc(T.free(k), 1)
        yield


def self_attention(nc, g, name, wts, spec):
    LANES = 2
    nk, rope = spec["kchunks"], spec["rope"]
    st = Stage(nc, name)
    w, loaded = wts.of, wts.loaded
    ktab = st.sb("ktab", [128, nk, S])
    turned = st.sb("turned", [128, nk, S])
    phase = st.sb("phase", [128, 4, nk])
    tables, step = st.sem("tables"), st.sem("step")

    lanes = [SelfLane(st, n, LANES, g, w, ktab, spec) for n in range(LANES)]

    with nc.Block(f"{name}_block") as block:
        @block.sync
        def _(sp):
            for ln in lanes:
                ln.sync_setup(sp)

        @block.gpsimd
        def _(pool):
            for ln in lanes:
                ln.pool_setup(pool)
            pool.wait_ge(loaded, 16)
            for ln in lanes:
                ln.nrm.pool(pool, 0)
            with pool.Fori(0, B // LANES) as i:
                in_turn(*(ln.pool(pool, i) for ln in lanes))

        @block.tensor
        def _(pe):
            pe.wait_ge(loaded, 16)
            with pe.Fori(0, B // LANES) as i:
                in_turn(*(ln.tensor(pe, i) for ln in lanes))

        @block.scalar
        def _(act):
            if not rope:
                act.wait_ge(tables, 1)
                act.activation(phase[:, 1, :], phase[:, 0, :], ACT.Sin).then_inc(tables, 1)
                act.activation(phase[:, 2, :], phase[:, 0, :], ACT.Sin, scale=0.5).then_inc(tables, 1)
            with act.Fori(0, B // LANES) as i:
                in_turn(*(ln.scalar(act, i) for ln in lanes))

        @block.vector
        def _(v):
            v.wait_ge(loaded, 16)
            if not rope:
                v.tensor_scalar(phase[:, 3, :], w("bias"), 0.0, -2 * np.pi, ALU.min, ALU.max).then_inc(step, 1)
                v.wait_ge(step, 1)
                v.tensor_scalar(phase[:, 3, :], phase[:, 3, :], np.pi, 3.1415925, ALU.add, ALU.min)\
                    .then_inc(step, 1)
                v.wait_ge(step, 2)
                v.tensor_scalar(phase[:, 0, :], phase[:, 3, :], -3.1415925, None, ALU.max).then_inc(tables, 1)
                v.wait_ge(tables, 3)
                v.tensor_tensor(phase[:, 3, :], phase[:, 2, :], phase[:, 2, :], ALU.mult).then_inc(step, 1)
                v.wait_ge(step, 3)
                v.tensor_scalar(phase[:, 2, :], phase[:, 3, :], 2.0, -1.0, ALU.mult, ALU.add).then_inc(step, 1)
                v.wait_ge(step, 4)
                for c in range(nk):
                    v.tensor_scalar(turned[:, c, :], w("turn"), phase[:, 1, c:c + 1], None, ALU.mult)\
                        .then_inc(step, 1)
                for c in range(nk):
                    v.wait_ge(step, 5 + c)
                    v.scalar_tensor_tensor(ktab[:, c, :], w("cos"), phase[:, 2, c:c + 1], turned[:, c, :],
                                           ALU.mult, ALU.subtract).then_inc(tables, 1)
                v.wait_ge(tables, 3 + nk)
            for ln in lanes:
                v.wait_ge(ln.v_set, 1)
                ln.nrm.take_moments(v, 0)
            for ln in lanes:
                ln.nrm.norm_rows(v, 0)
            with v.Fori(0, B // LANES) as i:
                in_turn(*(ln.vector(v, i) for ln in lanes))
    st.close()


class CrossLane:
    HI = 8
    NI = QT * H // HI
    SR = 2
    XT, Q, V, I0 = 0, 1, 2, 3

    def __init__(self, st, lane, lanes, g, w, kT, qbias, w1s, mode):
        self.g, self.w, self.kT, self.qbias, self.w1s, self.mode = g, w, kT, qbias, w1s, mode
        self.stats = mode == "stats"
        st = Lane(st, lane, lanes)
        self.batch = st.batch
        HI, NI = self.HI, self.NI
        self.T = Ring(st, "t", 2, 4 if self.stats else self.I0 + NI + 2)
        self.scores = [st.ps(f"s{i}") for i in range(self.SR)]
        self.nrm = Norm(st, g["x"])
        self.xnT = st.sb("xnT", [128, S])
        self.q_sb = st.sb("q", [128, S])
        self.kbd = st.sb("kbd", [128, H, SC])
        self.ctx2 = st.sb("ctx2", [128, 2, SC])
        self.vbd = st.sb("vbd", [128, H // 2, 32])
        self.P = st.sb("p", [128, NI, HI, SC])
        self.sq = st.sb("sq", [128, NI, HI, SC]) if self.stats else None
        self.PT = st.sb("pt", [128, H // 2, S])
        self.OT = st.sb("ot", [128, 2, S])
        self.top = st.sb("top", [128, NI, HI])
        self.sums = st.sb("sums", [128, NI, HI])
        self.rec = st.sb("rec", [128, NI, HI])
        self.row = st.sb("row", [128, 3, NI, HI]) if self.stats else None
        self.factor = st.sb("factor", [128, H])
        self.kbd_done, self.ctx2_done = st.sem("kbd_done"), st.sem("ctx2_done")
        self.v_set, self.v_half = st.sem("v_set"), st.sem("v_half")
        self.s_filled, self.top_done, self.sub_done = st.sem("s_filled"), st.sem("top_done"), st.sem("sub_done")
        self.factor_done, self.tempered = st.sem("factor_done"), st.sem("tempered")
        self.exp_done, self.sum_done, self.rec_done = st.sem("exp_done"), st.sem("sum_done"), st.sem("rec_done")
        self.p_done, self.sq_done, self.rows_done = st.sem("p_done"), st.sem("sq_done"), st.sem("rows_done")
        self.added = st.sem("added")

    def sync_setup(self, sp):
        self.T.credit(sp)
        sp.sem_inc(self.sub_done, self.SR)

    def pool_setup(self, pool):
        self.nrm.pool_setup(pool)
        pool.memset(self.vbd[:, :, :], 0.0).then_inc(self.v_set, 1)

    def pool(self, pool, b):
        HI, NI, P = self.HI, self.NI, self.P
        for h in range(0, H, 4):
            pool.tensor_tensor(self.kbd[:, h:h + 4, :],
                               self.kT[:, self.batch(b), :].unsqueeze(1).to_broadcast([128, 4, SC]),
                               self.w("kmask")[:, h:h + 4].unsqueeze(2).to_broadcast([128, 4, SC]),
                               ALU.mult).then_inc(self.kbd_done, 1)
        yield
        if self.mode == "tempered":
            pool.tensor_copy(self.factor[:, :], self.g["factor"][:, self.batch(b), :]).then_inc(self.factor_done, 1)
            pool.wait_ge(self.factor_done, b + 1)
        yield
        for s in range(NI + 3):
            i = s - 1
            if self.mode == "tempered" and 0 <= i < NI:
                hh = i % 2
                pool.wait_ge(self.sub_done, b * NI + i + 1 + self.SR)
                pool.tensor_tensor(P[:, i, :, :], P[:, i, :, :],
                                   self.factor[:, hh * HI:hh * HI + HI].unsqueeze(2)
                                   .to_broadcast([128, HI, SC]), ALU.mult).then_inc(self.tempered, 1)
            i = s - 2
            if 0 <= i < NI:
                pool.wait_ge(self.rec_done, b * NI + i + 1)
                pool.tensor_tensor(P[:, i, :, :], P[:, i, :, :],
                                   self.rec[:, i, :].unsqueeze(2).to_broadcast([128, HI, SC]),
                                   ALU.mult).then_inc(self.p_done, 1)
            if s == NI + 1:
                self.nrm.pool(pool, b + 1)
            yield

    def tensor(self, pe, b):
        HI, NI, T, w, g = self.HI, self.NI, self.T, self.w, self.g
        self.nrm.wait(pe, b)
        T.wait_free(pe, b, self.XT)
        for t in range(QT):
            mm = pe.transpose(T.bank(self.XT)[:, t * 128:t * 128 + 128], self.nrm.xn[:, t, :], g["ident"][:, :])
        mm.then_inc(T.full(self.XT), 1)
        yield
        T.wait_emptied(pe, b, self.XT)
        T.wait_free(pe, b, self.Q)
        pe.matmul(T.bank(self.Q)[:, 0:S], w("q"), self.xnT[:, :], start=True, stop=True).then_inc(T.full(self.Q), 1)
        pe.wait_ge(self.ctx2_done, b + 1)
        T.wait_free(pe, b, self.V)
        pe.matmul(T.bank(self.V)[:, 0:D], self.ctx2[:, :, :], w("v"), start=True, stop=True)\
            .then_inc(T.full(self.V), 1)
        yield
        for s in range(NI + 3):
            i = s
            if i == 0:
                T.wait_emptied(pe, b, self.Q)
            if i < NI:
                t, hh = divmod(i, 2)
                if i < 2:
                    pe.wait_ge(self.kbd_done, b * 4 + 2 * i + 2)
                pe.wait_ge(self.sub_done, b * NI + i + 1)
                bank = self.scores[i % self.SR]
                mm = pe.matmul(bank[:, :], self.q_sb[:, t * 128:t * 128 + 128],
                               self.kbd[:, hh * HI:hh * HI + HI, :], start=True, stop=(self.mode != "plain"))
                if self.mode == "plain":
                    mm = pe.matmul(bank[:, :].rearrange("p (h k) -> p h k", h=HI), g["onesb"][:, :],
                                   g["pad"][:, self.batch(b), :].unsqueeze(1).to_broadcast([128, HI, SC]),
                                   start=False, stop=True)
                mm.then_inc(self.s_filled, 1)
            i = s - 3
            if i >= 0 and not self.stats:
                pe.wait_ge(self.p_done, b * NI + i + 1)
                T.wait_free(pe, b, self.I0 + i)
                for m in range(4):
                    mm = pe.transpose(T.bank(self.I0 + i)[:, m * 128:m * 128 + 128],
                                      self.P[:, i, 2 * m:2 * m + 2, :], g["ident"][:, :])
                mm.then_inc(T.full(self.I0 + i), 1)
            yield
        if self.stats:
            pe.wait_ge(self.rows_done, b * 3 * NI + 3 * NI)
            k = self.I0
            T.wait_free(pe, b, k)
            n = 0
            for f in range(3):
                for t in range(QT):
                    mm = pe.matmul(T.bank(k)[0:64, 0:H], self.w1s[:, f * 64:f * 64 + 64],
                                   self.row[:, f, 2 * t:2 * t + 2, :], start=(n == 0), stop=(n == 3 * QT - 1))
                    n += 1
            mm.then_inc(T.full(k), 1)
            yield
        else:
            k = self.I0 + NI
            pe.wait_ge(self.v_half, 2 * b + 2)
            T.wait_emptied(pe, b, k - 2)
            T.wait_emptied(pe, b, k - 1)
            for m in range(H // 2):
                gr, j = divmod(m, 4)
                mm = pe.matmul(T.bank(k)[32 * j:32 * j + 32, gr * S:gr * S + S], self.vbd[:, m, :], self.PT[:, m, :],
                               start=True, stop=True, tile_position=(0, 32 * j))
            mm.then_inc(T.full(k), 1)
            yield
            T.wait_emptied(pe, b, k)
            k += 1
            for t in range(QT):
                for gr in range(2):
                    mm = pe.matmul(T.bank(k)[:, t * 128:t * 128 + 128],
                                   self.OT[:, gr, t * 128:t * 128 + 128], w("o")[:, gr * 128:gr * 128 + 128],
                                   start=(gr == 0), stop=(gr == 1))
            mm.then_inc(T.full(k), 1)
            yield

    def scalar(self, act, b):
        NI, T = self.NI, self.T
        T.wait_filled(act, b, self.XT)
        act.activation(self.xnT[:, :], T.bank(self.XT)[:, 0:S], ACT.Copy).then_inc(T.free(self.XT), 1)
        yield
        T.wait_filled(act, b, self.Q)
        act.activation(self.q_sb[:, :], T.bank(self.Q)[:, 0:S], ACT.Identity, scale=self.SCALE[self.mode],
                       bias=self.qbias[:, :]).then_inc(T.free(self.Q), 1)
        yield
        for s in range(NI + 3):
            i = s - 3
            if i >= 0 and self.stats:
                act.wait_ge(self.p_done, b * NI + i + 1)
                act.activation(self.sq[:, i, :, :], self.P[:, i, :, :], ACT.Square, bias=self.g["minus_mean"][:, :])\
                    .then_inc(self.sq_done, 1)
            if i >= 0 and not self.stats:
                t, hh = divmod(i, 2)
                T.wait_filled(act, b, self.I0 + i)
                act.activation(self.PT[:, 4 * hh:4 * hh + 4, t * 128:t * 128 + 128],
                               T.bank(self.I0 + i)[:, :].rearrange("p (m q) -> p m q", m=4), ACT.Copy)\
                    .then_inc(T.free(self.I0 + i), 1)
            i = s - 1
            if 0 <= i < NI:
                if self.mode == "tempered":
                    act.wait_ge(self.tempered, b * NI + i + 1)
                else:
                    act.wait_ge(self.sub_done, b * NI + i + 1 + self.SR)
                act.activation(self.P[:, i, :, :], self.P[:, i, :, :], ACT.Exp).then_inc(self.exp_done, 1)
            yield
        if not self.stats:
            k = self.I0 + NI
            T.wait_filled(act, b, k)
            act.activation(self.OT[:, :, :], T.bank(k)[:, :].rearrange("p (g q) -> p g q", g=2), ACT.Copy)\
                .then_inc(T.free(k), 1)
        yield

    def vector(self, v, b):
        HI, NI, T, w, g, P = self.HI, self.NI, self.T, self.w, self.g, self.P
        d = D // H
        x, c = g["x"], self.batch(b)
        v.tensor_copy(self.ctx2[:, :, :], g["ctxT"][:, c, :].unsqueeze(1).to_broadcast([128, 2, SC]))\
            .then_inc(self.ctx2_done, 1)
        yield
        T.wait_filled(v, b, self.V)
        for j in range(2):
            lo = 64 * j
            vv = T.bank(self.V)[lo:lo + 64, 0:D].rearrange("p (m j e) -> p m j e", j=2, e=d)[:, :, j, :]
            bb = w("vb")[lo:lo + 64, :].rearrange("p (m j e) -> p m j e", j=2, e=d)[:, :, j, :]
            v.tensor_tensor(self.vbd[lo:lo + 64, :, d * j:d * j + d], vv, bb, ALU.add).then_inc(self.v_half, 1)
        v.wait_ge(self.v_half, 2 * b + 2)
        v.sem_inc(T.free(self.V), 1)
        yield
        for s in range(NI + 3):
            i = s
            if i < NI:
                v.wait_ge(self.s_filled, b * NI + i + 1)
                sv = self.scores[i % self.SR][:, :].rearrange("p (h k) -> p h k", h=HI)
                dst = self.row[:, 1, i, :] if self.stats else self.top[:, i, :]
                v.tensor_reduce(dst, sv, AX.X, ALU.max).then_inc(self.top_done, 1)
                if self.stats:
                    v.tensor_reduce(self.row[:, 0, i, :], sv, AX.X, ALU.add).then_inc(self.rows_done, 1)
            i = s - 1
            if 0 <= i < NI:
                sv = self.scores[i % self.SR][:, :].rearrange("p (h k) -> p h k", h=HI)
                src = self.row[:, 1, i, :] if self.stats else self.top[:, i, :]
                v.wait_ge(self.top_done, b * NI + i + 1)
                v.tensor_tensor(P[:, i, :, :], sv, src.unsqueeze(2).to_broadcast([128, HI, SC]),
                                ALU.subtract).then_inc(self.sub_done, 1)
            i = s - 2
            if 0 <= i < NI:
                v.wait_ge(self.exp_done, b * NI + i + 1)
                v.tensor_reduce(self.sums[:, i, :], P[:, i, :, :], AX.X, ALU.add).then_inc(self.sum_done, 1)
                v.wait_ge(self.sum_done, b * NI + i + 1)
                v.reciprocal(self.rec[:, i, :], self.sums[:, i, :]).then_inc(self.rec_done, 1)
            i = s - 3
            if i >= 0 and self.stats:
                v.wait_ge(self.sq_done, b * NI + i + 1)
                v.tensor_reduce(self.row[:, 2, i, :], self.sq[:, i, :, :], AX.X, ALU.add).then_inc(self.rows_done, 2)
            if s == NI + 1:
                self.nrm.take_moments(v, b + 1)
            if s == NI + 2:
                self.nrm.norm_rows(v, b + 1)
            yield
        if self.stats:
            k = self.I0
            T.wait_filled(v, b, k)
            v.tensor_copy(g["hidden"][:, c, :], T.bank(k)[0:64, 0:H]).then_inc(T.free(k), 1)
            yield
        else:
            yield
            k = self.I0 + NI + 1
            T.wait_filled(v, b, k)
            v.tensor_tensor(x[:, bass.ds(QT * c, QT), :], x[:, bass.ds(QT * c, QT), :],
                            T.bank(k)[:, 0:QT * 128].rearrange("p (t f) -> p t f", t=QT),
                            ALU.add).then_inc(T.free(k), 1)
            T.wait_emptied(v, b, k)
            v.tensor_tensor(x[:, bass.ds(QT * c, QT), :], x[:, bass.ds(QT * c, QT), :],
                            w("ob").unsqueeze(1).to_broadcast([128, QT, D]), ALU.add).then_inc(self.added, 1)
            yield

    SCALE = {"plain": (D // H) ** -0.5, "stats": (D // H) ** -0.5, "tempered": 1.0}


def cross_attention(nc, g, name, wts, mode):
    LANES = 2
    SCALE = CrossLane.SCALE[mode]
    st = Stage(nc, name)
    w, loaded = wts.of, wts.loaded
    kT = st.sb("kT", [128, B, SC])
    qbias = st.sb("qbias", [128, 1])
    w1s = st.sb("w1s", [128, 3 * 64]) if mode == "stats" else None
    set_up, w1s_done = st.sem("set_up"), st.sem("w1s_done")
    kT_filled, kT_done = st.sem("kT_filled"), st.sem("kT_done")

    lanes = [CrossLane(st, n, LANES, g, w, kT, qbias, w1s, mode) for n in range(LANES)]
    kps = lanes[0].scores[0]

    with nc.Block(f"{name}_block") as block:
        @block.sync
        def _(sp):
            for ln in lanes:
                ln.sync_setup(sp)

        @block.gpsimd
        def _(pool):
            for ln in lanes:
                ln.pool_setup(pool)
            for ln in lanes:
                ln.nrm.pool(pool, 0)
            pool.wait_ge(kT_done, 1)
            with pool.Fori(0, B // LANES) as i:
                in_turn(*(ln.pool(pool, i) for ln in lanes))

        @block.tensor
        def _(pe):
            pe.wait_ge(loaded, 16)
            pe.matmul(kps[:, :], w("k"), g["ctxT"][:, :, :], start=True, stop=True).then_inc(kT_filled, 1)
            pe.wait_ge(kT_done, 1)
            if mode == "stats":
                pe.wait_ge(w1s_done, 3)
            with pe.Fori(0, B // LANES) as i:
                in_turn(*(ln.tensor(pe, i) for ln in lanes))

        @block.scalar
        def _(act):
            act.wait_ge(loaded, 16)
            act.activation(qbias[:, :], w("qb"), ACT.Copy, scale=SCALE).then_inc(set_up, 1)
            act.wait_ge(kT_filled, 1)
            act.activation(kT[:, :, :], kps[:, :].rearrange("p (b k) -> p b k", b=B), ACT.Identity, bias=w("kb"))\
                .then_inc(kT_done, 1)
            act.wait_ge(set_up, 1)
            with act.Fori(0, B // LANES) as i:
                in_turn(*(ln.scalar(act, i) for ln in lanes))

        @block.vector
        def _(v):
            v.wait_ge(loaded, 16)
            if mode == "stats":
                for f, n in enumerate((SC * S, S, (SC - 1) * S)):
                    v.tensor_scalar(w1s[:, f * 64:f * 64 + 64], w("w1")[:, f * 64:f * 64 + 64], 1.0 / n, None,
                                    ALU.mult).then_inc(w1s_done, 1)
            for ln in lanes:
                v.wait_ge(ln.v_set, 1)
                ln.nrm.take_moments(v, 0)
            for ln in lanes:
                ln.nrm.norm_rows(v, 0)
            with v.Fori(0, B // LANES) as i:
                in_turn(*(ln.vector(v, i) for ln in lanes))
    st.close()


def temperature(nc, g, wts):
    st = Stage(nc, "temp")
    loaded = wts.loaded
    ps = st.ps("ps")
    N = B * H
    h1 = st.sb("h1", [64, N])
    h2 = st.sb("h2", [64, N])
    lt = st.sb("lt", [128, N])
    product = st.sem("product")
    gelu = st.sem("gelu")
    clipped = st.sem("clipped")
    done = st.sem("done")

    def w(key, rows=64):
        return wts.of(key)[0:rows, :]

    with nc.Block("temp_block") as block:
        @block.scalar
        def _(act):
            act.wait_ge(loaded, 16)
            act.activation(h1[:, :], g["hidden"][:, :, :].rearrange("p b h -> p (b h)"), ACT.Gelu, bias=w("b1"))\
                .then_inc(gelu, 1)
            act.wait_ge(product, 1)
            act.activation(h2[:, :], ps[0:64, 0:N], ACT.Gelu, bias=w("b2")).then_inc(gelu, 1)
            act.wait_ge(clipped, 2)
            act.activation(lt[:, :], lt[:, :], ACT.Exp, scale=-1.0).then_inc(clipped, 1)

        @block.tensor
        def _(pe):
            pe.wait_ge(loaded, 16)
            pe.wait_ge(gelu, 1)
            pe.matmul(ps[0:64, 0:N], w("w2"), h1[:, :], start=True, stop=True).then_inc(product, 1)
            pe.wait_ge(gelu, 2)
            pe.matmul(ps[:, N:2 * N], w("w3"), h2[:, :], start=True, stop=True).then_inc(product, 1)

        @block.vector
        def _(v):
            v.wait_ge(loaded, 16)
            v.wait_ge(product, 2)
            v.tensor_scalar(lt[:, :], ps[:, N:2 * N], w("b3", 128), float(np.log(10.0)), ALU.add, ALU.min)\
                .then_inc(clipped, 1)
            v.wait_ge(clipped, 1)
            v.tensor_scalar(lt[:, :], lt[:, :], float(np.log(0.1)), None, ALU.max).then_inc(clipped, 1)
            v.wait_ge(clipped, 3)
            v.tensor_scalar(g["factor"][:, :, :].rearrange("p b h -> p (b h)"), lt[:, :], 0.5, None, ALU.mult)\
                .then_inc(done, 1)
    st.close()


def L2_xattn(nc, g, wts):
    with nc.sbuf_tensor("hidden", [64, B, H], F32) as hidden, nc.sbuf_tensor("factor", [128, B, H], F32) as factor:
        g["hidden"], g["factor"] = hidden, factor
        cross_attention(nc, g, "l2xs", wts, "stats")
        temperature(nc, g, wts)
        cross_attention(nc, g, "l2x", wts, "tempered")


class L0_xattn_lane:
    XT, Q, V, SCORES, PTURNED, OUT = 0, 1, 2, 3, 4, 5

    def __init__(self, st, lane, lanes, g, w, kT, qbias, keep, fill):
        self.g, self.w, self.kT, self.qbias, self.keep, self.fill = g, w, kT, qbias, keep, fill
        st = Lane(st, lane, lanes)
        self.batch = st.batch
        self.T = Ring(st, "t", 2, self.OUT + QT)
        self.nrm = Norm(st, g["x"])
        self.xnT = st.sb("xnT", [128, S])
        self.q_sb = st.sb("q", [128, S])
        self.ctx1 = st.sb("ctx1", [128, 2, SC])
        self.v_sb = st.sb("v", [2 * SC, D])
        self.P = st.sb("p", [128, QT, SC])
        self.P2 = st.sb("p2", [128, QT, SC])
        self.PT = st.sb("pt", [QT * SC, 128])
        self.top = st.sb("top", [128, QT])
        self.sums = st.sb("sums", [128, QT])
        self.rec = st.sb("rec", [128, QT])
        self.ctx1_done, self.masked, self.top_done = st.sem("ctx1_done"), st.sem("masked"), st.sem("top_done")
        self.less_top, self.exp_done, self.sum_done = st.sem("less_top"), st.sem("exp_done"), st.sem("sum_done")
        self.rec_done, self.p_done = st.sem("rec_done"), st.sem("p_done")

    def pool(self, pool, b):
        self.nrm.pool(pool, b + 1)
        yield

    def tensor(self, pe, b):
        T, w = self.T, self.w
        self.nrm.wait(pe, b)
        T.wait_free(pe, b, self.XT)
        for t in range(QT):
            mm = pe.transpose(T.bank(self.XT)[:, t * 128:t * 128 + 128], self.nrm.xn[:, t, :], self.g["ident"][:, :])
        mm.then_inc(T.full(self.XT), 1)
        yield
        T.wait_emptied(pe, b, self.XT)
        T.wait_free(pe, b, self.Q)
        pe.matmul(T.bank(self.Q)[:, 0:S], w("q"), self.xnT[:, :], start=True, stop=True).then_inc(T.full(self.Q), 1)
        pe.wait_ge(self.ctx1_done, b + 1)
        pe.matmul(T.bank(self.V)[:, 0:D], self.ctx1[:, :, :], w("v"), start=True, stop=True)\
            .then_inc(T.full(self.V), 1)
        yield
        T.wait_emptied(pe, b, self.Q)
        for t in range(QT):
            mm = pe.matmul(T.bank(self.SCORES)[:, t * SC:t * SC + SC], self.q_sb[:, t * 128:t * 128 + 128],
                           self.kT[:, self.batch(b), :], start=True, stop=True)
        mm.then_inc(T.full(self.SCORES), 1)
        yield
        yield
        yield
        pe.wait_ge(self.p_done, b + 1)
        T.wait_free(pe, b, self.PTURNED)
        pe.transpose(T.bank(self.PTURNED)[:, 0:128], self.P2[:, :, :], self.g["ident"][:, :])\
            .then_inc(T.full(self.PTURNED), 1)
        yield
        T.wait_emptied(pe, b, self.PTURNED)
        for t in range(QT):
            k = self.OUT + t
            T.wait_free(pe, b, k)
            pe.matmul(T.bank(k)[:, 0:128], self.PT[SC * t:SC * t + SC, :], self.v_sb[SC * t:SC * t + SC, :],
                      start=True, stop=True).then_inc(T.full(k), 1)
        yield

    def scalar(self, act, b):
        T = self.T
        T.wait_filled(act, b, self.XT)
        act.activation(self.xnT[:, :], T.bank(self.XT)[:, 0:S], ACT.Copy).then_inc(T.free(self.XT), 1)
        yield
        T.wait_filled(act, b, self.Q)
        act.activation(self.q_sb[:, :], T.bank(self.Q)[:, 0:S], ACT.Identity, scale=D ** -0.5,
                       bias=self.qbias[:, :]).then_inc(T.free(self.Q), 1)
        yield
        yield
        yield
        act.wait_ge(self.less_top, b + 1)
        act.activation(self.P[:, :, :], self.P[:, :, :], ACT.Exp).then_inc(self.exp_done, 1)
        yield
        T.wait_filled(act, b, self.PTURNED)
        act.activation(self.PT[:, :], T.bank(self.PTURNED)[:, 0:128], ACT.Copy).then_inc(T.free(self.PTURNED), 1)
        yield

    def vector(self, v, b):
        T, w, P, x, c = self.T, self.w, self.P, self.g["x"], self.batch(b)
        v.tensor_copy(self.ctx1[:, :, :], self.g["ctxT"][:, c, :].unsqueeze(1).to_broadcast([128, 2, SC]))\
            .then_inc(self.ctx1_done, 1)
        yield
        T.wait_filled(v, b, self.V)
        v.tensor_tensor(self.v_sb[:, :], T.bank(self.V)[:, 0:D], w("vb"), ALU.add).then_inc(T.free(self.V), 1)
        yield
        T.wait_filled(v, b, self.SCORES)
        v.tensor_tensor(P[:, :, :], T.bank(self.SCORES)[:, 0:QT * SC].rearrange("p (t k) -> p t k", t=QT),
                        self.keep[:, :, :], ALU.mult).then_inc(T.free(self.SCORES), 1)
        yield
        T.wait_emptied(v, b, self.SCORES)
        v.tensor_tensor(P[:, :, :], P[:, :, :], self.fill[:, :, :], ALU.add).then_inc(self.masked, 1)
        v.wait_ge(self.masked, b + 1)
        v.tensor_reduce(self.top[:, :], P[:, :, :], AX.X, ALU.max).then_inc(self.top_done, 1)
        v.wait_ge(self.top_done, b + 1)
        v.tensor_tensor(P[:, :, :], P[:, :, :], self.top[:, :].unsqueeze(2).to_broadcast([128, QT, SC]),
                        ALU.subtract).then_inc(self.less_top, 1)
        yield
        self.nrm.take_moments(v, b + 1)
        yield
        v.wait_ge(self.exp_done, b + 1)
        v.tensor_reduce(self.sums[:, :], P[:, :, :], AX.X, ALU.add).then_inc(self.sum_done, 1)
        v.wait_ge(self.sum_done, b + 1)
        v.reciprocal(self.rec[:, :], self.sums[:, :]).then_inc(self.rec_done, 1)
        v.wait_ge(self.rec_done, b + 1)
        v.tensor_tensor(self.P2[:, :, :], P[:, :, :], self.rec[:, :].unsqueeze(2).to_broadcast([128, QT, SC]),
                        ALU.mult).then_inc(self.p_done, 1)
        yield
        self.nrm.norm_rows(v, b + 1)
        yield
        for t in range(QT):
            T.wait_filled(v, b, self.OUT + t)
            v.tensor_tensor(x[:, QT * c + t, :], x[:, QT * c + t, :], T.bank(self.OUT + t)[:, 0:128], ALU.add)\
                .then_inc(T.free(self.OUT + t), 1)
        yield


def L0_xattn(nc, g, wts):
    LANES = 4
    st = Stage(nc, "l0x")
    w, loaded = wts.of, wts.loaded
    qbias = st.sb("qbias", [128, 1])
    kT = st.sb("kT", [128, B, SC])
    mask8 = g["mask8"]
    keep = st.sb("keep", [128, QT, SC])
    fill = st.sb("fill", [128, QT, SC])
    set_up, masks_done = st.sem("set_up"), st.sem("masks_done")
    kT_filled, kT_done = st.sem("kT_filled"), st.sem("kT_done")

    lanes = [L0_xattn_lane(st, n, LANES, g, w, kT, qbias, keep, fill) for n in range(LANES)]
    kps = lanes[0].T.bank(0)

    with nc.Block("l0x_block") as block:
        @block.sync
        def _(sp):
            for ln in lanes:
                ln.T.credit(sp)

        @block.gpsimd
        def _(pool):
            for ln in lanes:
                ln.nrm.pool_setup(pool)
            for ln in lanes:
                ln.nrm.pool(pool, 0)
            with pool.Fori(0, B // LANES) as i:
                in_turn(*(ln.pool(pool, i) for ln in lanes))

        @block.tensor
        def _(pe):
            pe.wait_ge(loaded, 16)
            pe.matmul(kps[:, :], w("k"), g["ctxT"][:, :, :], start=True, stop=True).then_inc(kT_filled, 1)
            pe.wait_ge(kT_done, 1)
            with pe.Fori(0, B // LANES) as i:
                in_turn(*(ln.tensor(pe, i) for ln in lanes))

        @block.scalar
        def _(act):
            act.wait_ge(loaded, 16)
            act.activation(qbias[:, :], w("qb"), ACT.Copy, scale=D ** -0.5).then_inc(set_up, 1)
            act.wait_ge(kT_filled, 1)
            act.activation(kT[:, :, :], kps[:, :].rearrange("p (b k) -> p b k", b=B), ACT.Identity, bias=w("kb"))\
                .then_inc(kT_done, 1)
            act.wait_ge(set_up, 1)
            with act.Fori(0, B // LANES) as i:
                in_turn(*(ln.scalar(act, i) for ln in lanes))

        @block.vector
        def _(v):
            v.wait_ge(loaded, 16)
            v.tensor_scalar(keep[:, :, :], mask8[:, :, :], -1.0, 1.0, ALU.mult, ALU.add).then_inc(masks_done, 1)
            v.tensor_scalar(fill[:, :, :], mask8[:, :, :], -1e9, None, ALU.mult).then_inc(masks_done, 1)
            v.wait_ge(masks_done, 2)
            for ln in lanes:
                ln.nrm.take_moments(v, 0)
            for ln in lanes:
                ln.nrm.norm_rows(v, 0)
            with v.Fori(0, B // LANES) as i:
                in_turn(*(ln.vector(v, i) for ln in lanes))
    st.close()


ROUND = 1.5 * 2 ** 23


class L1_ffn_lane:
    F = 512
    FC = F // 128
    XS, HS = 6, 6

    def __init__(self, st, lane, lanes, g, wq, wmean):
        self.g, self.wq, self.wmean = g, wq, wmean
        F, FC = self.F, self.FC
        st = Lane(st, lane, lanes)
        self.batch = st.batch
        self.nrm = Norm(st, g["x"])
        self.amax = st.sb("amax", [128, QT])
        self.ascale = st.sb("ascale", [128, QT])
        self.xr = st.sb("xr", [128, QT, D])
        self.xr2 = st.sb("xr2", [128, QT, D])
        self.xq = st.sb("xq", [128, QT, D], BF16)
        self.xqT = st.sb("xqT", [128, S], BF16)
        self.back = st.sb("back", [128, QT, 3])
        self.gate = st.sb("gate", [128, QT, F])
        self.h = st.sb("h", [128, QT, F])
        self.hr = st.sb("hr", [128, QT, F])
        self.hq = st.sb("hq", [128, QT, F], BF16)
        self.hqT = st.sb("hqT", [128, QT, FC, 128], BF16)
        self.hmax = st.sb("hmax", [128, QT])
        self.hscale = st.sb("hscale", [128, QT])
        self.tps = st.ps("tps", (128, 1024), BF16)
        self.gps, self.ups, self.yps = st.ps("gps"), st.ps("ups"), st.ps("yps")
        self.xstep, self.xq_done = st.sem("xstep"), st.sem("xq_done")
        self.xT_filled, self.xT_done = st.sem("xT_filled"), st.sem("xT_done")
        self.g_filled, self.u_filled = st.sem("g_filled"), st.sem("u_filled")
        self.gate_done, self.h_done = st.sem("gate_done"), st.sem("h_done")
        self.hstep, self.hq_done = st.sem("hstep"), st.sem("hq_done")
        self.hT_filled, self.hT_done = st.sem("hT_filled"), st.sem("hT_done")
        self.y_filled, self.y_done = st.sem("y_filled"), st.sem("y_done")

    def pool(self, pool, b):
        self.nrm.pool(pool, b + 1)
        yield

    def first_products(self, pe, b, t):
        pe.wait_ge(self.h_done, QT * b + t + 1)
        for bank, n, sem in ((self.gps, 0, self.g_filled), (self.ups, 1, self.u_filled)):
            pe.matmul(bank[:, :], self.xqT[:, t * 128:t * 128 + 128], self.wq[:, n, :], start=True, stop=True)\
                .then_inc(sem, 1)

    def tensor(self, pe, b):
        FC, F, identb = self.FC, self.F, self.g["identb"]
        yield
        pe.wait_ge(self.xq_done, b + 1)
        pe.wait_ge(self.hT_done, QT * b + QT)
        for t in range(QT):
            mm = pe.transpose(self.tps[:, F + t * 128:F + t * 128 + 128], self.xq[:, t, :], identb[:, :])
        mm.then_inc(self.xT_filled, 1)
        yield
        pe.wait_ge(self.xT_done, b + 1)
        self.first_products(pe, b, 0)
        yield
        for t in range(QT):
            if t + 1 < QT:
                self.first_products(pe, b, t + 1)
            pe.wait_ge(self.hq_done, QT * b + t + 1)
            if t > 0:
                pe.wait_ge(self.hT_done, QT * b + t + QT)
            for c in range(FC):
                mm = pe.transpose(self.tps[:, c * 128:c * 128 + 128], self.hq[:, t, c * 128:c * 128 + 128], identb[:, :])
            mm.then_inc(self.hT_filled, 1)
            yield
        pe.wait_ge(self.y_done, QT * b + QT)
        for t in range(QT):
            pe.wait_ge(self.hT_done, QT * b + t + 1 + QT)
            for c in range(FC):
                mm = pe.matmul(self.yps[:, t * 128:t * 128 + 128], self.hqT[:, t, c, :],
                               self.wq[:, 2, c * 128:c * 128 + 128], start=(c == 0), stop=(c == FC - 1))
        mm.then_inc(self.y_filled, 1)
        yield

    def scalar(self, act, b):
        FC, F = self.FC, self.F
        yield
        act.wait_ge(self.xT_filled, b + 1)
        act.activation(self.xqT[:, :], self.tps[:, F:F + S], ACT.Copy).then_inc(self.xT_done, 1)
        yield
        act.wait_ge(self.xstep, self.XS * b + self.XS)
        for t in range(QT + 1):
            if t > 0:
                act.wait_ge(self.hT_filled, QT * b + t)
                act.activation(self.hqT[:, t - 1, :, :], self.tps[:, 0:F].rearrange("p (c q) -> p c q", c=FC),
                               ACT.Copy).then_inc(self.hT_done, 1)
            if t < QT:
                act.wait_ge(self.g_filled, QT * b + t + 1)
                act.activation(self.gate[:, t, :], self.gps[:, :], ACT.Silu, scale=self.back[:, t, 0:1])\
                    .then_inc(self.gate_done, 1)
            yield

    def vector(self, v, b):
        nrm, xstep, hstep, x, wmean, back = self.nrm, self.xstep, self.hstep, self.g["x"], self.wmean, self.back
        XS, HS, c = self.XS, self.HS, self.batch(b)
        nrm.wait(v, b)
        v.tensor_reduce(self.amax[:, :], nrm.xn[:, :, :], AX.X, ALU.max, apply_absolute_value=True).then_inc(xstep, 1)
        yield
        v.wait_ge(xstep, XS * b + 1)
        v.tensor_scalar(self.amax[:, :], self.amax[:, :], 1e-5, 1.0 / 127.0, ALU.max, ALU.mult).then_inc(xstep, 1)
        yield
        v.wait_ge(xstep, XS * b + 2)
        v.reciprocal(self.ascale[:, :], self.amax[:, :]).then_inc(xstep, 1)
        yield
        v.wait_ge(xstep, XS * b + 3)
        v.tensor_tensor(self.xr[:, :, :], nrm.xn[:, :, :], self.ascale[:, :].unsqueeze(2).to_broadcast([128, QT, D]),
                        ALU.mult).then_inc(xstep, 1)
        yield
        v.wait_ge(xstep, XS * b + 4)
        v.tensor_scalar(self.xr2[:, :, :], self.xr[:, :, :], 127.0, -128.0, ALU.min, ALU.max).then_inc(xstep, 1)
        yield
        v.wait_ge(xstep, XS * b + 5)
        v.tensor_scalar(self.xq[:, :, :], self.xr2[:, :, :], ROUND, -ROUND, ALU.add, ALU.add).then_inc(self.xq_done, 1)
        v.tensor_tensor(back[:, :, 0:2], self.amax[:, :].unsqueeze(2).to_broadcast([128, QT, 2]),
                        wmean[:, 0:2].unsqueeze(1).to_broadcast([128, QT, 2]), ALU.mult).then_inc(xstep, 1)
        yield
        v.wait_ge(xstep, XS * b + 6)
        yield
        nrm.take_moments(v, b + 1)
        yield
        h, hr, hmax = self.h, self.hr, self.hmax
        for t in range(QT):
            hs = HS * (QT * b + t)
            v.wait_ge(self.u_filled, QT * b + t + 1)
            v.wait_ge(self.gate_done, QT * b + t + 1)
            v.scalar_tensor_tensor(h[:, t, :], self.ups[:, :], back[:, t, 1:2], self.gate[:, t, :],
                                   ALU.mult, ALU.mult).then_inc(self.h_done, 1)
            yield
            v.wait_ge(self.h_done, QT * b + t + 2)
            v.tensor_reduce(hmax[:, t:t + 1], h[:, t, :], AX.X, ALU.max, apply_absolute_value=True)\
                .then_inc(hstep, 1)
            yield
            v.wait_ge(hstep, hs + 1)
            v.tensor_scalar(hmax[:, t:t + 1], hmax[:, t:t + 1], 1e-5, 1.0 / 127.0, ALU.max, ALU.mult)\
                .then_inc(hstep, 1)
            yield
            v.wait_ge(hstep, hs + 2)
            v.reciprocal(self.hscale[:, t:t + 1], hmax[:, t:t + 1]).then_inc(hstep, 1)
            v.tensor_tensor(back[:, t, 2:3], hmax[:, t:t + 1], wmean[:, 2:3], ALU.mult).then_inc(hstep, 1)
            yield
            v.wait_ge(hstep, hs + 4)
            v.tensor_scalar(hr[:, t, :], h[:, t, :], self.hscale[:, t:t + 1], 127.0, ALU.mult, ALU.min)\
                .then_inc(hstep, 1)
            yield
            v.wait_ge(hstep, hs + 5)
            v.tensor_scalar(hr[:, t, :], hr[:, t, :], -128.0, ROUND, ALU.max, ALU.add).then_inc(hstep, 1)
            yield
            v.wait_ge(hstep, hs + 6)
            v.tensor_scalar(self.hq[:, t, :], hr[:, t, :], -ROUND, None, ALU.add).then_inc(self.hq_done, 1)
            yield
        nrm.norm_rows(v, b + 1)
        yield
        v.wait_ge(self.y_filled, b + 1)
        for t in range(QT):
            v.scalar_tensor_tensor(x[:, QT * c + t, :], self.yps[:, t * 128:t * 128 + 128], back[:, t, 2:3],
                                   x[:, QT * c + t, :], ALU.mult, ALU.add).then_inc(self.y_done, 1)
        yield


def L1_ffn(nc, g, wts):
    LANES = 2
    F = L1_ffn_lane.F
    st = Stage(nc, "l1f")
    wf, loaded = wts.sb, wts.loaded
    wq = st.sb("wq", [128, 3, F], BF16)
    ones = st.sb("ones", [128, 128])
    wabs = st.sb("wabs", [128, 3])
    wmean = st.sb("wmean", [128, 3])
    wscale = st.sb("wscale", [128, 3])
    ones_set, wabs_done, wsum_done = st.sem("ones_set"), st.sem("wabs_done"), st.sem("wsum_done")
    wstep = st.sem("wstep")
    lanes = [L1_ffn_lane(st, n, LANES, g, wq, wmean) for n in range(LANES)]
    yps = lanes[0].yps

    with nc.Block("l1f_block") as block:
        @block.sync
        def _(sp):
            for ln in lanes:
                sp.sem_inc(ln.h_done, 1)
                sp.sem_inc(ln.hT_done, QT)
                sp.sem_inc(ln.y_done, QT)

        @block.gpsimd
        def _(pool):
            pool.memset(ones[:, :], 1.0).then_inc(ones_set, 1)
            for ln in lanes:
                ln.nrm.pool_setup(pool)
            for ln in lanes:
                ln.nrm.pool(pool, 0)
            with pool.Fori(0, B // LANES) as i:
                in_turn(*(ln.pool(pool, i) for ln in lanes))

        @block.tensor
        def _(pe):
            pe.wait_ge(ones_set, 1)
            pe.wait_ge(wabs_done, 1)
            pe.matmul(yps[:, 0:3], ones[:, :], wabs[:, :], start=True, stop=True).then_inc(wsum_done, 1)
            pe.wait_ge(wstep, 12)
            with pe.Fori(0, B // LANES) as i:
                in_turn(*(ln.tensor(pe, i) for ln in lanes))

        @block.scalar
        def _(act):
            with act.Fori(0, B // LANES) as i:
                in_turn(*(ln.scalar(act, i) for ln in lanes))

        @block.vector
        def _(v):
            v.wait_ge(loaded, 16)
            v.tensor_reduce(wabs[:, :], wf[:, :].rearrange("p (a f) -> p a f", a=3), AX.X, ALU.add, apply_absolute_value=True).then_inc(wabs_done, 1)
            v.wait_ge(wsum_done, 1)
            v.tensor_scalar(wmean[:, :], yps[:, 0:3], 1.0 / (F * D), 1e-5, ALU.mult, ALU.max).then_inc(wstep, 1)
            v.wait_ge(wstep, 1)
            v.reciprocal(wscale[:, :], wmean[:, :]).then_inc(wstep, 2)
            v.wait_ge(wstep, 3)
            for n in range(3):
                v.tensor_scalar(wf[:, n * F:(n + 1) * F], wf[:, n * F:(n + 1) * F], wscale[:, n:n + 1], ROUND, ALU.mult, ALU.add).then_inc(wstep, 1)
                v.wait_ge(wstep, 3 * n + 4)
                v.tensor_scalar(wf[:, n * F:(n + 1) * F], wf[:, n * F:(n + 1) * F], -ROUND, 1.0, ALU.add, ALU.min).then_inc(wstep, 1)
                v.wait_ge(wstep, 3 * n + 5)
                v.tensor_scalar(wq[:, n, :], wf[:, n * F:(n + 1) * F], -1.0, None, ALU.max).then_inc(wstep, 1)
            for ln in lanes:
                ln.nrm.take_moments(v, 0)
            for ln in lanes:
                ln.nrm.norm_rows(v, 0)
            with v.Fori(0, B // LANES) as i:
                in_turn(*(ln.vector(v, i) for ln in lanes))
    st.close()


def L1_attn(nc, g, wts):
    x, ident = g["x"], g["ident"]
    NS = 16
    HB = B // 2
    LANES = 4
    AHEAD = 2
    NB = 4
    YB = NT * D // 512
    st = Stage(nc, "l1a")
    w, loaded = wts.of, wts.loaded
    u = st.sb("u", [128, B, S])
    dt = st.sb("dt", [128, B, S])
    A = st.sb("A", [128, NS])
    BA = st.sb("BA", [128, NS])
    CBA = st.sb("CBA", [128, NS])
    cols = st.sb("cols", [128, NS, 3])
    cur = [st.sb(f"cur{i}", [128, 3]) for i in range(NB)]
    diag = [st.sb(f"diag{i}", [128, 128]) for i in range(NB)]
    diag_D = st.sb("diag_D", [128, 128])
    decay = [st.sb(f"decay{i}", [128, HB, S]) for i in range(NB)]
    th = [st.sb(f"th{i}", [128, HB, S]) for i in range(NB)]
    state = [st.sb(f"state{i}", [128, HB, S]) for i in range(2)]
    lanes = [Lane(st, n, LANES) for n in range(LANES)]
    norms = [Norm(ln, x) for ln in lanes]
    turn_ps = [ln.ps("ps") for ln in lanes]
    t_filled = [ln.sem("t_filled") for ln in lanes]
    u_done = [ln.sem("u_done") for ln in lanes]
    d_filled = [ln.sem("d_filled") for ln in lanes]
    d_left = [ln.sem("d_left") for ln in lanes]
    yps = [st.ps(f"y{i}") for i in range(YB)]
    aset, dt_exp, dt_done = st.sem("aset"), st.sem("dt_exp"), st.sem("dt_done")
    decay_done, th_done, coef_done = st.sem("decay_done"), st.sem("th_done"), st.sem("coef_done")
    drive_done, reset_done, state_done = st.sem("drive_done"), st.sem("reset_done"), st.sem("state_done")
    summed, cols_done, cur_done, diag_done = st.sem("summed"), st.sem("cols_done"), st.sem("cur_done"), st.sem("diag_done")
    direct, added = st.sem("direct"), st.sem("added")

    def y_of(batch, t):
        n = QT * batch + t
        return yps[n // 4][:, n % 4 * 128:n % 4 * 128 + 128]

    def all_units(eng, unit):
        with eng.Fori(0, NS // NB) as m:
            for s in range(NB):
                for hf in range(2):
                    unit(NB * m + s, s, hf)

    with nc.Block("l1a_block") as block:
        @block.sync
        def _(sp):
            sp.sem_inc(state_done, NB)
            sp.sem_inc(summed, 2)
            for ln in range(LANES):
                sp.sem_inc(d_left[ln], 1)

        @block.gpsimd
        def _(pool):
            for nrm in norms:
                nrm.pool_setup(pool)
            with pool.Fori(0, B // LANES) as b:
                for nrm in norms:
                    nrm.pool(pool, b)
            for ln in range(LANES):
                pool.wait_ge(u_done[ln], B // LANES)

            def unit(n, s, hf):
                i = 2 * n + hf
                buf = th[(2 * s + hf) % NB]
                pool.wait_ge(coef_done, i + 1)
                pool.tensor_tensor(buf[:, :, :], buf[:, :, :], u[:, HB * hf:HB * hf + HB, :], ALU.mult)\
                    .then_inc(drive_done, 1)

            all_units(pool, unit)

        @block.tensor
        def _(pe):
            pe.wait_ge(loaded, 16)
            with pe.Fori(0, B // LANES) as b:
                for ln in range(LANES):
                    norms[ln].wait(pe, b)
                    pe.wait_ge(d_left[ln], b + 1)
                    for t in range(QT):
                        mm = pe.transpose(turn_ps[ln][:, t * 128:t * 128 + 128], norms[ln].xn[:, t, :], ident[:, :])
                    mm.then_inc(t_filled[ln], 1)
                for ln in range(LANES):
                    pe.wait_ge(u_done[ln], b + 1)
                    pe.matmul(turn_ps[ln][:, S:2 * S], w("dt"), u[:, lanes[ln].batch(b), :], start=True, stop=True)\
                        .then_inc(d_filled[ln], 1)
            pe.wait_ge(cols_done, 3)
            for batch in range(B):
                for t in range(QT):
                    mm = pe.matmul(y_of(batch, t), u[:, batch, t * 128:t * 128 + 128], diag_D[:, :],
                                   start=(QT * batch + t) % 4 == 0, stop=False, skip_group_check=True)

            def unit(n, s, hf):
                i = 2 * n + hf
                pe.wait_ge(state_done, i + 1 + NB)
                pe.wait_ge(diag_done, n + 1)
                for bb in range(HB):
                    for t in range(QT):
                        mm = pe.matmul(y_of(HB * hf + bb, t), state[hf][:, bb, t * 128:t * 128 + 128], diag[s][:, :],
                                       start=False, stop=True, skip_group_check=True)
                mm.then_inc(summed, 1)

            all_units(pe, unit)

        @block.scalar
        def _(act):
            act.wait_ge(aset, 1)
            act.activation(A[:, :], A[:, :], ACT.Exp).then_inc(aset, 1)
            for ln in range(LANES):
                act.wait_ge(d_left[ln], B // LANES + 1)
            act.activation(dt[:, :, :], dt[:, :, :], ACT.Exp).then_inc(dt_exp, 1)
            act.wait_ge(dt_done, 1)

            def unit(n, s, hf):
                i = 2 * n + hf
                rows = dt[:, HB * hf:HB * hf + HB, :]
                act.wait_ge(cur_done, n + 1)
                act.wait_ge(state_done, i + 1)
                k = (2 * s + hf) % NB
                act.activation(decay[k][:, :, :], rows, ACT.Exp, scale=cur[s][:, 0:1]).then_inc(decay_done, 1)
                act.activation(th[k][:, :, :], rows, ACT.Tanh, scale=cur[s][:, 1:2]).then_inc(th_done, 1)

            all_units(act, unit)

        @block.vector
        def _(v):
            v.wait_ge(loaded, 16)
            v.tensor_scalar(A[:, :], w("A"), 88.5, None, ALU.min).then_inc(aset, 1)
            v.wait_ge(aset, 2)
            v.tensor_scalar(A[:, :], A[:, :], -1.0, None, ALU.mult).then_inc(aset, 1)
            v.wait_ge(aset, 3)
            v.reciprocal(BA[:, :], A[:, :]).then_inc(aset, 1)
            v.wait_ge(aset, 4)
            v.tensor_tensor(BA[:, :], BA[:, :], w("B"), ALU.mult).then_inc(aset, 1)
            v.wait_ge(aset, 5)
            v.tensor_tensor(CBA[:, :], BA[:, :], w("C"), ALU.mult).then_inc(aset, 1)
            v.tensor_copy(cols[:, :, 0], A[:, :]).then_inc(cols_done, 1)
            v.tensor_scalar(cols[:, :, 1], A[:, :], 0.5, None, ALU.mult)
            v.tensor_scalar(diag_D[:, :], ident[:, :], w("D"), None, ALU.mult).then_inc(cols_done, 1)
            v.wait_ge(aset, 6)
            v.tensor_copy(cols[:, :, 2], CBA[:, :]).then_inc(cols_done, 1)
            v.wait_ge(cols_done, 3)
            for n in range(NB - 1):
                v.tensor_copy(cur[n][:, :], cols[:, n, :]).then_inc(cur_done, 1)
            v.wait_ge(cur_done, NB - 1)
            for n in range(NB - 1):
                v.tensor_scalar(diag[n][:, :], ident[:, :], cur[n][:, 2:3], None, ALU.mult).then_inc(diag_done, 1)
            with v.Fori(0, B // LANES) as b:
                for nrm in norms:
                    nrm.take_moments(v, b)
                for nrm in norms:
                    nrm.norm_rows(v, b)
                for ln in range(LANES):
                    v.wait_ge(t_filled[ln], b + 1)
                    v.tensor_scalar(u[:, lanes[ln].batch(b), :], turn_ps[ln][:, 0:S], 1.0, None, ALU.mult)\
                        .then_inc(u_done[ln], 1)
                for ln in range(LANES):
                    v.wait_ge(d_filled[ln], b + 1)
                    v.tensor_scalar(dt[:, lanes[ln].batch(b), :], turn_ps[ln][:, S:2 * S], w("bdt"), 0.0, ALU.add, ALU.min)\
                        .then_inc(d_left[ln], 1)
            v.wait_ge(dt_exp, 1)
            v.tensor_scalar(dt[:, :, :], dt[:, :, :], 0.001, 0.02, ALU.max, ALU.min).then_inc(dt_done, 1)

            def coefficient(i, k):
                v.wait_ge(decay_done, i + 1)
                v.wait_ge(th_done, i + 1)
                v.scalar_tensor_tensor(th[k][:, :, :], decay[k][:, :, :], 1.0, th[k][:, :, :],
                                       ALU.add, ALU.mult).then_inc(coef_done, 1)

            def reset(i, k):
                v.wait_ge(coef_done, i + 1)
                v.memset(decay[k][:, :, 0:1], 0.0).then_inc(reset_done, 1)

            def four_states(m, last):
                for s in range(NB):
                    n = NB * m + s
                    for hf in range(2):
                        i, k = 2 * n + hf, (2 * s + hf) % NB
                        more = not last or 2 * s + hf + AHEAD < 2 * NB
                        if more:
                            coefficient(i + AHEAD, (k + AHEAD) % NB)
                        v.wait_ge(summed, i + 1)
                        v.wait_ge(drive_done, i + 1)
                        v.wait_ge(reset_done, i + 1)
                        v.tensor_tensor_scan(state[hf][:, :, :].rearrange("p b s -> p (b s)"),
                                             decay[k][:, :, :].rearrange("p b s -> p (b s)"),
                                             th[k][:, :, :].rearrange("p b s -> p (b s)"), 0.0, ALU.mult, ALU.add)\
                            .then_inc(state_done, 1)
                        if more:
                            reset(i + AHEAD, (k + AHEAD) % NB)
                        if not last or s + NB - 1 < NB:
                            c = (s + NB - 1) % NB
                            if hf == 0:
                                v.tensor_scalar(cur[c][:, :], cols[:, n + NB - 1, :], 1.0, None, ALU.mult)\
                                    .then_inc(cur_done, 1)
                            else:
                                v.wait_ge(cur_done, n + NB)
                                v.wait_ge(summed, 2 * n + 2)
                                v.tensor_scalar(diag[c][:, :], ident[:, :], cur[c][:, 2:3], None, ALU.mult)\
                                    .then_inc(diag_done, 1)

            for i in range(AHEAD):
                coefficient(i, i)
                reset(i, i)
            with v.Fori(0, NS // NB - 1) as m:
                four_states(m, False)
            four_states(NS // NB - 1, True)
            v.wait_ge(summed, 2 * NS + 2)
            for n in range(YB):
                v.tensor_tensor(x[:, 4 * n:4 * n + 4, :], x[:, 4 * n:4 * n + 4, :],
                                yps[n][:, :].rearrange("p (t f) -> p t f", t=4), ALU.add).then_inc(added, 1)
    st.close()




class L2_ffn_lane:
    C, HI = S // 2, 4
    NI = H // HI
    SR = 2
    XT, GATE, PICK, QK, V, SELT, ITEM = 0, 1, 2, 3, 4, 5, 6
    AV, PROJ, BACK = ITEM + NI, ITEM + NI + 1, ITEM + NI + 2
    GS = 5

    def __init__(self, st, lane, lanes, g, w):
        self.g, self.w = g, w
        C, NI, HI = self.C, self.NI, self.HI
        st = Lane(st, lane, lanes)
        self.batch = st.batch
        self.T = Ring(st, "t", 2, self.BACK + 1)
        self.scores = [st.ps(f"s{i}") for i in range(self.SR)]
        self.nrm = Norm(st, g["x"])
        self.xnT = st.sb("xnT", [128, S])
        self.gates = st.sb("gates", [128, S])
        self.junk = st.sb("junk", [128, 3 * QT, S])
        self.own = st.sb("own", [128, QT])
        self.above = st.sb("above", [128, QT])
        self.equal = st.sb("equal", [128, QT])
        self.rank = st.sb("rank", [128, QT])
        self.sel = st.sb("sel", [128, QT, C])
        self.selT = st.sb("selT", [C, S])
        self.picked = st.sb("picked", [128, C])
        self.q_sb = st.sb("q", [128, C])
        self.k_sb = st.sb("k", [128, C])
        self.kbd = st.sb("kbd", [128, H, C])
        self.v_sb = st.sb("v", [C, H, 32])
        self.P = st.sb("p", [128, NI, HI, C])
        self.PT = st.sb("pt", [C, NI, HI, C])
        self.OT = st.sb("ot", [128, NI, C])
        self.o_sb = st.sb("o_sb", [C, D])
        self.top = st.sb("top", [128, NI, HI])
        self.sums = st.sb("sums", [128, NI, HI])
        self.rec = st.sb("rec", [128, NI, HI])
        self.v_set, self.gstep, self.sel_done = st.sem("v_set"), st.sem("gstep"), st.sem("sel_done")
        self.kbd_done, self.s_filled, self.top_done = st.sem("kbd_done"), st.sem("s_filled"), st.sem("top_done")
        self.sub_done, self.exp_done, self.sum_done = st.sem("sub_done"), st.sem("exp_done"), st.sem("sum_done")
        self.rec_done, self.p_done = st.sem("rec_done"), st.sem("p_done")

    def pool(self, pool, b):
        T, C, HI, NI = self.T, self.C, self.HI, self.NI
        for _ in range(4):
            yield
        T.wait_emptied(pool, b, self.QK)
        for h in range(0, H, 4):
            pool.tensor_tensor(self.kbd[:, h:h + 4, :], self.k_sb[:, :].unsqueeze(1).to_broadcast([128, 4, C]),
                               self.w("kmask")[:, h:h + 4].unsqueeze(2).to_broadcast([128, 4, C]),
                               ALU.mult).then_inc(self.kbd_done, 1)
        yield
        for s in range(NI + 3):
            i = s - 2
            if 0 <= i < NI:
                pool.wait_ge(self.rec_done, b * NI + i + 1)
                pool.tensor_tensor(self.P[:, i, :, :], self.P[:, i, :, :],
                                   self.rec[:, i, :].unsqueeze(2).to_broadcast([128, HI, C]),
                                   ALU.mult).then_inc(self.p_done, 1)
            if s == NI + 1:
                self.nrm.pool(pool, b + 1)
            yield

    def tensor(self, pe, b):
        T, C, HI, NI, w, ident, sel = self.T, self.C, self.HI, self.NI, self.w, self.g["ident"], self.sel
        XT, GATE, PICK, QK, V, SELT, ITEM = self.XT, self.GATE, self.PICK, self.QK, self.V, self.SELT, self.ITEM
        self.nrm.wait(pe, b)
        T.wait_free(pe, b, XT)
        for t in range(QT):
            mm = pe.transpose(T.bank(XT)[:, t * 128:t * 128 + 128], self.nrm.xn[:, t, :], ident[:, :])
        mm.then_inc(T.full(XT), 1)
        yield
        T.wait_emptied(pe, b, XT)
        T.wait_free(pe, b, GATE)
        pe.matmul(T.bank(GATE)[:, 0:S], w("gate"), self.xnT[:, :], start=True, stop=True).then_inc(T.full(GATE), 1)
        yield
        yield
        pe.wait_ge(self.sel_done, QT * b + QT)
        for t in range(QT):
            mm = pe.matmul(T.bank(PICK)[:, 0:C], self.nrm.xn[:, t, :], sel[:, t, :], start=(t == 0),
                           stop=(t == QT - 1))
        mm.then_inc(T.full(PICK), 1)
        yield
        T.wait_emptied(pe, b, PICK)
        T.wait_free(pe, b, QK)
        for n, key in enumerate("qk"):
            mm = pe.matmul(T.bank(QK)[:, n * C:(n + 1) * C], w(key), self.picked[:, :], start=True, stop=True)
        mm.then_inc(T.full(QK), 1)
        pe.matmul(T.bank(V)[:, 0:D], self.picked[:, :], w("v"), start=True, stop=True).then_inc(T.full(V), 1)
        T.wait_free(pe, b, SELT)
        for t in range(QT):
            mm = pe.transpose(T.bank(SELT)[:, t * 128:t * 128 + 128], sel[:, t, :], ident[:, :])
        mm.then_inc(T.full(SELT), 1)
        yield
        for s in range(NI + 3):
            if s < NI:
                pe.wait_ge(self.kbd_done, b * NI + s + 1)
                pe.wait_ge(self.sub_done, b * NI + s + 1)
                pe.matmul(self.scores[s % self.SR][:, :], self.q_sb[:, :], self.kbd[:, s * HI:s * HI + HI, :],
                          start=True, stop=True).then_inc(self.s_filled, 1)
            i = s - 3
            if i >= 0:
                pe.wait_ge(self.p_done, b * NI + i + 1)
                T.wait_free(pe, b, ITEM + i)
                for m in range(HI):
                    mm = pe.transpose(T.bank(ITEM + i)[:, m * C:m * C + C], self.P[:, i, m, :], ident[:, :])
                mm.then_inc(T.full(ITEM + i), 1)
            yield
        T.wait_emptied(pe, b, self.AV - 2)
        T.wait_emptied(pe, b, self.AV - 1)
        for i in range(NI):
            for m in range(HI):
                mm = pe.matmul(T.bank(self.AV)[32 * m:32 * m + 32, i * C:i * C + C], self.v_sb[:, i * HI + m, :],
                               self.PT[:, i, m, :], start=True, stop=True, tile_position=(0, 32 * m))
        mm.then_inc(T.full(self.AV), 1)
        yield
        T.wait_emptied(pe, b, self.AV)
        for i in range(NI):
            mm = pe.matmul(T.bank(self.PROJ)[:, 0:D], self.OT[:, i, :], w("o")[:, i * D:i * D + D], start=(i == 0),
                           stop=(i == NI - 1))
        mm.then_inc(T.full(self.PROJ), 1)
        yield
        T.wait_emptied(pe, b, self.PROJ)
        for t in range(QT):
            mm = pe.matmul(T.bank(self.BACK)[:, t * D:t * D + D], self.selT[:, t * 128:t * 128 + 128], self.o_sb[:, :],
                           start=True, stop=True)
        mm.then_inc(T.full(self.BACK), 1)
        yield

    def scalar(self, act, b):
        T, C, HI, NI = self.T, self.C, self.HI, self.NI
        XT, GATE, PICK, QK, SELT, ITEM = self.XT, self.GATE, self.PICK, self.QK, self.SELT, self.ITEM
        T.wait_filled(act, b, XT)
        act.activation(self.xnT[:, :], T.bank(XT)[:, 0:S], ACT.Copy).then_inc(T.free(XT), 1)
        yield
        T.wait_filled(act, b, GATE)
        act.activation(self.gates[:, :], T.bank(GATE)[:, 0:S], ACT.Exp, scale=-1.0).then_inc(T.free(GATE), 1)
        yield
        yield
        T.wait_filled(act, b, PICK)
        act.activation(self.picked[:, :], T.bank(PICK)[:, 0:C], ACT.Copy).then_inc(T.free(PICK), 1)
        yield
        T.wait_filled(act, b, QK)
        act.activation(self.q_sb[:, :], T.bank(QK)[:, 0:C], ACT.Copy, scale=(D // H) ** -0.5)
        act.activation(self.k_sb[:, :], T.bank(QK)[:, C:2 * C], ACT.Copy).then_inc(T.free(QK), 1)
        T.wait_filled(act, b, SELT)
        act.activation(self.selT[:, :], T.bank(SELT)[:, 0:S], ACT.Copy).then_inc(T.free(SELT), 1)
        yield
        for s in range(NI + 3):
            i = s - 3
            if i >= 0:
                T.wait_filled(act, b, ITEM + i)
                act.activation(self.PT[:, i, :, :], T.bank(ITEM + i)[:, :].rearrange("p (m q) -> p m q", m=HI), ACT.Copy)\
                    .then_inc(T.free(ITEM + i), 1)
            i = s - 1
            if 0 <= i < NI:
                act.wait_ge(self.sub_done, b * NI + i + 1 + self.SR)
                act.activation(self.P[:, i, :, :], self.P[:, i, :, :], ACT.Exp).then_inc(self.exp_done, 1)
            yield
        T.wait_filled(act, b, self.AV)
        act.activation(self.OT[:, :, :], T.bank(self.AV)[:, :].rearrange("p (i q) -> p i q", i=NI), ACT.Copy)\
            .then_inc(T.free(self.AV), 1)
        yield
        T.wait_filled(act, b, self.PROJ)
        act.activation(self.o_sb[:, :], T.bank(self.PROJ)[:, 0:D], ACT.Copy).then_inc(T.free(self.PROJ), 1)
        yield
        yield

    def vector(self, v, b):
        T, C, HI, NI, GS, w, ident = self.T, self.C, self.HI, self.NI, self.GS, self.w, self.g["ident"]
        gates, gstep, own, junk = self.gates, self.gstep, self.own, self.junk
        x, c, d = self.g["x"], self.batch(b), D // H
        yield
        yield
        T.wait_emptied(v, b, self.GATE)
        v.tensor_scalar(gates[:, :], gates[:, :], 1.0, None, ALU.add).then_inc(gstep, 1)
        v.wait_ge(gstep, GS * b + 1)
        v.reciprocal(gates[:, :], gates[:, :]).then_inc(gstep, 1)
        v.wait_ge(gstep, GS * b + 2)
        for t in range(QT):
            o = v.scalar_tensor_tensor(junk[:, t, 0:128], gates[:, t * 128:t * 128 + 128], 1.0, ident[:, :],
                                       ALU.mult, ALU.mult, accum_out=own[:, t:t + 1])
        o.then_inc(gstep, 1)
        v.wait_ge(gstep, GS * b + 3)
        for t in range(QT):
            v.tensor_scalar(junk[:, QT + t, :], gates[:, :], own[:, t:t + 1], 0.0, ALU.is_gt, ALU.add,
                            accum_out=self.above[:, t:t + 1])
            e = v.scalar_tensor_tensor(junk[:, 2 * QT + t, :], gates[:, :], own[:, t:t + 1],
                                       w("before")[:, t * S:t * S + S], ALU.is_equal, ALU.mult,
                                       accum_out=self.equal[:, t:t + 1])
        e.then_inc(gstep, 1)
        v.wait_ge(gstep, GS * b + 4)
        v.tensor_tensor(self.rank[:, :], self.above[:, :], self.equal[:, :], ALU.add).then_inc(gstep, 1)
        v.wait_ge(gstep, GS * b + 5)
        for t in range(QT):
            v.tensor_scalar(self.sel[:, t, :], w("iota"), self.rank[:, t:t + 1], None, ALU.is_equal)\
                .then_inc(self.sel_done, 1)
        yield
        yield
        T.wait_filled(v, b, self.V)
        v.tensor_copy(self.v_sb[:, :, 0:d], T.bank(self.V)[:, 0:D].rearrange("p (h d) -> p h d", d=d))\
            .then_inc(T.free(self.V), 1)
        yield
        for s in range(NI + 3):
            i = s
            if i < NI:
                v.wait_ge(self.s_filled, b * NI + i + 1)
                v.tensor_reduce(self.top[:, i, :], self.scores[i % self.SR][:, :].rearrange("p (h k) -> p h k", h=HI),
                                AX.X, ALU.max).then_inc(self.top_done, 1)
            i = s - 1
            if 0 <= i < NI:
                v.wait_ge(self.top_done, b * NI + i + 1)
                v.tensor_tensor(self.P[:, i, :, :], self.scores[i % self.SR][:, :].rearrange("p (h k) -> p h k", h=HI),
                                self.top[:, i, :].unsqueeze(2).to_broadcast([128, HI, C]),
                                ALU.subtract).then_inc(self.sub_done, 1)
            i = s - 2
            if 0 <= i < NI:
                v.wait_ge(self.exp_done, b * NI + i + 1)
                v.tensor_reduce(self.sums[:, i, :], self.P[:, i, :, :], AX.X, ALU.add).then_inc(self.sum_done, 1)
                v.wait_ge(self.sum_done, b * NI + i + 1)
                v.reciprocal(self.rec[:, i, :], self.sums[:, i, :]).then_inc(self.rec_done, 1)
            if s == NI + 1:
                self.nrm.take_moments(v, b + 1)
            if s == NI + 2:
                self.nrm.norm_rows(v, b + 1)
            yield
        yield
        yield
        T.wait_filled(v, b, self.BACK)
        for t in range(QT):
            f = v.scalar_tensor_tensor(x[:, QT * c + t, :], T.bank(self.BACK)[:, t * D:t * D + D], own[:, t:t + 1],
                                       x[:, QT * c + t, :], ALU.mult, ALU.add)
        f.then_inc(T.free(self.BACK), 1)
        yield


def L2_ffn(nc, g, wts):
    LANES = 2
    st = Stage(nc, "l2f")
    w, loaded = wts.of, wts.loaded

    lanes = [L2_ffn_lane(st, n, LANES, g, w) for n in range(LANES)]

    with nc.Block("l2f_block") as block:
        @block.sync
        def _(sp):
            for ln in lanes:
                ln.T.credit(sp)
                sp.sem_inc(ln.sub_done, ln.SR)

        @block.gpsimd
        def _(pool):
            for ln in lanes:
                ln.nrm.pool_setup(pool)
                pool.memset(ln.v_sb[:, :, :], 0.0).then_inc(ln.v_set, 1)
            for ln in lanes:
                ln.nrm.pool(pool, 0)
            pool.wait_ge(loaded, 16)
            with pool.Fori(0, B // LANES) as i:
                in_turn(*(ln.pool(pool, i) for ln in lanes))

        @block.tensor
        def _(pe):
            pe.wait_ge(loaded, 16)
            with pe.Fori(0, B // LANES) as i:
                in_turn(*(ln.tensor(pe, i) for ln in lanes))

        @block.scalar
        def _(act):
            with act.Fori(0, B // LANES) as i:
                in_turn(*(ln.scalar(act, i) for ln in lanes))

        @block.vector
        def _(v):
            v.wait_ge(loaded, 16)
            for ln in lanes:
                v.wait_ge(ln.v_set, 1)
                ln.nrm.take_moments(v, 0)
            for ln in lanes:
                ln.nrm.norm_rows(v, 0)
            with v.Fori(0, B // LANES) as i:
                in_turn(*(ln.vector(v, i) for ln in lanes))
    st.close()


class L3_xattn_lane:
    d, NP, INNER = 64, H // 2, 1024
    NI = NP * QT
    K = SC + S
    LAG, PR = 2, 3
    XT, Q0 = 0, 1
    K0 = Q0 + 4
    V0 = K0 + NP
    VC0 = V0 + 2 * QT
    I0 = VC0 + 2
    OUT = I0 + 4 * NP

    def __init__(self, st, lane, lanes, g, w, cnT):
        self.g, self.w, self.cnT = g, w, cnT
        NP, K = self.NP, self.K
        st = Lane(st, lane, lanes)
        self.batch = st.batch
        self.T = Ring(st, "t", 2, self.OUT + 1)
        self.scores = st.ps("s", (128, 1024))
        self.nrm = Norm(st, g["x"])
        self.nrm2 = Norm(st, g["x"], of=self.nrm)
        self.xnT = st.sb("xnT", [128, S])
        self.ctx2 = st.sb("ctx2", [128, 2, SC])
        self.q_sb = st.sb("q", [128, NP, S])
        self.kbd = st.sb("kbd", [128, H, K])
        self.v_sb = st.sb("v", [128, QT, H, self.d])
        self.vc = st.sb("vc", [128, NP, 128])
        self.P = [st.sb(f"p{i}", [128, 2, K]) for i in range(self.PR)]
        self.Pc = [st.sb(f"pc{i}", [128, 2, SC]) for i in range(self.PR)]
        self.PT = [st.sb(f"pt{i}", [128, 2, QT, S]) for i in range(2)]
        self.PTc = [st.sb(f"ptc{i}", [128, S]) for i in range(2)]
        self.OT = st.sb("ot", [128, NP, S])
        self.nmax = st.sb("nmax", [128, self.PR, 2])
        self.sums = st.sb("sums", [128, self.PR, 2])
        self.rec = st.sb("rec", [128, self.PR, 2])
        self.ctx2_done, self.vc_half, self.v_set = st.sem("ctx2_done"), st.sem("vc_half"), st.sem("v_set")
        self.s_filled, self.max_done, self.exp_done = st.sem("s_filled"), st.sem("max_done"), st.sem("exp_done")
        self.rec_done, self.p_done, self.added = st.sem("rec_done"), st.sem("p_done"), st.sem("added")

    def keys_of(self, qt):
        return SC + 128 * (qt + 1)

    def use_of(self, u, n):
        return self.I0 + 4 * u + n

    def sync_setup(self, sp):
        self.T.credit(sp)
        sp.sem_inc(self.exp_done, 1)

    def pool_setup(self, pool):
        self.nrm.pool_setup(pool)
        self.nrm2.pool_setup(pool)
        pool.memset(self.vc[:, :, :], 0.0).then_inc(self.v_set, 1)

    def pool(self, pool, b):
        for _ in range(self.I0):
            yield
        for s in range(self.NI + self.LAG + 1):
            i = s - 1
            if 0 <= i < self.NI:
                n, m = self.keys_of(i % QT), i % self.PR
                P, by = self.P[m], self.rec[:, m, :].unsqueeze(2)
                pool.wait_ge(self.rec_done, b * self.NI + i + 1)
                pool.tensor_tensor(self.Pc[m][:, :, :], P[:, :, 0:SC], by.to_broadcast([128, 2, SC]), ALU.mult)
                pool.tensor_tensor(P[:, :, SC:n], P[:, :, SC:n], by.to_broadcast([128, 2, n - SC]),
                                   ALU.mult).then_inc(self.p_done, 1)
            if s == self.NI - 1:
                self.nrm.pool(pool, b + 1)
            if s == self.NI + 1:
                self.nrm2.pool(pool, b + 1)
            yield

    def tensor(self, pe, b):
        T, w, g, xnT, NI, NP, LAG, K = self.T, self.w, self.g, self.xnT, self.NI, self.NP, self.LAG, self.K
        ident, c0 = g["ident"], self.batch(b)
        self.nrm2.wait(pe, b)
        T.wait_free(pe, b, self.XT)
        for t in range(QT):
            mm = pe.transpose(T.bank(self.XT)[:, t * 128:t * 128 + 128], self.nrm2.xn[:, t, :], ident[:, :])
        mm.then_inc(T.full(self.XT), 1)
        yield
        T.wait_emptied(pe, b, self.XT)
        for n in range(4):
            k = self.Q0 + n
            T.wait_free(pe, b, k)
            for j in range(2):
                c = 2 * n + j
                mm = pe.matmul(T.bank(k)[:, j * S:(j + 1) * S], w("q")[:, c * 128:c * 128 + 128],
                               xnT[:, :], start=True, stop=True)
            mm.then_inc(T.full(k), 1)
            yield
        for c in range(NP):
            k = self.K0 + c
            T.wait_free(pe, b, k)
            wk = w("k")[:, c * 128:c * 128 + 128]
            pe.matmul(T.bank(k)[:, 0:SC], wk, self.cnT[:, c0, :], start=True, stop=True)
            pe.matmul(T.bank(k)[:, SC:K], wk, xnT[:, :], start=True, stop=True).then_inc(T.full(k), 1)
            yield
        for n in range(2 * QT):
            t, hf = divmod(n, 2)
            k = self.V0 + n
            T.wait_free(pe, b, k)
            pe.matmul(T.bank(k)[:, :], xnT[:, t * 128:t * 128 + 128], w("v")[:, hf * 512:hf * 512 + 512],
                      start=True, stop=True).then_inc(T.full(k), 1)
            yield
        pe.wait_ge(self.ctx2_done, b + 1)
        for hf in range(2):
            k = self.VC0 + hf
            T.wait_free(pe, b, k)
            pe.matmul(T.bank(k)[:, :], self.ctx2[:, :, :], w("v")[:, hf * 512:hf * 512 + 512],
                      start=True, stop=True).then_inc(T.full(k), 1)
            yield
        T.wait_emptied(pe, b, self.VC0 - 2)
        T.wait_emptied(pe, b, self.VC0 - 1)
        for i in range(NI + LAG + 1):
            if i < NI:
                u, qt = divmod(i, QT)
                n = self.keys_of(qt)
                pe.wait_ge(self.exp_done, b * NI + i + 1)
                for j in range(2):
                    so = self.scores[:, j * 512:j * 512 + n]
                    pe.matmul(so, self.q_sb[:, u, qt * 128:qt * 128 + 128], self.kbd[:, 2 * u + j, 0:n],
                              start=True, stop=False)
                    pe.matmul(so[:, n - 128:n], g["identb"][:, :], g["tri"][:, :], start=False, stop=False)
                    mm = pe.matmul(so[:, 0:SC], g["onesb"][:, :], g["hide"][:, c0, :], start=False, stop=True)
                mm.then_inc(self.s_filled, 1)
            j = i - LAG - 1
            if j >= 0 and j % QT == QT - 1:
                self.products(pe, b, j // QT)
            j = i - LAG
            if 0 <= j < NI:
                u, qt = divmod(j, QT)
                nb = qt + 1
                k = self.use_of(u, qt)
                pe.wait_ge(self.p_done, b * NI + j + 1)
                T.wait_free(pe, b, k)
                for hh in range(2):
                    for kt in range(nb):
                        at = (hh * nb + kt) * 128
                        mm = pe.transpose(T.bank(k)[:, at:at + 128],
                                          self.P[j % self.PR][:, hh, SC + kt * 128:SC + kt * 128 + 128], ident[:, :])
                if qt == 1:
                    mm.then_inc(T.full(k), 1)
                    k += 1
                    T.wait_free(pe, b, k)
                at = 256 if qt == 0 else 0
                pe.transpose(T.bank(k)[:, at:at + 128], self.Pc[j % self.PR][:, :, :].rearrange("p j k -> p (j k)"),
                             ident[:, :]).then_inc(T.full(k), 1)
            yield
        k = self.OUT
        T.wait_emptied(pe, b, k - 1)
        T.wait_free(pe, b, k)
        for t in range(QT):
            for u in range(NP):
                mm = pe.matmul(T.bank(k)[:, t * 128:t * 128 + 128], self.OT[:, u, t * 128:t * 128 + 128],
                               w("o")[:, u * 128:u * 128 + 128], start=(u == 0), stop=(u == NP - 1))
        mm.then_inc(T.full(k), 1)
        yield

    def products(self, pe, b, u):
        T, k = self.T, self.use_of(u, 3)
        T.wait_emptied(pe, b, k - 2)
        T.wait_emptied(pe, b, k - 1)
        T.wait_free(pe, b, k)
        o = T.bank(k)
        pe.matmul(o[:, 0:S], self.vc[:, u, :], self.PTc[u % 2][:, :], start=True, stop=False, skip_group_check=True)
        for hh in range(2):
            for kt in range(QT):
                mm = pe.matmul(o[64 * hh:64 * hh + 64, 128 * kt:S], self.v_sb[:, kt, 2 * u + hh, :],
                               self.PT[u % 2][:, hh, kt, 128 * kt:S], start=False, stop=(kt == QT - 1),
                               tile_position=(0, 64 * hh), skip_group_check=True)
        mm.then_inc(T.full(k), 1)

    def scalar(self, act, b):
        T, w, NI, LAG, K = self.T, self.w, self.NI, self.LAG, self.K
        T.wait_filled(act, b, self.XT)
        act.activation(self.xnT[:, :], T.bank(self.XT)[:, 0:S], ACT.Identity, scale=w("g1"), bias=w("b1"))\
            .then_inc(T.free(self.XT), 1)
        yield
        for n in range(4):
            k = self.Q0 + n
            T.wait_filled(act, b, k)
            act.activation(self.q_sb[:, 2 * n:2 * n + 2, :], T.bank(k)[:, :].rearrange("p (c q) -> p c q", c=2),
                           ACT.Copy, scale=self.d ** -0.5).then_inc(T.free(k), 1)
            yield
        for c in range(self.NP):
            if c % 2:
                T.wait_filled(act, b, self.K0 + c)
                for j in range(2):
                    kk = act.activation(self.kbd[:, 2 * c + j, :], T.bank(self.K0 + c)[:, 0:K], ACT.Copy,
                                        scale=w("kmask")[:, j:j + 1])
                kk.then_inc(T.free(self.K0 + c), 1)
            yield
        for n in range(2 * QT):
            t, hf = divmod(n, 2)
            k = self.V0 + n
            T.wait_filled(act, b, k)
            act.activation(self.v_sb[:, t, 8 * hf:8 * hf + 8, :],
                           T.bank(k)[:, :].rearrange("p (h d) -> p h d", d=self.d), ACT.Copy).then_inc(T.free(k), 1)
            yield
        yield
        yield
        for i in range(NI + LAG + 1):
            if i < NI:
                n, m = self.keys_of(i % QT), i % self.PR
                act.wait_ge(self.max_done, b * NI + i + 1)
                if i >= self.PR:
                    u, qt = divmod(i - self.PR, QT)
                    T.wait_filled(act, b, self.use_of(u, 2 * qt))
                for hh in range(2):
                    e = act.activation(self.P[m][:, hh, 0:n], self.scores[:, hh * 512:hh * 512 + n], ACT.Exp,
                                       bias=self.nmax[:, m, hh:hh + 1], accum_out=self.sums[:, m, hh:hh + 1])
                e.then_inc(self.exp_done, 1)
            j = i - LAG
            if 0 <= j < NI and j % QT == 1:
                self.pt_copy(act, lambda dst, src: act.activation(dst, src, ACT.Copy), b, j // QT, 1)
            yield
        yield

    def pt_copy(self, eng, copy, b, u, qt):
        T, k, nb = self.T, self.use_of(u, qt), qt + 1
        T.wait_filled(eng, b, k)
        if u >= 2:
            T.wait_filled(eng, b, self.use_of(u - 2, 3))
        c = copy(self.PT[u % 2][:, :, 0:nb, qt * 128:qt * 128 + 128],
                 T.bank(k)[:, 0:2 * nb * 128].rearrange("p (j t q) -> p j t q", j=2, t=nb))
        if qt == 1:
            c.then_inc(T.free(k), 1)

    def vector(self, v, b):
        T, w, x, NI, LAG, K, c0 = self.T, self.w, self.g["x"], self.NI, self.LAG, self.K, self.batch(b)
        v.tensor_copy(self.ctx2[:, :, :], self.cnT[:, c0, :].unsqueeze(1).to_broadcast([128, 2, SC]))\
            .then_inc(self.ctx2_done, 1)
        yield
        for n in range(4):
            yield
        for c in range(self.NP):
            if c % 2 == 0:
                T.wait_filled(v, b, self.K0 + c)
                for j in range(2):
                    kk = v.tensor_scalar(self.kbd[:, 2 * c + j, :], T.bank(self.K0 + c)[:, 0:K],
                                         w("kmask")[:, j:j + 1], None, ALU.mult)
                kk.then_inc(T.free(self.K0 + c), 1)
            yield
        for n in range(2 * QT):
            yield
        for hf in range(2):
            k = self.VC0 + hf
            T.wait_filled(v, b, k)
            for j in range(2):
                cc = v.tensor_copy(self.vc[64 * j:64 * j + 64, 4 * hf:4 * hf + 4, 64 * j:64 * j + 64],
                                   T.bank(k)[64 * j:64 * j + 64, :]
                                   .rearrange("p (m j e) -> p m j e", j=2, e=self.d)[:, :, j, :])
                if j == 0:
                    cc.then_inc(self.vc_half, 1)
                    v.wait_ge(self.vc_half, 2 * b + hf + 1)
            cc.then_inc(T.free(k), 1)
            yield
        for i in range(NI + LAG + 1):
            j = i - LAG - 1
            if j >= 0 and j % QT == QT - 1:
                u = j // QT
                k = self.use_of(u, 3)
                T.wait_filled(v, b, k)
                v.tensor_copy(self.OT[:, u, :], T.bank(k)[:, 0:S]).then_inc(T.free(k), 1)
            if i < NI:
                n = self.keys_of(i % QT)
                v.wait_ge(self.s_filled, b * NI + i + 1)
                v.tensor_reduce(self.nmax[:, i % self.PR, :],
                                self.scores[:, :].rearrange("p (j k) -> p j k", j=2)[:, :, 0:n],
                                AX.X, ALU.max, negate=True).then_inc(self.max_done, 1)
            j = i - 1
            if 0 <= j < NI:
                v.wait_ge(self.exp_done, b * NI + j + 2)
                v.reciprocal(self.rec[:, j % self.PR, :], self.sums[:, j % self.PR, :]).then_inc(self.rec_done, 1)
            j = i - LAG
            if 0 <= j < NI:
                u, qt = divmod(j, QT)
                if qt == 0:
                    self.pt_copy(v, v.tensor_copy, b, u, qt)
                    k, at = self.use_of(u, 0), 256
                else:
                    k, at = self.use_of(u, 2), 0
                    T.wait_filled(v, b, k)
                v.tensor_copy(self.PTc[u % 2][:, qt * 128:qt * 128 + 128], T.bank(k)[:, at:at + 128])\
                    .then_inc(T.free(k), 1)
            if i == NI - 1:
                self.nrm.take_moments(v, b + 1)
            if i == NI:
                self.nrm.norm_rows(v, b + 1)
            if i == NI + 1:
                self.nrm2.take_moments(v, b + 1)
            if i == NI + 2:
                self.nrm2.norm_rows(v, b + 1)
            yield
        k = self.OUT
        T.wait_filled(v, b, k)
        v.tensor_tensor(x[:, bass.ds(QT * c0, QT), :], x[:, bass.ds(QT * c0, QT), :],
                        T.bank(k)[:, 0:QT * 128].rearrange("p (t f) -> p t f", t=QT),
                        ALU.add).then_inc(T.free(k), 1)
        T.wait_emptied(v, b, k)
        v.tensor_tensor(x[:, bass.ds(QT * c0, QT), :], x[:, bass.ds(QT * c0, QT), :],
                        w("ob").unsqueeze(1).to_broadcast([128, QT, D]), ALU.add).then_inc(self.added, 1)
        yield


def L3_xattn(nc, g, wts):
    LANES = 2
    CT = B * SC // 128
    st = Stage(nc, "l3x")
    w, loaded = wts.of, wts.loaded
    raw = st.sb("raw", [128, CT, D])
    cstats = st.sb("cstats", [128, CT, 6])
    cmv = st.sb("cmv", [128, CT, 2])
    cveps = st.sb("cveps", [128, CT])
    crstd = st.sb("crstd", [128, CT])
    chalf = st.sb("chalf", [128, CT])
    cnT = st.sb("cnT", [128, B, SC])
    raw_in, half_set = st.sem("raw_in"), st.sem("half_set")
    cstep, cfilled, cn_done = st.sem("cstep"), st.sem("cfilled"), st.sem("cn_done")

    lanes = [L3_xattn_lane(st, n, LANES, g, w, cnT) for n in range(LANES)]
    cps = lanes[0].scores

    with nc.Block("l3x_block") as block:
        @block.sync
        def _(sp):
            sp.dma_start(raw[:, :, :], g["dram"]["ctx"].rearrange("(t p) d -> p t d", p=128)).then_inc(raw_in, 16)
            for ln in lanes:
                ln.sync_setup(sp)

        @block.gpsimd
        def _(pool):
            pool.memset(chalf[:, :], -0.5).then_inc(half_set, 1)
            for ln in lanes:
                ln.pool_setup(pool)
            pool.wait_ge(half_set, 1)
            pool.wait_ge(cstep, CT + 1)
            pool.tensor_tensor(crstd[:, :], cveps[:, :], chalf[:, :], ALU.pow).then_inc(cstep, 1)
            for ln in lanes:
                ln.nrm.pool(pool, 0)
            for ln in lanes:
                ln.nrm2.pool(pool, 0)
            with pool.Fori(0, B // LANES) as i:
                in_turn(*(ln.pool(pool, i) for ln in lanes))

        @block.tensor
        def _(pe):
            pe.wait_ge(loaded, 16)
            pe.wait_ge(cstep, 2 * CT + 2)
            for t in range(CT):
                mm = pe.transpose(cps[:, t * 128:t * 128 + 128], raw[:, t, :], g["ident"][:, :])
            mm.then_inc(cfilled, 1)
            pe.wait_ge(cn_done, 1)
            with pe.Fori(0, B // LANES) as i:
                in_turn(*(ln.tensor(pe, i) for ln in lanes))

        @block.scalar
        def _(act):
            act.wait_ge(loaded, 16)
            act.wait_ge(cfilled, 1)
            act.activation(cnT[:, :, :], cps[:, 0:CT * 128].rearrange("p (b k) -> p b k", b=B), ACT.Identity,
                           scale=w("g2"), bias=w("b2")).then_inc(cn_done, 1)
            with act.Fori(0, B // LANES) as i:
                in_turn(*(ln.scalar(act, i) for ln in lanes))

        @block.vector
        def _(v):
            v.wait_ge(loaded, 16)
            v.wait_ge(raw_in, 16)
            for t in range(CT):
                v.bn_stats(cstats[:, t, :], raw[:, t, :])
            v.drain()
            for t in range(CT):
                v.bn_aggr(cmv[:, t, :], cstats[:, t, :]).then_inc(cstep, 1)
            v.wait_ge(cstep, CT)
            v.tensor_scalar(cveps[:, :], cmv[:, :, 1], EPS, None, ALU.add).then_inc(cstep, 1)
            v.wait_ge(cstep, CT + 2)
            for t in range(CT):
                v.tensor_scalar(raw[:, t, :], raw[:, t, :], cmv[:, t, 0:1], crstd[:, t:t + 1], ALU.subtract, ALU.mult)\
                    .then_inc(cstep, 1)
            v.wait_ge(cn_done, 1)
            for ln in lanes:
                v.wait_ge(ln.v_set, 1)
                ln.nrm.take_moments(v, 0)
            for ln in lanes:
                ln.nrm.norm_rows(v, 0)
            for ln in lanes:
                ln.nrm2.take_moments(v, 0)
            for ln in lanes:
                ln.nrm2.norm_rows(v, 0)
            with v.Fori(0, B // LANES) as i:
                in_turn(*(ln.vector(v, i) for ln in lanes))
    st.close()


def L3_ffn(nc, g, wts):
    name = "l3f"
    x, ident, identb = g["x"], g["ident"], g["identb"]
    E, F = 8, 512
    CAP = B * S // E
    FC, ST = F // 128, CAP // 128
    W1, W2 = g["dram"]["L3_ffn_W1"], g["dram"]["L3_ffn_W2"]
    slots = nc.dram_tensor("slots", [E * CAP, D], F32, kind="Internal").ap()
    outs = nc.dram_tensor("outs", [E * CAP, D], F32, kind="Internal").ap()
    st = Stage(nc, name)
    w, loaded = wts.of, wts.loaded
    nrm = Norm(st, x)
    xn = st.sb("xn_all", [128, NT, D])
    xnT = st.sb("xnT", [128, S])
    zeros = st.sb("zeros", [128, NT, D])
    logit = st.sb("logit", [128, NT, E])
    work = st.sb("work", [128, NT, E])
    cand = st.sb("cand", [128, NT, E])
    first = st.sb("first", [128, NT])
    lmax = st.sb("lmax", [128, NT])
    esum = st.sb("esum", [128, NT])
    prob = st.sb("prob", [128, NT])
    hot = st.sb("hot", [128, NT, E])
    hotb = st.sb("hotb", [128, NT, E], BF16)
    below_b = st.sb("below_b", [128, 128], BF16)
    rank = st.sb("rank", [128, NT])
    keep = st.sb("keep", [128, NT])
    weight = st.sb("weight", [128, NT])
    slotf = st.sb("slotf", [128, NT])
    slot = st.sb("slot", [128, NT])
    to_f = st.sb("to_f", [128, NT])
    to_u = st.sb("to_u", [128, NT], U32)
    from_u = st.sb("from_u", [128, NT], U32)
    w1 = [st.sb(f"w1_{i}", [128, F]) for i in range(2)]
    w2 = [st.sb(f"w2_{i}", [128, FC, D]) for i in range(2)]
    xe = [st.sb(f"xe{i}", [128, ST, D]) for i in range(2)]
    xeT = [st.sb(f"xeT{i}", [128, CAP]) for i in range(2)]
    hT = [st.sb(f"hT{i}", [128, FC, CAP]) for i in range(2)]
    ye = [st.sb(f"ye{i}", [128, ST, D]) for i in range(2)]
    yg = st.sb("yg", [128, NT, D])
    tps, lps, rps = st.ps("tps"), st.ps("lps"), st.ps("rps")
    eps_ = [st.ps(f"x{i}") for i in range(1)]
    hps = [st.ps(f"h{i}") for i in range(2)]
    yps = [st.ps(f"y{i}") for i in range(2)]
    set_up = st.sem("set_up")
    t_filled, xnT_done, l_filled, l_left = st.sem("t_filled"), st.sem("xnT_done"), st.sem("l_filled"), st.sem("l_left")
    rstep, exped, hot_done, r_filled = st.sem("rstep"), st.sem("exped"), st.sem("hot_done"), st.sem("r_filled")
    zeroed, indexed, scattered = st.sem("zeroed"), st.sem("indexed"), st.sem("scattered")
    w_in = [st.sem(f"w_in{i}") for i in range(2)]
    x_in = [st.sem(f"x_in{i}") for i in range(2)]
    xe_filled, xeT_done, h_filled, h_done = st.sem("xe_filled"), st.sem("xeT_done"), st.sem("h_filled"), st.sem("h_done")
    y_filled, ye_done = st.sem("y_filled"), st.sem("ye_done")
    ye_out = [st.sem(f"ye_out{i}") for i in range(2)]
    gathered, added = st.sem("gathered"), st.sem("added")

    with nc.Block(f"{name}_block") as block:
        @block.sync
        def _(sp):
            sp.wait_ge(set_up, 1)
            sp.dma_start(slots.rearrange("(t p) d -> p t d", p=128), zeros[:, :, :]).then_inc(zeroed, 16)
            sp.sem_inc(y_filled, 2)
            sp.sem_inc(xe_filled, 2)
            with sp.Fori(0, E // 2) as m:
                for p in range(2):
                    e = 2 * m + p
                    sp.wait_ge(y_filled, e + 1)
                    sp.dma_start(w1[p][:, :], W1[e, :, :]).then_inc(w_in[p], 16)
                    sp.dma_start(w2[p][:, :, :], W2[e, :, :].rearrange("(c p) d -> p c d", p=128)).then_inc(w_in[p], 16)
                    sp.wait_ge(scattered, 16 * NT)
                    sp.wait_ge(xe_filled, e + 1)
                    sp.dma_start(xe[p][:, :, :], slots[bass.ds(CAP * e, CAP), :].rearrange("(t p) d -> p t d", p=128))\
                        .then_inc(x_in[p], 16)

        @block.gpsimd
        def _(pool):
            nrm.pool_setup(pool)
            pool.memset(zeros[:, :, :], 0.0).then_inc(set_up, 1)
            with pool.Fori(0, B) as b:
                nrm.pool(pool, b)
            pool.wait_ge(zeroed, 16)
            pool.wait_ge(indexed, 2)
            pool.wait_ge(xnT_done, B)
            for t in range(NT):
                pool.indirect_dma_start(slots, bass.IndirectOffsetOnAxis(ap=to_u[:, t:t + 1], axis=0), xn[:, t, :], None,
                                        bounds_check=E * CAP - 1, oob_is_err=False).then_inc(scattered, 16)
            for p in range(2):
                pool.wait_ge(ye_out[p], 16 * E // 2 + 16)
            for t in range(NT):
                pool.indirect_dma_start(yg[:, t, :], None, outs, bass.IndirectOffsetOnAxis(ap=from_u[:, t:t + 1], axis=0))\
                    .then_inc(gathered, 16)

        @block.tensor
        def _(pe):
            pe.wait_ge(loaded, 16)
            with pe.Fori(0, B) as b:
                nrm.wait(pe, b)
                for t in range(QT):
                    mm = pe.transpose(tps[:, t * 128:t * 128 + 128], nrm.xn[:, t, :], ident[:, :])
                mm.then_inc(t_filled, 1)
                pe.wait_ge(xnT_done, b + 1)
                pe.wait_ge(l_left, b + 1)
                for t in range(QT):
                    mm = pe.matmul(lps[:, t * E:t * E + E], xnT[:, t * 128:t * 128 + 128], w("r"), start=True, stop=True)
                mm.then_inc(l_filled, 1)
            pe.wait_ge(hot_done, 2)
            pe.matmul(rps[:, 0:NT * E], below_b[:, :], hotb[:, :, :], start=True, stop=False)
            for t in range(NT - 1):
                n = NT - 1 - t
                mm = pe.matmul(rps[:, (t + 1) * E:NT * E].rearrange("p (t e) -> p t e", e=E), g["onesb"][:, :],
                               hotb[:, t, :].unsqueeze(1).to_broadcast([128, n, E]), start=False, stop=(t == NT - 2))
            mm.then_inc(r_filled, 1)
            with pe.Fori(0, E // 2) as m:
                for p in range(2):
                    e = 2 * m + p
                    pe.wait_ge(x_in[p], 16 * m + 16)
                    for t in range(ST):
                        mm = pe.transpose(eps_[0][:, t * 128:t * 128 + 128], xe[p][:, t, :], ident[:, :])
                    mm.then_inc(xe_filled, 1)
                    pe.wait_ge(xeT_done, e + 1)
                    pe.wait_ge(w_in[p], 32 * m + 32)
                    for n in range(2):
                        pe.wait_ge(h_done, 2 * e + n + 1)
                        for j in range(2):
                            c = 2 * n + j
                            mm = pe.matmul(hps[n][:, j * CAP:(j + 1) * CAP], w1[p][:, c * 128:c * 128 + 128],
                                           xeT[p][:, :], start=True, stop=True)
                        mm.then_inc(h_filled, 1)
                    pe.wait_ge(h_done, 2 * e + 2 + 2)
                    pe.wait_ge(ye_done, e + 1)
                    for t in range(ST):
                        for c in range(FC):
                            mm = pe.matmul(yps[p][:, t * D:t * D + D], hT[p][:, c, t * 128:t * 128 + 128], w2[p][:, c, :],
                                           start=(c == 0), stop=(c == FC - 1))
                    mm.then_inc(y_filled, 1)

        @block.scalar
        def _(act):
            act.sem_inc(h_done, 2)
            act.sem_inc(ye_done, 2)
            act.sem_inc(l_left, 1)
            with act.Fori(0, B) as b:
                act.wait_ge(t_filled, b + 1)
                act.activation(xnT[:, :], tps[:, 0:S], ACT.Copy).then_inc(xnT_done, 1)
            act.wait_ge(rstep, 2)
            act.activation(work[:, :, :], work[:, :, :], ACT.Exp).then_inc(exped, 1)
            with act.Fori(0, E // 2) as m:
                for p in range(2):
                    e = 2 * m + p
                    act.wait_ge(xe_filled, e + 1 + 2)
                    act.activation(xeT[p][:, :], eps_[0][:, 0:CAP], ACT.Copy).then_inc(xeT_done, 1)
                    act.wait_ge(y_filled, e + 1)
                    for n in range(2):
                        act.wait_ge(h_filled, 2 * e + n + 1)
                        act.activation(hT[p][:, 2 * n:2 * n + 2, :], hps[n][:, :].rearrange("p (c s) -> p c s", c=2),
                                       ACT.Relu).then_inc(h_done, 1)
                    act.wait_ge(ye_done, e + 1 + 2)
                    act.dma_start(outs[bass.ds(CAP * e, CAP), :].rearrange("(t p) d -> p t d", p=128), ye[p][:, :, :])\
                        .then_inc(ye_out[p], 16)

        @block.vector
        def _(v):
            v.wait_ge(loaded, 16)
            v.sem_inc(ye_out[0], 16)
            v.sem_inc(ye_out[1], 16)
            with v.Fori(0, B) as b:
                nrm.vector(v, b)
                nrm.wait(v, b)
                v.tensor_scalar(xn[:, bass.ds(QT * b, QT), :], nrm.xn[:, :, :], 1.0, None, ALU.mult)
                v.wait_ge(l_filled, b + 1)
                v.tensor_scalar(logit[:, bass.ds(QT * b, QT), :], lps[:, 0:QT * E].rearrange("p (t e) -> p t e", e=E), 1.0,
                                None, ALU.mult).then_inc(l_left, 1)
            v.wait_ge(l_left, B + 1)
            v.tensor_reduce(lmax[:, :], logit[:, :, :], AX.X, ALU.max).then_inc(rstep, 1)
            v.wait_ge(rstep, 1)
            v.tensor_tensor(work[:, :, :], logit[:, :, :], lmax[:, :].unsqueeze(2).to_broadcast([128, NT, E]),
                            ALU.subtract).then_inc(rstep, 1)
            v.wait_ge(exped, 1)
            v.tensor_reduce(esum[:, :], work[:, :, :], AX.X, ALU.add).then_inc(rstep, 1)
            v.tensor_reduce(lmax[:, :], work[:, :, :], AX.X, ALU.max).then_inc(rstep, 1)
            v.wait_ge(rstep, 4)
            v.reciprocal(prob[:, :], esum[:, :]).then_inc(rstep, 1)
            v.tensor_tensor(cand[:, :, :], work[:, :, :], lmax[:, :].unsqueeze(2).to_broadcast([128, NT, E]), ALU.is_lt)\
                .then_inc(rstep, 1)
            v.wait_ge(rstep, 6)
            v.scalar_tensor_tensor(hot[:, :, :].rearrange("p t e -> p (t e)"), cand[:, :, :].rearrange("p t e -> p (t e)"),
                                   float(E), w("expert"), ALU.mult, ALU.add).then_inc(rstep, 1)
            v.wait_ge(rstep, 7)
            v.tensor_reduce(first[:, :], hot[:, :, :], AX.X, ALU.min).then_inc(rstep, 1)
            v.wait_ge(rstep, 8)
            v.tensor_tensor(cand[:, :, :], w("expert").rearrange("p (t e) -> p t e", e=E),
                            first[:, :].unsqueeze(2).to_broadcast([128, NT, E]), ALU.is_equal).then_inc(rstep, 1)
            v.wait_ge(rstep, 9)
            v.tensor_copy(hotb[:, :, :], cand[:, :, :]).then_inc(hot_done, 1)
            v.tensor_copy(below_b[:, :], w("below")).then_inc(hot_done, 1)
            v.wait_ge(r_filled, 1)
            v.tensor_tensor(work[:, :, :], rps[:, 0:NT * E].rearrange("p (t e) -> p t e", e=E), cand[:, :, :], ALU.mult)\
                .then_inc(rstep, 1)
            v.wait_ge(rstep, 10)
            v.tensor_reduce(rank[:, :], work[:, :, :], AX.X, ALU.add).then_inc(rstep, 1)
            v.wait_ge(rstep, 11)
            v.tensor_scalar(keep[:, :], rank[:, :], float(CAP), None, ALU.is_lt).then_inc(rstep, 1)
            v.scalar_tensor_tensor(slot[:, :], first[:, :], float(CAP), rank[:, :], ALU.mult, ALU.add).then_inc(rstep, 1)
            v.wait_ge(rstep, 13)
            v.tensor_tensor(weight[:, :], prob[:, :], keep[:, :], ALU.mult).then_inc(rstep, 1)
            v.tensor_tensor(slotf[:, :], slot[:, :], keep[:, :], ALU.mult).then_inc(rstep, 1)
            v.tensor_scalar(to_f[:, :], keep[:, :], -float(E * CAP), float(E * CAP), ALU.mult, ALU.add).then_inc(rstep, 1)
            v.wait_ge(rstep, 16)
            v.tensor_tensor(to_u[:, :], to_f[:, :], slotf[:, :], ALU.add).then_inc(indexed, 1)
            v.tensor_copy(from_u[:, :], slotf[:, :]).then_inc(indexed, 1)
            with v.Fori(0, E // 2) as m:
                for p in range(2):
                    e = 2 * m + p
                    v.wait_ge(ye_out[p], 16 * m + 16)
                    v.wait_ge(y_filled, e + 1 + 2)
                    v.tensor_scalar(ye[p][:, :, :], yps[p][:, 0:ST * D].rearrange("p (t d) -> p t d", t=ST), 1.0, None,
                                    ALU.mult).then_inc(ye_done, 1)
            for t in range(NT):
                if t == 0:
                    v.wait_ge(gathered, 16 * NT)
                v.scalar_tensor_tensor(x[:, t, :], yg[:, t, :], weight[:, t:t + 1], x[:, t, :], ALU.mult, ALU.add)\
                    .then_inc(added, 1)
    st.close()


def L0_ffn(nc, g, wts):
    name = "l0f"
    x, ident = g["x"], g["ident"]
    E, F, F2 = 8, 512, 256
    FC = F // 128
    st = Stage(nc, name)
    NORM0, NORM1, PLAIN2 = (0, 4), (1, 5), (2, 6)
    order = [("xT",), ("route",)]
    order += [("up", e, n) for e in NORM0 for n in range(2)]
    order += [("z", e, t) for e in NORM0 for t in range(QT)]
    order += [("up", e, n) for e in NORM1 for n in range(2)] + [("mid", e) for e in NORM1]
    order += [("up", e, n) for e in PLAIN2 for n in range(2)]
    order += [("z", e, t) for e in NORM1 for t in range(QT)]
    order += [("flat", e, n) for e in PLAIN2 for n in range(2)]
    order += [("up", e, n) for e in (3, 7) for n in range(2)] + [("wT",), ("bias",)]
    order += [("zT", e, t) for e in NORM0 for t in range(QT)]
    DOWN = (3, 7, 2, 6, 0, 4, 1, 5)
    order += [("down", e) for e in DOWN[:6]]
    order += [("zT", e, t) for e in NORM1 for t in range(QT)]
    order += [("down", e) for e in DOWN[6:]]
    at = {label: k for k, label in enumerate(order)}
    R = Ring(st, "r", 8, len(order))

    w, loaded = wts.of, wts.loaded
    nrm = Norm(st, x)
    nrm2 = Norm(st, x, of=nrm)
    xnT = st.sb("xnT", [128, S])
    hT = st.sb("hT", [128, E, FC, S])
    flat = st.sb("flat", [128, 2, FC, S])
    mid = st.sb("mid", [128, 2, 2, S])
    z = st.sb("z", [128, 2, 4, F])
    zstats = st.sb("zstats", [128, 4, 6])
    zmv = st.sb("zmv", [128, 4, 2])
    zveps = st.sb("zveps", [128, 4])
    zrstd = st.sb("zrstd", [128, 4])
    zhalf = st.sb("zhalf", [128, 4])
    e_base = st.sb("e_base", [128, QT * E])
    lg = st.sb("lg", [128, QT, E])
    lmax = st.sb("lmax", [128, QT])
    ex = st.sb("ex", [128, QT, E])
    more = st.sb("more", [128, QT, E, E])
    same = st.sb("same", [128, QT, E, E])
    place = st.sb("place", [128, QT, E])
    wsum = st.sb("wsum", [128, QT])
    wrec = st.sb("wrec", [128, QT])
    wt = st.sb("wt", [128, QT, E])
    wT = st.sb("wT", [E, S])
    acc = st.sb("acc", [128, QT, D])

    consts = st.sem("consts")
    rt, powed, wt_done = st.sem("rt"), st.sem("powed"), st.sem("wt_done")
    zaggr, zveps_done, zrstd_done = st.sem("zaggr"), st.sem("zveps_done"), st.sem("zrstd_done")
    zn_done, zg_done, zb_done, zact_done = (st.sem(n) for n in ("zn_done", "zg_done", "zb_done", "zact_done"))
    acc_done, x_done = st.sem("acc_done"), st.sem("x_done")
    RS = 11

    def w_of(key, i, n):
        return w(key)[:, i * n:(i + 1) * n]

    def tile(e, t):
        return (0, QT * NORM0.index(e) + t) if e in NORM0 else (1, QT * NORM1.index(e) + t)

    with nc.Block(f"{name}_block") as block:
        @block.sync
        def _(sp):
            R.credit(sp)

        @block.gpsimd
        def _(pool):
            nrm.pool_setup(pool)
            nrm2.pool_setup(pool)
            pool.memset(zhalf[:, :], -0.5).then_inc(consts, 1)
            pool.memset(e_base[:, :], float(np.e)).then_inc(consts, 1)
            pool.wait_ge(consts, 2)
            pool.wait_ge(loaded, 16)
            nrm.pool(pool, 0)
            nrm2.pool(pool, 0)

            def batch(b, ahead):
                pool.wait_ge(rt, RS * b + 2)
                pool.tensor_tensor(ex[:, :, :].rearrange("p t e -> p (t e)"), e_base[:, :],
                                   lg[:, :, :].rearrange("p t e -> p (t e)"), ALU.pow).then_inc(powed, 1)
                for gr, experts in enumerate((NORM0, NORM1)):
                    pool.wait_ge(zveps_done, 2 * b + gr + 1)
                    pool.tensor_tensor(zrstd[:, :], zveps[:, :], zhalf[:, :], ALU.pow).then_inc(zrstd_done, 1)
                    for i in range(4):
                        n = 8 * b + 4 * gr + i + 1
                        zz = z[:, gr, i, :]
                        pool.wait_ge(zn_done, n)
                        pool.tensor_tensor(zz, zz, w_of(f"ln{gr}_g", i // QT, F), ALU.mult).then_inc(zg_done, 1)
                        pool.wait_ge(zg_done, n)
                        pool.tensor_tensor(zz, zz, w_of(f"ln{gr}_b", i // QT, F), ALU.add).then_inc(zb_done, 1)
                if ahead:
                    nrm.pool(pool, b + 1)
                    nrm2.pool(pool, b + 1)

            with pool.Fori(0, B - 1) as b:
                batch(b, True)
            batch(B - 1, False)

        @block.tensor
        def _(pe):
            pe.wait_ge(loaded, 16)
            with pe.Fori(0, B) as b:
                for k, label in enumerate(order):
                    kind, e = label[0], label[1] if len(label) > 1 else None
                    bank = R.bank(k)
                    if kind == "xT":
                        nrm2.wait(pe, b)
                        R.wait_free(pe, b, k)
                        for t in range(QT):
                            mm = pe.transpose(bank[:, t * 128:t * 128 + 128], nrm2.xn[:, t, :], ident[:, :])
                    if kind == "route":
                        R.wait_for(pe, b, [at["xT",]], k) if k >= R.n else R.wait_emptied(pe, b, at["xT",])
                        R.wait_free(pe, b, k)
                        for t in range(QT):
                            mm = pe.matmul(bank[:, t * E:t * E + E], xnT[:, t * 128:t * 128 + 128], w("router"),
                                           start=True, stop=True)
                    if kind == "up":
                        R.wait_free(pe, b, k)
                        for j in range(2):
                            c = FC * e + 2 * label[2] + j
                            mm = pe.matmul(bank[:, j * S:(j + 1) * S], w_of("up", c, 128), xnT[:, :], start=True, stop=True)
                    if kind == "z":
                        gr, i = tile(e, label[2])
                        t = label[2]
                        if gr == 0:
                            R.wait_for(pe, b, [at["up", e, n] for n in range(2)], k)
                            for c in range(FC):
                                mm = pe.matmul(bank[:, :], hT[:, e, c, t * 128:t * 128 + 128],
                                               w_of("spec0", FC * (i // QT) + c, F), start=(c == 0), stop=(c == FC - 1))
                        else:
                            R.wait_for(pe, b, [at["mid", e]], k)
                            for c in range(2):
                                mm = pe.matmul(bank[:, :], mid[:, i // QT, c, t * 128:t * 128 + 128],
                                               w_of("spec1b", 2 * (i // QT) + c, F), start=(c == 0), stop=(c == 1))
                    if kind == "mid":
                        R.wait_for(pe, b, [at["up", e, n] for n in range(2)], k)
                        for j in range(2):
                            for c in range(FC):
                                wc = w_of("spec1a", FC * NORM1.index(e) + c, F2)[:, j * 128:j * 128 + 128]
                                mm = pe.matmul(bank[:, j * S:(j + 1) * S], wc, hT[:, e, c, :], start=(c == 0),
                                               stop=(c == FC - 1))
                    if kind == "flat":
                        R.wait_for(pe, b, [at["up", e, n] for n in range(2)], k)
                        for j in range(2):
                            o = 2 * label[2] + j
                            for c in range(FC):
                                wc = w_of("spec2", FC * PLAIN2.index(e) + c, F)[:, o * 128:o * 128 + 128]
                                mm = pe.matmul(bank[:, j * S:(j + 1) * S], wc, hT[:, e, c, :], start=(c == 0),
                                               stop=(c == FC - 1))
                    if kind == "wT":
                        pe.wait_ge(wt_done, b + 1)
                        R.wait_free(pe, b, k)
                        for t in range(QT):
                            mm = pe.transpose(bank[0:E, t * 128:t * 128 + 128], wt[:, t, :], ident[:, :])
                    if kind == "bias":
                        R.wait_for(pe, b, [at["wT",]], k)
                        for t in range(QT):
                            mm = pe.matmul(bank[:, t * D:t * D + D], wT[:, t * 128:t * 128 + 128], w("down_b")[0:E, :],
                                           start=True, stop=True)
                    if kind == "zT":
                        gr, i = tile(e, label[2])
                        pe.wait_ge(zb_done if gr else zact_done, (8 * b + 4 + i + 1) if gr else (4 * b + i + 1))
                        R.wait_free(pe, b, k)
                        for c in range(FC):
                            mm = pe.transpose(bank[:, c * 128:c * 128 + 128], z[:, gr, i, c * 128:c * 128 + 128],
                                              ident[:, :])
                    if kind == "down":
                        if e in PLAIN2:
                            src, need = flat[:, PLAIN2.index(e), :, :], [at["flat", e, n] for n in range(2)]
                        elif e in (3, 7):
                            src, need = hT[:, e, :, :], [at["up", e, n] for n in range(2)]
                        else:
                            src, need = hT[:, e, :, :], [at["zT", e, t] for t in range(QT)]
                        R.wait_for(pe, b, need, k)
                        for t in range(QT):
                            for c in range(FC):
                                mm = pe.matmul(bank[:, t * D:t * D + D], src[:, c, t * 128:t * 128 + 128],
                                               w_of("down", FC * e + c, D), start=(c == 0), stop=(c == FC - 1))
                    mm.then_inc(R.full(k), 1)

        @block.scalar
        def _(act):
            act.wait_ge(loaded, 16)
            with act.Fori(0, B) as b:
                for k, label in enumerate(order):
                    kind, e = label[0], label[1] if len(label) > 1 else None
                    bank = R.bank(k)
                    if kind == "xT":
                        R.wait_filled(act, b, k)
                        act.activation(xnT[:, :], bank[:, 0:S], ACT.Identity, scale=w("ln_g"), bias=w("ln_b"))\
                            .then_inc(R.free(k), 1)
                    if kind in ("up", "mid", "flat"):
                        R.wait_filled(act, b, k)
                        for j in range(2):
                            src = bank[:, j * S:(j + 1) * S]
                            if kind == "up":
                                c = 2 * label[2] + j
                                dst, bias = hT[:, e, c, :], w("up_b")[:, FC * e + c:FC * e + c + 1]
                            elif kind == "mid":
                                m = NORM1.index(e)
                                dst, bias = mid[:, m, j, :], w("spec1a_b")[:, 2 * m + j:2 * m + j + 1]
                            else:
                                c, m = 2 * label[2] + j, PLAIN2.index(e)
                                dst, bias = flat[:, m, c, :], w("spec2_b")[:, FC * m + c:FC * m + c + 1]
                            a = act.activation(dst, src, ACT.Gelu, bias=bias)
                        a.then_inc(R.free(k), 1)
                    if kind == "wT":
                        R.wait_filled(act, b, k)
                        act.activation(wT[:, :], bank[0:E, 0:S], ACT.Copy).then_inc(R.free(k), 1)
                        for i in range(4):
                            act.wait_ge(zb_done, 8 * b + i + 1)
                            act.activation(z[:, 0, i, :], z[:, 0, i, :], ACT.Gelu).then_inc(zact_done, 1)
                    if kind == "zT":
                        t = label[2]
                        R.wait_filled(act, b, k)
                        act.activation(hT[:, e, :, t * 128:t * 128 + 128], bank[:, :].rearrange("p (c q) -> p c q", c=FC),
                                       ACT.Copy).then_inc(R.free(k), 1)

        @block.vector
        def _(v):
            v.wait_ge(loaded, 16)
            nrm.vector(v, 0)
            nrm2.vector(v, 0)

            def batch(b, ahead):
                k = at["route",]
                R.wait_filled(v, b, k)
                rl = R.bank(k)[:, 0:QT * E].rearrange("p (t e) -> p t e", e=E)
                v.tensor_reduce(lmax[:, :], rl, AX.X, ALU.max).then_inc(rt, 1)
                v.wait_ge(rt, RS * b + 1)
                v.tensor_tensor(lg[:, :, :], rl, lmax[:, :].unsqueeze(2).to_broadcast([128, QT, E]), ALU.subtract)\
                    .then_inc(rt, 1)
                v.wait_ge(rt, RS * b + 2)
                v.sem_inc(R.free(k), 1)
                v.wait_ge(powed, b + 1)
                for t in range(QT):
                    them = ex[:, t, :].unsqueeze(1).to_broadcast([128, E, E])
                    me = ex[:, t, :].unsqueeze(2).to_broadcast([128, E, E])
                    v.tensor_tensor(more[:, t, :, :], them, me, ALU.is_gt)
                    v.tensor_tensor(same[:, t, :, :], them, me, ALU.is_equal).then_inc(rt, 1)
                v.wait_ge(rt, RS * b + 4)
                for t in range(QT):
                    v.tensor_tensor(same[:, t, :, :], same[:, t, :, :], w("earlier").rearrange("p (j i) -> p j i", i=E),
                                    ALU.mult).then_inc(rt, 1)
                v.wait_ge(rt, RS * b + 6)
                v.tensor_tensor(more[:, :, :, :].rearrange("p t j i -> p (t j i)"),
                                more[:, :, :, :].rearrange("p t j i -> p (t j i)"),
                                same[:, :, :, :].rearrange("p t j i -> p (t j i)"), ALU.add).then_inc(rt, 1)
                v.wait_ge(rt, RS * b + 7)
                v.tensor_reduce(place[:, :, :].rearrange("p t j -> p (t j)"),
                                more[:, :, :, :].rearrange("p t j i -> p (t j) i"), AX.X, ALU.add).then_inc(rt, 1)
                v.wait_ge(rt, RS * b + 8)
                v.scalar_tensor_tensor(place[:, :, :], place[:, :, :], 2.0, ex[:, :, :], ALU.is_lt, ALU.mult)\
                    .then_inc(rt, 1)
                v.wait_ge(rt, RS * b + 9)
                v.tensor_reduce(wsum[:, :], place[:, :, :], AX.X, ALU.add).then_inc(rt, 1)
                v.wait_ge(rt, RS * b + 10)
                v.reciprocal(wrec[:, :], wsum[:, :]).then_inc(rt, 1)
                v.wait_ge(rt, RS * b + 11)
                v.tensor_tensor(wt[:, :, :], place[:, :, :], wrec[:, :].unsqueeze(2).to_broadcast([128, QT, E]), ALU.mult)\
                    .then_inc(wt_done, 1)
                for gr, experts in enumerate((NORM0, NORM1)):
                    for i in range(4):
                        k = at["z", experts[i // QT], i % QT]
                        R.wait_filled(v, b, k)
                        v.tensor_tensor(z[:, gr, i, :], R.bank(k)[:, :], w_of(f"zbias{gr}", i // QT, F), ALU.add)\
                            .then_inc(R.free(k), 1)
                    for i in range(4):
                        R.wait_emptied(v, b, at["z", experts[i // QT], i % QT])
                        v.bn_stats(zstats[:, i, :], z[:, gr, i, :])
                    v.drain()
                    for i in range(4):
                        v.bn_aggr(zmv[:, i, :], zstats[:, i, :]).then_inc(zaggr, 1)
                    v.wait_ge(zaggr, 8 * b + 4 * gr + 4)
                    v.tensor_scalar(zveps[:, :], zmv[:, :, 1], EPS, None, ALU.add).then_inc(zveps_done, 1)
                    v.wait_ge(zrstd_done, 2 * b + gr + 1)
                    for i in range(4):
                        v.tensor_scalar(z[:, gr, i, :], z[:, gr, i, :], zmv[:, i, 0:1], zrstd[:, i:i + 1],
                                        ALU.subtract, ALU.mult).then_inc(zn_done, 1)
                k = at["bias",]
                R.wait_filled(v, b, k)
                v.tensor_tensor(acc[:, :, :], R.bank(k)[:, 0:QT * D].rearrange("p (t d) -> p t d", t=QT), nrm.xn[:, :, :],
                                ALU.add).then_inc(R.free(k), 1)
                R.wait_emptied(v, b, k)
                if ahead:
                    nrm.vector(v, b + 1)
                    nrm2.vector(v, b + 1)
                for n, e in enumerate(DOWN):
                    k = at["down", e]
                    R.wait_filled(v, b, k)
                    for t in range(QT):
                        if n > 0:
                            v.wait_ge(acc_done, QT * (E * b + n - 1) + t + 1)
                        v.scalar_tensor_tensor(acc[:, t, :], R.bank(k)[:, t * D:t * D + D], wt[:, t, e:e + 1], acc[:, t, :],
                                               ALU.mult, ALU.add).then_inc(acc_done, 1)
                    v.wait_ge(acc_done, QT * (E * b + n + 1))
                    v.sem_inc(R.free(k), 1)
                v.tensor_tensor(x[:, bass.ds(QT * b, QT), :], x[:, bass.ds(QT * b, QT), :], acc[:, :, :], ALU.add)\
                    .then_inc(x_done, 1)

            with v.Fori(0, B - 1) as b:
                batch(b, True)
            batch(B - 1, False)
    st.close()


def heads_on(rows, head_rows, width):
    return (np.arange(rows)[:, None] // head_rows == np.arange(width)[None, :]).astype(np.float32)


def turned(wt, d):
    n = wt.shape[1] // d
    a = wt.reshape(wt.shape[0], n, 2, d // 2)
    return np.ascontiguousarray(a[:, :, ::-1, :]).reshape(wt.shape[0], n * d)


def rope_tables(d):
    half = d // 2
    inv = (1.0 / 10000.0 ** (np.arange(half, dtype=np.float32) / half)).astype(np.float32)
    ang = np.arange(S, dtype=np.float32)[None, :] * inv[:, None]
    f = np.arange(128) % d
    sign = np.where(f < half, -1.0, 1.0)[:, None]
    return np.cos(ang)[f % half].astype(np.float32), (np.sin(ang)[f % half] * sign).astype(np.float32)


def spread_o(wo, d, groups):
    mw = 128 * groups // H
    a = np.zeros((128, groups, D), np.float32)
    for h in range(H):
        gr, j = divmod(h, H // groups)
        a[mw * j:mw * j + d, gr, :] = wo[h * d:(h + 1) * d]
    return a.reshape(128, groups * D)


def pack(parts):
    at, n = {}, 0
    for key, a in parts.items():
        at[key] = (n, a.shape[1])
        n += a.shape[1]
    return np.concatenate([np.asarray(a, np.float32) for a in parts.values()], 1), at


def pack_L3_attn(i):
    wk = np.tile(i["L3_attn_wk"], (1, 4))
    wv = np.tile(i["L3_attn_wv"], (1, 4))
    cos, sin = rope_tables(8)
    return pack({"q": i["L3_attn_wq"], "qr": turned(i["L3_attn_wq"], 8), "k": wk, "kr": turned(wk, 8), "v": wv,
                 "o": spread_o(i["L3_attn_wo"], 8, 4), "cos": cos, "sin": sin, "kmask": heads_on(128, 8, 16)})


def pack_L0_attn(i):
    h, r = np.arange(256) // 16, np.arange(256) % 16
    rows = 8 * h + r % 8
    inv = (10000.0 ** -(np.arange(8, dtype=np.float32) / 8)).astype(np.float32)
    ang = (np.arange(S, dtype=np.float32)[None, :] * inv[:, None]).astype(np.float32)[r[:128] % 8]
    is_cos = (r[:128] < 8)[:, None]
    return pack({"q": i["L0_attn_wq"].T[:, rows], "k": i["L0_attn_wk"].T[:, rows], "v": i["L0_attn_wv"].T,
                 "o": spread_o(i["L0_attn_wo"].T, 8, 4), "cos": np.where(is_cos, np.cos(ang), np.sin(ang)),
                 "turn": np.where(is_cos, -np.sin(ang), np.cos(ang)),
                 "bias": i["L0_attn_pope_bias"].reshape(-1)[rows].reshape(2, 128).T, "kmask": heads_on(128, 16, 8)})


def pack_L2_attn(i):
    wk = np.concatenate([i["L2_attn_Wk"].T[:, 64 * g:64 * g + 64] for g in (0, 0, 1, 1, 2, 2, 3, 3)], 1)
    cos, sin = rope_tables(64)
    return pack({"q": i["L2_attn_Wq"].T, "qr": turned(i["L2_attn_Wq"].T, 64), "k": wk, "kr": turned(wk, 64),
                 "v": i["L2_attn_Wv"].T, "g": np.concatenate([i["L2_attn_Wg_slc"].T, i["L2_attn_Wg_swa"].T], 1),
                 "o": spread_o(i["L2_attn_Wo"].T, 64, 8), "cos": cos, "sin": sin, "kmask": heads_on(128, 64, 2)})


def pairs_o(wo):
    a = np.zeros((128, 2, D), np.float32)
    for m in range(H // 2):
        a[32 * (m % 4):32 * (m % 4) + 16, m // 4, :] = wo[16 * m:16 * m + 16]
    return a.reshape(128, 2 * D)


def rows_of(a):
    return np.broadcast_to(a[None, :], (128, a.shape[0]))


def below(a):
    return np.concatenate([a, np.zeros((128 - a.shape[0], a.shape[1]), np.float32)], 0)


def pack_L1_xattn(i):
    kv, kvb = i["L1_xattn_kv_w"].T, i["L1_xattn_kv_b"]
    return pack({"q": i["L1_xattn_q_w"].T, "qb": i["L1_xattn_q_b"][:, None], "k": kv[:, :D], "kb": kvb[:D, None],
                 "v": kv[:, D:], "vb": rows_of(kvb[D:]), "o": pairs_o(i["L1_xattn_proj_w"].T),
                 "ob": rows_of(i["L1_xattn_proj_b"]), "kmask": heads_on(128, 8, 16)})


def pack_L2_xattn(i):
    p = "L2_xattn_"
    return pack({"q": i[p + "Wq"].T, "qb": i[p + "bq"][:, None], "k": i[p + "Wk"].T, "kb": i[p + "bk"][:, None],
                 "v": i[p + "Wv"].T, "vb": rows_of(i[p + "bv"]), "o": pairs_o(i[p + "Wo"].T),
                 "ob": rows_of(i[p + "bo"]), "kmask": heads_on(128, 8, 16),
                 "w1": rows_of(i[p + "w1"].T.reshape(-1)), "b1": below(i[p + "b1"][:, None]),
                 "w2": below(i[p + "w2"].T), "b2": below(i[p + "b2"][:, None]),
                 "w3": below(np.broadcast_to(i[p + "w3"].T, (64, 128))), "b3": rows_of(i[p + "b3"])})


def pack_L0_xattn(i):
    p = "L0_xattn_"
    a, at = pack({"q": i[p + "W_q"].T, "qb": i[p + "b_q"][:, None], "k": i[p + "W_k"].T, "kb": i[p + "b_k"][:, None],
                  "v": i[p + "W_v"].T, "vb": rows_of(i[p + "b_v"])})
    return {"L0_xattn": a, "mask_L0": i["mask_SxS2_bk1"]}, at


def pack_L1_attn(i):
    p = "L1_attn_"
    return pack({"A": i[p + "A_log"], "B": i[p + "B_p"], "C": i[p + "C_p"], "D": i[p + "D_p"][:, None],
                 "dt": i[p + "W_dt"].T, "bdt": i[p + "b_dt"][:, None]})


def chunks(a):
    n = a.shape[0] // 128
    return a.reshape(n, 128, -1).transpose(1, 0, 2).reshape(128, -1)


def pack_L1_ffn(i):
    return pack({"gate": i["L1_ffn_w_gate"].T, "up": i["L1_ffn_w_up"].T, "down": chunks(i["L1_ffn_w_down"].T)})


def pack_L2_ffn(i):
    p = "L2_ffn_"
    before = np.concatenate([np.arange(S)[None, :] < 128 * t + np.arange(128)[:, None] for t in range(QT)], 1)
    return pack({"gate": np.broadcast_to(i[p + "Wg"], (128, 128)), "q": i[p + "Wq"], "k": i[p + "Wk"],
                 "v": i[p + "Wv"], "o": spread_o(i[p + "Wo"], 8, 4), "kmask": heads_on(128, 8, 16),
                 "before": before, "iota": rows_of(np.arange(S // 2))})


def pack_L3_xattn(i):
    p = "L3_xattn_"
    return pack({"q": i[p + "Wq"], "k": i[p + "Wkv"][:, :1024], "v": i[p + "Wkv"][:, 1024:], "o": chunks(i[p + "Wo"]),
                 "ob": rows_of(i[p + "bo"]), "g1": i[p + "g1"][:, None], "b1": i[p + "b1"][:, None],
                 "g2": i[p + "g2"][:, None], "b2": i[p + "b2"][:, None], "kmask": heads_on(128, 64, 2)})


def pack_L3_ffn(i):
    a, at = pack({"r": i["L3_ffn_Wr"], "expert": rows_of(np.tile(np.arange(8), NT)),
                  "below": np.arange(128)[:, None] < np.arange(128)[None, :]})
    return {"L3_ffn": a, "L3_ffn_W1": i["L3_ffn_W1"], "L3_ffn_W2": i["L3_ffn_W2"]}, at


def pack_L0_ffn(i):
    p = "L0_ffn_"
    E, F = 8, 512
    of = lambda a: np.concatenate(list(a), 1)
    cols = lambda a: a.reshape(-1, 128).T
    return pack({
        "up": of(i[p + "up_W"]), "down": of(chunks(a) for a in i[p + "down_W"]),
        "spec0": of(chunks(a) for a in i[p + "spec0_W"]), "spec1a": of(chunks(a) for a in i[p + "spec1a_W"]),
        "spec1b": of(chunks(a) for a in i[p + "spec1b_W"]), "spec2": of(chunks(a) for a in i[p + "spec2_W"]),
        "up_b": cols(i[p + "up_b"]), "spec1a_b": cols(i[p + "spec1a_b"]), "spec2_b": cols(i[p + "spec2_b"]),
        "zbias0": rows_of(i[p + "spec0_b"].reshape(-1)), "zbias1": rows_of(i[p + "spec1b_b"].reshape(-1)),
        "ln0_g": rows_of(i[p + "ln0_g"].reshape(-1)), "ln0_b": rows_of(i[p + "ln0_b"].reshape(-1)),
        "ln1_g": rows_of(i[p + "ln1_g"].reshape(-1)), "ln1_b": rows_of(i[p + "ln1_b"].reshape(-1)),
        "ln_g": i[p + "ln_g"][:, None], "ln_b": i[p + "ln_b"][:, None], "router": i[p + "router_w"],
        "down_b": below(i[p + "down_b"]),
        "earlier": rows_of((np.arange(E)[None, :] < np.arange(E)[:, None]).reshape(-1))})


SPEC_L3 = dict(d=8, groups=4, causal=True, qchunks=1, kchunks=1, heads_of_kchunk=16, kvheads=16, gates=0, rope=True)
SPEC_L0 = dict(d=8, groups=4, causal=False, qchunks=2, kchunks=2, heads_of_kchunk=8, kvheads=16, gates=0, rope=False)
SPEC_L2 = dict(d=64, groups=8, causal=True, qchunks=8, kchunks=4, heads_of_kchunk=2, kvheads=4, gates=1, rope=True)
STAGES = {
    "L0_attn": (lambda nc, g, w: self_attention(nc, g, "l0a", w, SPEC_L0), pack_L0_attn),
    "L0_xattn": (L0_xattn, pack_L0_xattn),
    "L0_ffn": (L0_ffn, pack_L0_ffn),
    "L1_attn": (L1_attn, pack_L1_attn),
    "L1_xattn": (lambda nc, g, w: cross_attention(nc, g, "l1x", w, "plain"), pack_L1_xattn),
    "L1_ffn": (L1_ffn, pack_L1_ffn),
    "L2_attn": (lambda nc, g, w: self_attention(nc, g, "l2a", w, SPEC_L2), pack_L2_attn),
    "L2_xattn": (L2_xattn, pack_L2_xattn),
    "L2_ffn": (L2_ffn, pack_L2_ffn),
    "L3_attn": (lambda nc, g, w: self_attention(nc, g, "l3a", w, SPEC_L3), pack_L3_attn),
    "L3_xattn": (L3_xattn, pack_L3_xattn),
    "L3_ffn": (L3_ffn, pack_L3_ffn),
}
TOGETHER = (("L0_attn",), ("L0_xattn", "L0_ffn"),
            ("L1_attn", "L1_xattn", "L1_ffn", "L2_attn", "L2_xattn", "L2_ffn", "L3_attn", "L3_xattn", "L3_ffn"))


def program(nc, stages, dram, ats, x_in, out):
    with ExitStack() as ctx:
        g = {}

        def kept(name, shape, dt=F32):
            g[name] = ctx.enter_context(nc.sbuf_tensor(f"sb_{name}", shape, dt))
            return g[name]

        x = kept("x", [128, NT + QT * MAX_LANES, D])
        ident = kept("ident", [128, 128])
        identb = kept("identb", [128, 128], BF16)
        onesb = kept("onesb", [128, 128], BF16)
        tri = kept("tri", [128, 128], BF16)
        pad = kept("pad", [128, B, SC], BF16)
        hide = kept("hide", [128, B, SC], BF16)
        mask8 = kept("mask8", [128, QT, SC], U8)
        ctxT = kept("ctxT", [128, B, SC])
        minus_mean = kept("minus_mean", [128, 1])
        st = Stage(nc, "in")
        trif = st.sb("trif", [128, 128])
        raw = st.sb("raw", [128, B * SC // 128, D])
        masks = st.sb("masks", [128, 2, B, SC], U8)
        ps = st.ps("ps")
        mask_in = st.sem("mask_in")
        landed, cast, turned_in, out_of = st.sem("landed"), st.sem("cast"), st.sem("turned"), st.sem("out_of")
        with nc.Block("in_block") as block:
            @block.sync
            def _(sp):
                sp.dma_start(x[:, 0:NT, :], x_in.rearrange("(t p) d -> p t d", p=128)).then_inc(landed, 16)
                sp.dma_start(ident[:, :], dram["ident"]).then_inc(landed, 16)
                sp.dma_start(trif[:, :], dram["tri"]).then_inc(landed, 16)
                sp.dma_start(raw[:, :, :], dram["ctx"].rearrange("(t p) d -> p t d", p=128)).then_inc(landed, 16)
                if "mask_L0" in dram:
                    sp.dma_start(mask8[:, :, :], dram["mask_L0"].rearrange("(t p) k -> p t k", p=128))\
                        .then_inc(mask_in, 16)
                for n, key in enumerate(("mask_pad", "mask_keep")):
                    sp.dma_start(masks[:, n, :, :], dram[key].partition_broadcast(128)).then_inc(landed, 16)

            @block.tensor
            def _(pe):
                pe.wait_ge(landed, 96)
                for t in range(B * SC // 128):
                    mm = pe.transpose(ps[:, t * 128:t * 128 + 128], raw[:, t, :], ident[:, :])
                mm.then_inc(turned_in, 1)

            @block.vector
            def _(v):
                if "mask_L0" in dram:
                    v.wait_ge(mask_in, 16)
                v.memset(x[:, NT:, :], 0.0)
                v.memset(onesb[:, :], 1.0).then_inc(cast, 1)
                v.memset(minus_mean[:, :], -1.0 / SC).then_inc(cast, 1)
                v.wait_ge(landed, 96)
                v.tensor_copy(identb[:, :], ident[:, :]).then_inc(cast, 1)
                v.tensor_copy(tri[:, :], trif[:, :]).then_inc(cast, 1)
                v.tensor_scalar(pad[:, :, :], masks[:, 0, :, :], MASKED, None, ALU.mult).then_inc(cast, 1)
                v.tensor_scalar(hide[:, :, :], masks[:, 1, :, :], -MASKED, MASKED, ALU.mult, ALU.add)\
                    .then_inc(cast, 1)
                v.wait_ge(turned_in, 1)
                v.tensor_copy(ctxT[:, :, :].rearrange("p b k -> p (b k)"), ps[:, :]).then_inc(out_of, 1)
        st.close()
        g["dram"] = dram
        for group in TOGETHER:
            group = [s for s in group if s in stages]
            if not group:
                continue
            weights = {s: Weights(nc, s, dram[s], ats[s]) for s in reversed(group)}
            with nc.Block(f"fetch_{group[0]}") as block:
                @block.sync
                def _(sp):
                    for s in group:
                        weights[s].fetch(sp)
            for s in group:
                STAGES[s][0](nc, g, weights[s])
                weights[s].close()
        st = Stage(nc, "out")
        stored = st.sem("stored")
        with nc.Block("out_block") as block:
            @block.sync
            def _(sp):
                sp.dma_start(out.rearrange("(t p) d -> p t d", p=128), g["x"][:, 0:NT, :]).then_inc(stored, 16)
                sp.wait_ge(stored, 16)
        st.close()


def laid_out(inputs, stages):
    arrays = {
        "ident": np.eye(128, dtype=np.float32),
        "tri": np.where(np.arange(128)[None, :] > np.arange(128)[:, None], MASKED, 0).astype(np.float32),
        "ctx": np.ascontiguousarray(inputs["ctx_1024"].reshape(B * SC, D)),
        "mask_pad": inputs["mask_BxS2_bk0"],
        "mask_keep": inputs["mask_BxS2_bf1"],
        "x_in": np.ascontiguousarray(inputs["x"].reshape(B * S, D)),
    }
    ats = {}
    for s in stages:
        a, ats[s] = STAGES[s][1](inputs)
        arrays.update(a if isinstance(a, dict) else {s: a})
    return arrays, ats


def build(nc, arrays, ats, stages):
    dram = {n: nc.dram_tensor(n, list(a.shape), mybir.dt.from_np(a.dtype), kind="ExternalInput").ap()
            for n, a in arrays.items()}
    out = nc.dram_tensor("out", [B * S, D], F32, kind="ExternalOutput").ap()
    program(nc, stages, dram, ats, dram["x_in"], out)


def kernel(**inputs):
    import concourse.bacc as bacc
    from concourse.bass_utils import run_bass_kernel_spmd

    arrays, ats = laid_out({k: np.asarray(v) for k, v in inputs.items()}, list(STAGES))
    nc = bacc.Bacc("TRN2", target_bir_lowering=False, num_devices=1)
    build(nc, arrays, ats, list(STAGES))
    r = run_bass_kernel_spmd(nc, [arrays], core_ids=[0])
    return r.results[0]["out"].reshape(B, S, D)
```

```python
from contextlib import ExitStack
from itertools import zip_longest

import numpy as np

import concourse.bass as bass
from concourse import mybir

F32 = mybir.dt.float32
BF16 = mybir.dt.bfloat16
U8 = mybir.dt.uint8
U32 = mybir.dt.uint32
ALU = mybir.AluOpType
ACT = mybir.ActivationFunctionType
AX = mybir.AxisListType

B, S, D, SC = 8, 256, 128, 64
QT = S // 128
NT = B * QT
H = 16
EPS = 1e-5
MAX_LANES = 4
MASKED = -1e30


class Weights:

    def __init__(self, nc, name, dram, at):
        self.nc, self.dram, self.at = nc, dram, at
        self.stack = ExitStack()
        self.sb = self.stack.enter_context(nc.sbuf_tensor(f"{name}_weights", [128, dram.shape[1]], F32))
        self.loaded = nc.alloc_semaphore(f"{name}_weights_loaded")

    def of(self, key):
        a, n = self.at[key]
        return self.sb[:, a:a + n]

    def fetch(self, sp):
        sp.dma_start(self.sb[:, :], self.dram).then_inc(self.loaded, 16)

    def close(self):
        self.stack.close()
        self.nc.clear_and_free_semaphores([self.loaded])
        self.nc.all_engine_barrier()


class Stage:

    def __init__(self, nc, name):
        self.nc, self.name = nc, name
        self.stack = ExitStack()
        self.sems = []

    def sb(self, name, shape, dt=F32):
        return self.stack.enter_context(self.nc.sbuf_tensor(f"{self.name}_{name}", shape, dt))

    def ps(self, name, shape=(128, 512), dt=F32):
        return self.stack.enter_context(self.nc.psum_tensor(f"{self.name}_{name}", list(shape), dt))

    def sem(self, name):
        s = self.nc.alloc_semaphore(f"{self.name}_{name}")
        self.sems.append(s)
        return s

    def close(self):
        self.stack.close()
        self.nc.clear_and_free_semaphores(self.sems)
        self.nc.all_engine_barrier()


class Ring:

    def __init__(self, st, name, banks, uses):
        self.banks = [st.ps(f"{name}{i}") for i in range(banks)]
        self.filled = [st.sem(f"{name}{i}_filled") for i in range(banks)]
        self.freed = [st.sem(f"{name}{i}_freed") for i in range(banks)]
        self.n = banks
        self.per = [(uses - i + banks - 1) // banks for i in range(banks)]

    def bank(self, k):
        return self.banks[k % self.n]

    def full(self, k):
        return self.filled[k % self.n]

    def free(self, k):
        return self.freed[k % self.n]

    def credit(self, eng):
        for f in self.freed:
            eng.sem_inc(f, 1)

    def wait_free(self, eng, b, k):
        eng.wait_ge(self.free(k), b * self.per[k % self.n] + k // self.n + 1)

    def wait_filled(self, eng, b, k):
        eng.wait_ge(self.full(k), b * self.per[k % self.n] + k // self.n + 1)

    def wait_emptied(self, eng, b, k):
        eng.wait_ge(self.free(k), b * self.per[k % self.n] + k // self.n + 2)


    def wait_for(self, eng, b, emptied, k):
        last = {}
        for j in [*emptied, k - self.n]:
            last[j % self.n] = max(last.get(j % self.n, j), j)
        for j in last.values():
            eng.wait_ge(self.free(j), b * self.per[j % self.n] + j // self.n + 2)


class Lane:

    def __init__(self, st, lane=0, lanes=1, tag=None):
        tag = f"lane{lane}_" if tag is None else tag
        self.nc, self.lane, self.lanes = st.nc, lane, lanes
        self.sb = lambda name, *a: st.sb(tag + name, *a)
        self.ps = lambda name, *a: st.ps(tag + name, *a)
        self.sem = lambda name: st.sem(tag + name)

    def batch(self, i):
        return self.lanes * i + self.lane


def beside(*programs):
    for _ in zip_longest(*programs):
        yield


def in_turn(*programs):
    for _ in zip_longest(*programs):
        pass


class Norm:

    def __init__(self, st, x, of=None):
        self.x, self.nc, self.of = x, st.nc, of
        self.batch = st.batch if isinstance(st, Lane) else lambda i: i
        if of:
            st = Lane(st, tag="again_")
        self.stats = st.sb("stats", [128, QT, 6])
        self.mv = st.sb("mv", [128, QT, 2])
        self.veps = st.sb("veps", [128, QT])
        self.rstd = st.sb("rstd", [128, QT])
        self.neghalf = st.sb("neghalf", [128, QT])
        self.xn = st.sb("xn", [128, QT, D])
        self.mv_done = st.sem("mv_done")
        self.veps_done = st.sem("veps_done")
        self.rstd_done = st.sem("rstd_done")
        self.xn_done = st.sem("xn_done")
        self.half_set = st.sem("half_set")

    def pool_setup(self, eng):
        eng.memset(self.neghalf[:, :], -0.5).then_inc(self.half_set, 1)
        eng.wait_ge(self.half_set, 1)

    def source(self, i, t):
        return self.of.xn[:, t, :] if self.of else self.x[:, QT * self.batch(i) + t, :]

    def take_moments(self, eng, i):
        if self.of:
            self.of.wait(eng, i)
        for t in range(QT):
            eng.bn_stats(self.stats[:, t, :], self.source(i, t))
        eng.drain()
        for t in range(QT):
            eng.bn_aggr(self.mv[:, t, :], self.stats[:, t, :]).then_inc(self.mv_done, 1)
        eng.wait_ge(self.mv_done, QT * i + QT)
        eng.tensor_scalar(self.veps[:, :], self.mv[:, :, 1], EPS, None, ALU.add).then_inc(self.veps_done, 1)

    def norm_rows(self, eng, i):
        eng.wait_ge(self.rstd_done, i + 1)
        for t in range(QT):
            eng.tensor_scalar(self.xn[:, t, :], self.source(i, t), self.mv[:, t, 0:1],
                              self.rstd[:, t:t + 1], ALU.subtract, ALU.mult).then_inc(self.xn_done, 1)

    def vector(self, eng, i):
        self.take_moments(eng, i)
        self.norm_rows(eng, i)

    def pool(self, eng, i):
        eng.wait_ge(self.veps_done, i + 1)
        eng.tensor_tensor(self.rstd[:, :], self.veps[:, :], self.neghalf[:, :], ALU.pow).then_inc(self.rstd_done, 1)

    def wait(self, eng, i):
        eng.wait_ge(self.xn_done, QT * i + QT)


class SelfLane:
    LAG, PR = 2, 3
    SR = 2

    def __init__(self, st, lane, lanes, g, w, ktab, spec):
        self.g, self.w, self.ktab, self.spec = g, w, ktab, spec
        self.d, self.NG, self.causal = spec["d"], spec["groups"], spec["causal"]
        self.nq, self.nk, self.kreps = spec["qchunks"], spec["kchunks"], spec["heads_of_kchunk"]
        self.gates, self.rope = spec["gates"], spec["rope"]
        self.NP = H // 2
        self.NI = self.NP * QT
        self.per_group = self.NP // self.NG
        self.MW = 128 * self.NG // H
        self.dense = self.d == 8
        self.nv = spec["kvheads"] * self.d
        self.NB = 2 * self.per_group
        self.CH = self.nq + self.nk
        self.v_uses = QT if self.nv > 128 else 1
        self.V_USE = 1 + self.CH
        self.G_USE = self.V_USE + self.v_uses
        self.SCORES = self.G_USE + self.gates
        self.OUT = self.NI + self.NG
        self.STEPS = self.NI + self.LAG + 2
        self.share = self.nk * self.kreps == H
        self.act_tile = 1 if self.causal else 0
        st = Lane(st, lane, lanes)
        self.batch = st.batch
        self.R = Ring(st, "r", self.SR, self.SCORES + self.NI)
        self.T = Ring(st, "t", 2, self.OUT + 1)
        self.nrm = Norm(st, g["x"])
        self.xnT = st.sb("xnT", [128, S])
        self.q_sb = st.sb("q", [128, self.nq, S])
        self.k_sb = st.sb("k", [128, self.nk, S])
        self.tmp = st.sb("tmp", [128, 2 if self.rope else self.CH, 2, S])
        self.kbd = st.sb("kbd", [128, self.nk * self.kreps, S])
        self.v_sb = st.sb("v", [128, QT, self.NG, 5 * self.MW] if self.dense else
                          [128, QT, self.nv // self.d, self.MW])
        self.P = [st.sb(f"p{i}", [128, 2, S]) for i in range(self.PR)]
        self.PT = [st.sb(f"pt{i}", [128, 2, QT, S]) for i in range(self.NB)]
        self.OT = st.sb("ot", [128, 1 if self.dense else self.NG, S])
        self.nmax = st.sb("nmax", [128, self.PR, 2])
        self.sums = st.sb("sums", [128, self.PR, 2])
        self.rec = st.sb("rec", [128, self.PR, 2])
        self.weight = st.sb("weight", [128, self.PR, 2])
        self.gate = st.sb("gate", [128, QT, 2, H])
        self.gsum = st.sb("gsum", [128, QT, H])
        self.parts, self.joined = st.sem("parts"), st.sem("joined")
        self.soft_abs, self.soft_exp, self.soft_ln = st.sem("soft_abs"), st.sem("soft_exp"), st.sem("soft_ln")
        self.soft_sum = st.sem("soft_sum")
        self.kbd_pool, self.kbd_vector, self.v_set = st.sem("kbd_pool"), st.sem("kbd_vector"), st.sem("v_set")
        self.kbd_scalar = st.sem("kbd_scalar")
        self.max_done = st.sem("max_done")
        self.rec_done, self.weight_done, self.p_done = st.sem("rec_done"), st.sem("weight_done"), st.sem("p_done")
        self.gate_step = st.sem("gate_step")

    def keys_of(self, qt):
        return 128 * (qt + 1) if self.causal else S

    def khead(self, h):
        return h if self.nk * self.kreps == H else 2 * (h // 4) + h % 2

    def chunk(self, k):
        return self.q_sb[:, k - 1, :] if k <= self.nq else self.k_sb[:, k - 1 - self.nq, :]

    def item_use(self, j):
        return j + j // (QT * self.per_group)

    def group_use(self, gr):
        return self.item_use((gr + 1) * QT * self.per_group - 1) + 1

    def ended_group(self, j):
        n = QT * self.per_group
        return j // n if 0 <= j < self.NI and j % n == n - 1 else None

    def sync_setup(self, sp):
        self.R.credit(sp)
        self.T.credit(sp)

    def pool_setup(self, pool):
        self.nrm.pool_setup(pool)
        pool.memset(self.v_sb[:, :, :, :], 0.0).then_inc(self.v_set, 1)

    def pool_start(self, pool, b):
        yield
        for k in range(1, self.CH + 1):
            if self.rope:
                part = self.tmp[:, (k - 1) % 2, :, :]
                pool.wait_ge(self.parts, b * self.CH + k)
                pool.tensor_tensor(self.chunk(k), part[:, 0, :], part[:, 1, :], ALU.add).then_inc(self.joined, 1)
                if k > self.nq and self.share:
                    self.lone_keys(pool, b, k - 1 - self.nq)
            yield
        yield
        if not self.rope:
            yield
            for c in range(self.nk):
                self.lone_keys(pool, b, c)
            yield

    def pool_items(self, pool, b, first, end):
        for s in range(first, end):
            i = s - 1
            if 0 <= i < self.NI:
                n = self.keys_of(i % QT)
                pool.wait_ge(self.weight_done if self.gates else self.rec_done, b * self.NI + i + 1)
                by = self.weight if self.gates else self.rec
                P = self.P[i % self.PR]
                pool.tensor_tensor(P[:, :, 0:n], P[:, :, 0:n],
                                   by[:, i % self.PR, :].unsqueeze(2).to_broadcast([128, 2, n]),
                                   ALU.mult).then_inc(self.p_done, 1)
            if s == self.NI - 5:
                self.nrm.pool(pool, b + 1)
            yield

    def lone_keys(self, pool, b, c):
        kreps = self.kreps
        pool.wait_ge(self.joined, b * self.CH + self.nq + c + 1)
        for j in range(0, kreps, 2):
            if (c * kreps + j) // 2 % 3 != 2:
                continue
            pool.tensor_tensor(self.kbd[:, c * kreps + j:c * kreps + j + 2, :],
                               self.k_sb[:, c, :].unsqueeze(1).to_broadcast([128, 2, S]),
                               self.w("kmask")[:, j:j + 2].unsqueeze(2).to_broadcast([128, 2, S]),
                               ALU.mult).then_inc(self.kbd_pool, 1)

    def lone_keys_vector(self, v, b, c):
        kreps = self.kreps
        v.wait_ge(self.joined, b * self.CH + self.nq + c + 1)
        for j in range(kreps):
            h = c * kreps + j
            if h // 2 % 3 == 0:
                one = v.tensor_scalar(self.kbd[:, h, :], self.k_sb[:, c, :], self.w("kmask")[:, j:j + 1], None, ALU.mult)
                if h % 2:
                    one.then_inc(self.kbd_vector, 1)

    def lone_keys_scalar(self, act, b, c):
        kreps = self.kreps
        act.wait_ge(self.joined, b * self.CH + self.nq + c + 1)
        for j in range(kreps):
            h = c * kreps + j
            if not self.share or h // 2 % 3 == 1:
                one = act.activation(self.kbd[:, h, :], self.k_sb[:, c, :], ACT.Identity,
                                     scale=self.w("kmask")[:, j:j + 1])
                if h % 2:
                    one.then_inc(self.kbd_scalar, 1)

    def tensor_start(self, pe, b):
        R, w, g, nv, xnT = self.R, self.w, self.g, self.nv, self.xnT
        self.nrm.wait(pe, b)
        R.wait_free(pe, b, 0)
        for t in range(QT):
            mm = pe.transpose(R.bank(0)[:, t * 128:t * 128 + 128], self.nrm.xn[:, t, :], g["ident"][:, :])
        mm.then_inc(R.full(0), 1)
        yield
        for k in range(1, self.CH + 1):
            if k == 1:
                R.wait_emptied(pe, b, 0)
            key, c = ("q", k - 1) if k <= self.nq else ("k", k - 1 - self.nq)
            R.wait_free(pe, b, k)
            for r in range(2 if self.rope else 1):
                mm = pe.matmul(R.bank(k)[:, r * S:(r + 1) * S], w(key + "r" * r)[:, c * 128:c * 128 + 128],
                               xnT[:, :], start=True, stop=True)
            mm.then_inc(R.full(k), 1)
            yield
        k = self.V_USE
        for t0 in range(0, QT, QT // self.v_uses):
            R.wait_free(pe, b, k)
            for t in range(t0, t0 + QT // self.v_uses):
                mm = pe.matmul(R.bank(k)[:, (t - t0) * nv:(t - t0 + 1) * nv],
                               xnT[:, t * 128:t * 128 + 128], w("v"), start=True, stop=True)
            mm.then_inc(R.full(k), 1)
            k += 1
        if self.gates:
            R.wait_free(pe, b, k)
            for t in range(QT):
                mm = pe.matmul(R.bank(k)[:, t * 2 * H:(t + 1) * 2 * H], xnT[:, t * 128:t * 128 + 128],
                               w("g"), start=True, stop=True)
            mm.then_inc(R.full(k), 1)
        yield
        if not self.rope:
            yield
            yield

    def tensor_items(self, pe, b, first, end):
        R, T, g, w, NI, LAG = self.R, self.T, self.g, self.w, self.NI, self.LAG
        for i in range(first, end):
            if i == 0:
                pe.wait_ge(self.joined, b * self.CH + self.nq)
            if i < NI:
                u, qt = divmod(i, QT)
                n = self.keys_of(qt)
                kh = self.khead(2 * u)
                if self.share:
                    by, turn = (self.kbd_vector, self.kbd_scalar, self.kbd_pool), kh // 2 % 3
                    pe.wait_ge(by[turn], b * ((self.NP + 2 - turn) // 3) + kh // 6 + 1)
                else:
                    pe.wait_ge(self.kbd_scalar, b * (self.nk * self.kreps // 2) + kh // 2 + 1)
                k = self.SCORES + i
                R.wait_free(pe, b, k)
                so = R.bank(k)[:, :].rearrange("p (j k) -> p j k", j=2)[:, :, 0:n]
                mm = pe.matmul(so, self.q_sb[:, u * self.nq // self.NP, qt * 128:qt * 128 + 128],
                               self.kbd[:, kh:kh + 2, 0:n], start=True, stop=not self.causal)
                if self.causal:
                    mm = pe.matmul(so[:, :, n - 128:n], g["identb"][:, :],
                                   g["tri"][:, :].unsqueeze(1).to_broadcast([128, 2, 128]),
                                   start=False, stop=True)
                mm.then_inc(R.full(k), 1)
            gr = self.ended_group(i - LAG - 1)
            if gr is not None:
                self.products(pe, b, gr)
            j = i - LAG
            if 0 <= j < NI:
                nb = self.keys_of(j % QT) // 128
                k = self.item_use(j)
                pe.wait_ge(self.p_done, b * NI + j + 1)
                T.wait_free(pe, b, k)
                for hh in range(2):
                    for kt in range(nb):
                        at = (hh * nb + kt) * 128
                        mm = pe.transpose(T.bank(k)[:, at:at + 128],
                                          self.P[j % self.PR][:, hh, kt * 128:kt * 128 + 128], g["ident"][:, :])
                mm.then_inc(T.full(k), 1)
            if i == self.STEPS - 1:
                k = self.OUT
                T.wait_emptied(pe, b, self.group_use(self.NG - 1))
                T.wait_free(pe, b, k)
                for t in range(QT):
                    last = self.OT.shape[1] - 1
                    for c in range(last + 1):
                        mm = pe.matmul(T.bank(k)[:, t * 128:t * 128 + 128], self.OT[:, c, t * 128:t * 128 + 128],
                                       w("o")[:, c * 128:c * 128 + 128], start=(c == 0), stop=(c == last))
                mm.then_inc(T.full(k), 1)
            yield

    def products(self, pe, b, gr):
        T, MW, k = self.T, self.MW, self.group_use(gr)
        T.wait_emptied(pe, b, k - 2)
        T.wait_emptied(pe, b, k - 1)
        T.wait_free(pe, b, k)
        for u in range(gr * self.per_group, (gr + 1) * self.per_group):
            for hh in range(2):
                h = 2 * u + hh
                j = h % (128 // MW)
                row = MW * gr if self.dense else MW * j
                for kt in range(QT):
                    q0 = 128 * kt if self.causal else 0
                    values = self.v_sb[:, kt, gr, MW * j:MW * j + MW] if self.dense else \
                        self.v_sb[:, kt, h * (self.nv // self.d) // H, :]
                    mm = pe.matmul(T.bank(k)[row:row + MW, q0:S], values, self.PT[u % self.NB][:, hh, kt, q0:S],
                                   start=(kt == 0 and not (self.dense and j)),
                                   stop=(kt == QT - 1 and not (self.dense and j < 3)), tile_position=(0, row))
        mm.then_inc(T.full(k), 1)

    def pt_copy(self, copy, eng, b, j):
        T = self.T
        u, qt = divmod(j, QT)
        nb = self.keys_of(qt) // 128
        k = self.item_use(j)
        T.wait_filled(eng, b, k)
        gr = u // self.per_group
        if gr >= 2:
            T.wait_filled(eng, b, self.group_use(gr - 2))
        copy(self.PT[u % self.NB][:, :, 0:nb, qt * 128:qt * 128 + 128],
             T.bank(k)[:, 0:2 * nb * 128].rearrange("p (j t q) -> p j t q", j=2, t=nb)).then_inc(T.free(k), 1)

    def ot_copy(self, copy, eng, b, gr):
        k = self.group_use(gr)
        self.T.wait_filled(eng, b, k)
        r0, r1, c = (self.MW * gr, self.MW * gr + self.MW, 0) if self.dense else (0, 128, gr)
        copy(self.OT[r0:r1, c, :], self.T.bank(k)[r0:r1, 0:S]).then_inc(self.T.free(k), 1)

    def soft_exponential(self, act, b, k):
        a = self.tmp[:, k - 1, 0, :]
        act.wait_ge(self.soft_abs, b * self.CH + k)
        act.activation(a, a, ACT.Exp, scale=-1.0).then_inc(self.soft_exp, 1)

    def scalar_start(self, act, b):
        R, CH = self.R, self.CH
        R.wait_filled(act, b, 0)
        act.activation(self.xnT[:, :], R.bank(0)[:, 0:S], ACT.Copy).then_inc(R.free(0), 1)
        yield
        for k in range(1, CH + 1):
            if not self.rope:
                R.wait_filled(act, b, k)
                act.activation(self.tmp[:, k - 1, 0, :], R.bank(k)[:, 0:S], ACT.Abs).then_inc(self.soft_abs, 1)
                if k > 1:
                    self.soft_exponential(act, b, k - 1)
            if not self.share and k > self.nq + 1:
                self.lone_keys_scalar(act, b, k - 2 - self.nq)
            yield
        if not self.share:
            self.lone_keys_scalar(act, b, self.nk - 1)
        if self.gates:
            R.wait_filled(act, b, self.G_USE)
            act.activation(self.gate[:, :, :, :], R.bank(self.G_USE)[:, 0:QT * 2 * H]
                           .rearrange("p (t g h) -> p t g h", t=QT, g=2), ACT.Exp, scale=-1.0)\
                .then_inc(R.free(self.G_USE), 1)
        if self.rope and self.share:
            for c in range(self.nk):
                self.lone_keys_scalar(act, b, c)
        yield
        if not self.rope:
            self.soft_exponential(act, b, CH)
            yield
            act.wait_ge(self.soft_exp, b * CH + CH)
            for c0, c1 in ((0, self.nq), (self.nq, CH)):
                a = self.tmp[:, c0:c1, 0, :]
                act.activation(a, a, ACT.Ln, bias=1.0).then_inc(self.soft_ln, 1)
            yield
            for c in range(self.nk):
                self.lone_keys_scalar(act, b, c)

    def scalar_items(self, act, b, first, end):
        R, T, NI, LAG = self.R, self.T, self.NI, self.LAG

        def copy(dst, src):
            return act.activation(dst, src, ACT.Copy)

        for i in range(first, end):
            gr = self.ended_group(i - LAG - 1)
            if gr is not None and self.causal:
                self.ot_copy(copy, act, b, gr)
            if i < NI:
                n = self.keys_of(i % QT)
                act.wait_ge(self.max_done, b * NI + i + 1)
                if i >= self.PR:
                    T.wait_filled(act, b, self.item_use(i - self.PR))
                m, k = i % self.PR, self.SCORES + i
                for hh in range(2):
                    e = act.activation(self.P[m][:, hh, 0:n], R.bank(k)[:, hh * S:hh * S + n], ACT.Exp,
                                       bias=self.nmax[:, m, hh:hh + 1], accum_out=self.sums[:, m, hh:hh + 1])
                e.then_inc(R.free(k), 1)
            j = i - LAG
            if 0 <= j < NI and j % QT == self.act_tile:
                self.pt_copy(copy, act, b, j)
            yield

    def vector_start(self, v, b):
        R, CH, w = self.R, self.CH, self.w
        SCALE = self.d ** -0.5
        yield
        for k in range(1, CH + 1):
            R.wait_filled(v, b, k)
            if self.rope:
                part = self.tmp[:, (k - 1) % 2, :, :]
                scale = SCALE if k <= self.nq else 1.0
                if k > 2:
                    v.wait_ge(self.joined, b * CH + k - 2)
                v.scalar_tensor_tensor(part[:, 0, :], R.bank(k)[:, 0:S], scale, w("cos"), ALU.mult, ALU.mult)
                v.scalar_tensor_tensor(part[:, 1, :], R.bank(k)[:, S:2 * S], scale, w("sin"), ALU.mult, ALU.mult)\
                    .then_inc(self.parts, 1)
                v.wait_ge(self.parts, b * CH + k)
                v.sem_inc(R.free(k), 1)
            else:
                v.wait_ge(self.soft_abs, b * CH + k)
                v.tensor_scalar(self.tmp[:, k - 1, 1, :], R.bank(k)[:, 0:S], 0.0, None, ALU.max).then_inc(R.free(k), 1)
            yield
        if self.rope and self.share:
            for c in range(self.nk):
                self.lone_keys_vector(v, b, c)
        for n in range(self.v_uses):
            k = self.V_USE + n
            R.wait_filled(v, b, k)
            t = QT // self.v_uses
            if self.dense:
                for i in range(t):
                    to = self.v_sb[:, i, :, :].rearrange("p g (j c) -> p g j c", c=40)[:, :, :, 0:self.d]
                    one = v.tensor_copy(to,
                                        R.bank(k)[:, i * self.nv:(i + 1) * self.nv]
                                        .rearrange("p (g j d) -> p g j d", g=self.NG, d=self.d))
                one.then_inc(R.free(k), 1)
            else:
                v.tensor_copy(self.v_sb[:, n * t:(n + 1) * t, :, 0:self.d],
                              R.bank(k)[:, 0:t * self.nv].rearrange("p (t h d) -> p t h d", t=t, d=self.d))\
                    .then_inc(R.free(k), 1)
        if self.gates:
            gate, step = self.gate, self.gate_step
            R.wait_emptied(v, b, self.G_USE)
            v.tensor_scalar(gate[:, :, :, :], gate[:, :, :, :], 1.0, None, ALU.add).then_inc(step, 1)
            v.wait_ge(step, 3 * b + 1)
            v.reciprocal(gate[:, :, :, :], gate[:, :, :, :]).then_inc(step, 1)
            v.wait_ge(step, 3 * b + 2)
            v.tensor_tensor(self.gsum[:, :, :], gate[:, :, 0, :], gate[:, :, 1, :], ALU.add).then_inc(step, 1)
            v.wait_ge(step, 3 * b + 3)
        yield
        if not self.rope:
            yield
            R.wait_emptied(v, b, CH - 1)
            R.wait_emptied(v, b, CH)
            for isk, c0, c1 in ((0, 0, self.nq), (1, self.nq, CH)):
                v.wait_ge(self.soft_ln, 2 * b + isk + 1)
                v.tensor_tensor(self.tmp[:, c0:c1, 1, :], self.tmp[:, c0:c1, 1, :], self.tmp[:, c0:c1, 0, :], ALU.add)\
                    .then_inc(self.soft_sum, 1)
                v.wait_ge(self.soft_sum, 2 * b + isk + 1)
                for k in range(c0 + 1, c1 + 1):
                    v.scalar_tensor_tensor(self.chunk(k), self.tmp[:, k - 1, 1, :], 1.0 if isk else SCALE,
                                           self.ktab[:, k - 1 - self.nq, :] if isk else w("cos"),
                                           ALU.mult, ALU.mult).then_inc(self.joined, 1)
            for c in range(self.nk):
                self.lone_keys_vector(v, b, c)
            yield

    def vector_items(self, v, b, first, end):
        R, T, NI, LAG, x = self.R, self.T, self.NI, self.LAG, self.g["x"]
        for i in range(first, end):
            gr = self.ended_group(i - LAG - 1)
            if gr is not None and not self.causal:
                self.ot_copy(v.tensor_copy, v, b, gr)
            if i < NI:
                n = self.keys_of(i % QT)
                k = self.SCORES + i
                R.wait_filled(v, b, k)
                v.tensor_reduce(self.nmax[:, i % self.PR, :],
                                R.bank(k)[:, :].rearrange("p (j k) -> p j k", j=2)[:, :, 0:n],
                                AX.X, ALU.max, negate=True).then_inc(self.max_done, 1)
            j = i - 1
            if 0 <= j < NI:
                m = j % self.PR
                R.wait_emptied(v, b, self.SCORES + j)
                v.reciprocal(self.rec[:, m, :], self.sums[:, m, :]).then_inc(self.rec_done, 1)
                if self.gates:
                    u, qt = divmod(j, QT)
                    v.wait_ge(self.rec_done, b * NI + j + 1)
                    v.tensor_tensor(self.weight[:, m, :], self.rec[:, m, :], self.gsum[:, qt, 2 * u:2 * u + 2],
                                    ALU.mult).then_inc(self.weight_done, 1)
            j = i - LAG
            if 0 <= j < NI and j % QT != self.act_tile:
                self.pt_copy(v.tensor_copy, v, b, j)
            if i == NI - 5:
                self.nrm.take_moments(v, b + 1)
            if i == NI - 4:
                self.nrm.norm_rows(v, b + 1)
            if i == self.STEPS - 1:
                k, c = self.OUT, self.batch(b)
                T.wait_filled(v, b, k)
                v.tensor_tensor(x[:, bass.ds(QT * c, QT), :], x[:, bass.ds(QT * c, QT), :],
                                T.bank(k)[:, 0:QT * 128].rearrange("p (t f) -> p t f", t=QT),
                                ALU.add).then_inc(T.free(k), 1)
            yield


def batches(eng, parts):
    NI = H // 2 * QT
    last = B // len(parts) - 1

    def round_of(start, items, steps, i):
        yield from items(eng, i, 0, NI)
        yield from beside(items(eng, i, NI, steps), start(eng, i + 1))

    in_turn(*(start(eng, 0) for start, items, steps in parts))
    with eng.Fori(0, last) as i:
        in_turn(*(round_of(*part, i) for part in parts))
    in_turn(*(items(eng, last, 0, steps) for start, items, steps in parts))


def self_attention(nc, g, name, wts, spec):
    LANES = 2
    nk, rope = spec["kchunks"], spec["rope"]
    st = Stage(nc, name)
    w, loaded = wts.of, wts.loaded
    ktab = st.sb("ktab", [128, nk, S])
    turned = st.sb("turned", [128, nk, S])
    phase = st.sb("phase", [128, 4, nk])
    tables, step = st.sem("tables"), st.sem("step")

    lanes = [SelfLane(st, n, LANES, g, w, ktab, spec) for n in range(LANES)]

    with nc.Block(f"{name}_block") as block:
        @block.sync
        def _(sp):
            for ln in lanes:
                ln.sync_setup(sp)

        @block.gpsimd
        def _(pool):
            for ln in lanes:
                ln.pool_setup(pool)
            pool.wait_ge(loaded, 16)
            for ln in lanes:
                ln.nrm.pool(pool, 0)
            batches(pool, [(ln.pool_start, ln.pool_items, ln.STEPS) for ln in lanes])

        @block.tensor
        def _(pe):
            pe.wait_ge(loaded, 16)
            batches(pe, [(ln.tensor_start, ln.tensor_items, ln.STEPS) for ln in lanes])

        @block.scalar
        def _(act):
            if not rope:
                act.wait_ge(tables, 1)
                act.activation(phase[:, 1, :], phase[:, 0, :], ACT.Sin).then_inc(tables, 1)
                act.activation(phase[:, 2, :], phase[:, 0, :], ACT.Sin, scale=0.5).then_inc(tables, 1)
            batches(act, [(ln.scalar_start, ln.scalar_items, ln.STEPS) for ln in lanes])

        @block.vector
        def _(v):
            v.wait_ge(loaded, 16)
            if not rope:
                v.tensor_scalar(phase[:, 3, :], w("bias"), 0.0, -2 * np.pi, ALU.min, ALU.max).then_inc(step, 1)
                v.wait_ge(step, 1)
                v.tensor_scalar(phase[:, 3, :], phase[:, 3, :], np.pi, 3.1415925, ALU.add, ALU.min)\
                    .then_inc(step, 1)
                v.wait_ge(step, 2)
                v.tensor_scalar(phase[:, 0, :], phase[:, 3, :], -3.1415925, None, ALU.max).then_inc(tables, 1)
                v.wait_ge(tables, 3)
                v.tensor_tensor(phase[:, 3, :], phase[:, 2, :], phase[:, 2, :], ALU.mult).then_inc(step, 1)
                v.wait_ge(step, 3)
                v.tensor_scalar(phase[:, 2, :], phase[:, 3, :], 2.0, -1.0, ALU.mult, ALU.add).then_inc(step, 1)
                v.wait_ge(step, 4)
                for c in range(nk):
                    v.tensor_scalar(turned[:, c, :], w("turn"), phase[:, 1, c:c + 1], None, ALU.mult)\
                        .then_inc(step, 1)
                for c in range(nk):
                    v.wait_ge(step, 5 + c)
                    v.scalar_tensor_tensor(ktab[:, c, :], w("cos"), phase[:, 2, c:c + 1], turned[:, c, :],
                                           ALU.mult, ALU.subtract).then_inc(tables, 1)
                v.wait_ge(tables, 3 + nk)
            for ln in lanes:
                v.wait_ge(ln.v_set, 1)
                ln.nrm.take_moments(v, 0)
            for ln in lanes:
                ln.nrm.norm_rows(v, 0)
            batches(v, [(ln.vector_start, ln.vector_items, ln.STEPS) for ln in lanes])
    st.close()


class CrossLane:
    HI = 8
    NI = QT * H // HI
    SR = 2
    XT, Q, V, I0 = 0, 1, 2, 3

    def __init__(self, st, lane, lanes, g, w, kT, ksum, qbias, w1s, mode):
        self.g, self.w, self.kT, self.qbias, self.w1s, self.mode = g, w, kT, qbias, w1s, mode
        self.stats = mode == "stats"
        self.ksum = ksum
        st = Lane(st, lane, lanes)
        self.batch = st.batch
        HI, NI = self.HI, self.NI
        self.T = Ring(st, "t", 2, 4 if self.stats else self.I0 + NI + 3)
        self.scores = [st.ps(f"s{i}") for i in range(self.SR)]
        self.nrm = Norm(st, g["x"])
        self.xnT = st.sb("xnT", [128, S])
        self.q_sb = st.sb("q", [128, S])
        self.kbd = st.sb("kbd", [128, H, SC])
        self.ctx2 = st.sb("ctx2", [128, 2, SC])
        self.vbd = st.sb("vbd", [128, 2 * (128 + 16)])
        self.P = st.sb("p", [128, NI, HI, SC])
        self.sq = st.sb("sq", [128, NI, HI, SC]) if self.stats else None
        self.PT = st.sb("pt", [128, H // 2, S])
        self.OT = st.sb("ot", [128, S])
        self.over = st.sb("over", [128, S])
        self.top = st.sb("top", [128, NI, HI])
        self.sums = st.sb("sums", [128, NI, HI])
        self.rec = st.sb("rec", [128, NI, HI])
        self.row = st.sb("row", [128, 3, NI, HI]) if self.stats else None
        self.kbd_sum = st.sb("kbd_sum", [128, H]) if self.stats else None
        self.kbd_summed = st.sem("kbd_summed")
        self.kmask = st.sb("kmask", [128, H])
        self.kbd_vector, self.kbd_pool, self.ctx2_done = st.sem("kbd_vector"), st.sem("kbd_pool"), st.sem("ctx2_done")
        self.v_set, self.v_half = st.sem("v_set"), st.sem("v_half")
        self.s_filled, self.top_done, self.sub_done = st.sem("s_filled"), st.sem("top_done"), st.sem("sub_done")
        self.kmask_done = st.sem("kmask_done")
        self.exp_done, self.sum_done, self.rec_done = st.sem("exp_done"), st.sem("sum_done"), st.sem("rec_done")
        self.p_done, self.sq_done, self.rows_done = st.sem("p_done"), st.sem("sq_done"), st.sem("rows_done")
        self.added = st.sem("added")

    def sync_setup(self, sp):
        self.T.credit(sp)
        sp.sem_inc(self.sub_done, self.SR)

    def pool_setup(self, pool):
        self.nrm.pool_setup(pool)
        pool.memset(self.vbd[:, :], 0.0).then_inc(self.v_set, 1)

    def lone_keys(self, eng, b, half):
        h = self.HI * half
        return eng.tensor_tensor(self.kbd[:, h:h + self.HI, :],
                                 self.kT[:, self.batch(b), :].unsqueeze(1).to_broadcast([128, self.HI, SC]),
                                 self.kmask[:, h:h + self.HI].unsqueeze(2).to_broadcast([128, self.HI, SC]),
                                 ALU.mult)

    def pool(self, pool, b):
        HI, NI, P = self.HI, self.NI, self.P
        pool.wait_ge(self.kmask_done, b + 1)
        self.lone_keys(pool, b, 1).then_inc(self.kbd_pool, 1)
        yield
        yield
        for s in range(NI + 3):
            i = s - 2
            if 0 <= i < NI and self.stats:
                pool.wait_ge(self.rec_done, b * NI + i + 1)
                pool.tensor_tensor(P[:, i, :, :], P[:, i, :, :],
                                   self.rec[:, i, :].unsqueeze(2).to_broadcast([128, HI, SC]),
                                   ALU.mult).then_inc(self.p_done, 1)
            if s == NI + 1:
                self.nrm.pool(pool, b + 1)
            yield

    def tensor(self, pe, b):
        HI, NI, T, w, g = self.HI, self.NI, self.T, self.w, self.g
        self.nrm.wait(pe, b)
        T.wait_free(pe, b, self.XT)
        for t in range(QT):
            mm = pe.transpose(T.bank(self.XT)[:, t * 128:t * 128 + 128], self.nrm.xn[:, t, :], g["ident"][:, :])
        mm.then_inc(T.full(self.XT), 1)
        yield
        T.wait_emptied(pe, b, self.XT)
        T.wait_free(pe, b, self.Q)
        pe.matmul(T.bank(self.Q)[:, 0:S], w("q"), self.xnT[:, :], start=True, stop=True).then_inc(T.full(self.Q), 1)
        if not self.stats:
            pe.wait_ge(self.ctx2_done, b + 1)
            T.wait_free(pe, b, self.V)
            pe.matmul(T.bank(self.V)[:, 0:D], self.ctx2[:, :, :], w("v"), start=True, stop=True)\
                .then_inc(T.full(self.V), 1)
        yield
        for s in range(NI + 3):
            i = s
            if i == 0:
                T.wait_emptied(pe, b, self.Q)
            if i < NI:
                t, hh = divmod(i, 2)
                if i < 2:
                    pe.wait_ge(self.kbd_pool if i else self.kbd_vector, b + 1)
                pe.wait_ge(self.sub_done, b * NI + i + 1)
                bank = self.scores[i % self.SR]
                mm = pe.matmul(bank[:, :], self.q_sb[:, t * 128:t * 128 + 128],
                               self.kbd[:, hh * HI:hh * HI + HI, :], start=True, stop=(self.mode != "plain"))
                if self.mode == "plain":
                    mm = pe.matmul(bank[:, :].rearrange("p (h k) -> p h k", h=HI), g["onesb"][:, :],
                                   g["pad"][:, self.batch(b), :].unsqueeze(1).to_broadcast([128, HI, SC]),
                                   start=False, stop=True)
                mm.then_inc(self.s_filled, 1)
            if s == 1 and self.stats:
                pe.wait_ge(self.kbd_summed, b + 1)
                T.wait_free(pe, b, self.V)
                for t in range(QT):
                    mm = pe.matmul(T.bank(self.V)[:, t * H:t * H + H], self.q_sb[:, t * 128:t * 128 + 128],
                                   self.kbd_sum[:, :], start=True, stop=True)
                mm.then_inc(T.full(self.V), 1)
            i = s - 2
            if 0 <= i < NI and not self.stats:
                pe.wait_ge(self.exp_done, b * NI + i + 1)
                T.wait_free(pe, b, self.I0 + i)
                for m in range(4):
                    mm = pe.transpose(T.bank(self.I0 + i)[:, m * 128:m * 128 + 128],
                                      self.P[:, i, 2 * m:2 * m + 2, :], g["ident"][:, :])
                mm.then_inc(T.full(self.I0 + i), 1)
            yield
        if self.stats:
            T.wait_emptied(pe, b, self.V)
            pe.wait_ge(self.top_done, b * NI + NI)
            pe.wait_ge(self.rows_done, b * NI + NI)
            k = self.I0
            T.wait_free(pe, b, k)
            n = 0
            for f in range(3):
                for t in range(QT):
                    mm = pe.matmul(T.bank(k)[0:64, 0:H], self.w1s[:, f * 64:f * 64 + 64],
                                   self.row[:, f, 2 * t:2 * t + 2, :], start=(n == 0), stop=(n == 3 * QT - 1))
                    n += 1
            mm.then_inc(T.full(k), 1)
            yield
        else:
            k = self.I0 + NI
            pe.wait_ge(self.v_half, 2 * b + 2)
            T.wait_emptied(pe, b, k - 2)
            T.wait_emptied(pe, b, k - 1)
            for n, left in enumerate((self.vbd, w("ones"))):
                T.wait_free(pe, b, k + n)
                for m in range(4):
                    for gr in range(2):
                        at = (128 * gr + 32 * m) if n == 0 else 32 * gr
                        mm = pe.matmul(T.bank(k + n)[32 * m:32 * m + 32, 0:S], left[:, at:at + 32],
                                       self.PT[:, 4 * gr + m, :], start=(gr == 0), stop=(gr == 1),
                                       tile_position=(0, 32 * m))
                mm.then_inc(T.full(k + n), 1)
            yield
            T.wait_emptied(pe, b, k)
            k += 2
            T.wait_free(pe, b, k)
            for t in range(QT):
                mm = pe.matmul(T.bank(k)[:, t * 128:t * 128 + 128], self.OT[:, t * 128:t * 128 + 128], w("o"),
                               start=True, stop=True)
            mm.then_inc(T.full(k), 1)
            yield

    def scalar(self, act, b):
        NI, T = self.NI, self.T
        T.wait_filled(act, b, self.XT)
        act.activation(self.xnT[:, :], T.bank(self.XT)[:, 0:S], ACT.Copy).then_inc(T.free(self.XT), 1)
        yield
        T.wait_filled(act, b, self.Q)
        act.activation(self.q_sb[:, :], T.bank(self.Q)[:, 0:S], ACT.Identity, scale=self.SCALE[self.mode],
                       bias=self.qbias[:, :]).then_inc(T.free(self.Q), 1)
        yield
        for s in range(NI + 3):
            if s == 1 and self.stats:
                T.wait_filled(act, b, self.V)
                act.activation(self.row[:, 0, :, :],
                               T.bank(self.V)[:, 0:QT * H].rearrange("p (i h) -> p i h", h=self.HI), ACT.Copy).then_inc(T.free(self.V), 1)
            i = s - 3
            if i >= 0 and self.stats:
                act.wait_ge(self.p_done, b * NI + i + 1)
                act.activation(self.sq[:, i, :, :], self.P[:, i, :, :], ACT.Square, bias=self.g["minus_mean"][:, :])\
                    .then_inc(self.sq_done, 1)
            i = s - 2
            if 0 <= i < NI and not self.stats:
                t, hh = divmod(i, 2)
                T.wait_filled(act, b, self.I0 + i)
                act.activation(self.PT[:, 4 * hh:4 * hh + 4, t * 128:t * 128 + 128],
                               T.bank(self.I0 + i)[:, :].rearrange("p (m q) -> p m q", m=4), ACT.Copy)\
                    .then_inc(T.free(self.I0 + i), 1)
            i = s - 1
            if 0 <= i < NI:
                act.wait_ge(self.sub_done, b * NI + i + 1 + self.SR)
                act.activation(self.P[:, i, :, :], self.P[:, i, :, :], ACT.Exp).then_inc(self.exp_done, 1)
            yield

    def vector(self, v, b):
        HI, NI, T, w, g, P = self.HI, self.NI, self.T, self.w, self.g, self.P
        d = D // H
        x, c = g["x"], self.batch(b)
        if not self.stats:
            v.tensor_copy(self.ctx2[:, :, :], g["ctxT"][:, c, :].unsqueeze(1).to_broadcast([128, 2, SC]))\
                .then_inc(self.ctx2_done, 1)
        if self.mode == "tempered":
            v.tensor_tensor(self.kmask[:, :], w("kmask"), g["factor"][:, c, :], ALU.mult).then_inc(self.kmask_done, 1)
        else:
            v.tensor_copy(self.kmask[:, :], w("kmask")).then_inc(self.kmask_done, 1)
        v.wait_ge(self.kmask_done, b + 1)
        self.lone_keys(v, b, 0).then_inc(self.kbd_vector, 1)
        if self.stats:
            T.wait_free(v, b, self.V)
            v.tensor_tensor(self.kbd_sum[:, :], w("kmask"), self.ksum[:, bass.ds(c, 1)].to_broadcast([128, H]),
                            ALU.mult)\
                .then_inc(self.kbd_summed, 1)
        yield
        for j in range(0 if self.stats else 2):
            T.wait_filled(v, b, self.V)
            lo = 64 * j
            vv = T.bank(self.V)[lo:lo + 64, 0:D].rearrange("p (g m j e) -> p g m j e", g=2, j=2, e=d)[:, :, :, j, :]
            bb = w("vb")[lo:lo + 64, :].rearrange("p (g m j e) -> p g m j e", g=2, j=2, e=d)[:, :, :, j, :]
            to = self.vbd[lo:lo + 64, :].rearrange("p (g x) -> p g x", g=2)[:, :, 0:128]
            to = to.rearrange("p g (m c) -> p g m c", c=32)[:, :, :, d * j:d * j + d]
            v.tensor_tensor(to, vv, bb, ALU.add).then_inc(self.v_half, 1)
        if not self.stats:
            v.wait_ge(self.v_half, 2 * b + 2)
            v.sem_inc(T.free(self.V), 1)
        yield
        for s in range(NI + 3):
            i = s
            if i < NI:
                v.wait_ge(self.s_filled, b * NI + i + 1)
                sv = self.scores[i % self.SR][:, :].rearrange("p (h k) -> p h k", h=HI)
                dst = self.row[:, 1, i, :] if self.stats else self.top[:, i, :]
                v.tensor_reduce(dst, sv, AX.X, ALU.max).then_inc(self.top_done, 1)
            i = s - 1
            if 0 <= i < NI:
                sv = self.scores[i % self.SR][:, :].rearrange("p (h k) -> p h k", h=HI)
                src = self.row[:, 1, i, :] if self.stats else self.top[:, i, :]
                v.wait_ge(self.top_done, b * NI + i + 1)
                v.tensor_tensor(P[:, i, :, :], sv, src.unsqueeze(2).to_broadcast([128, HI, SC]),
                                ALU.subtract).then_inc(self.sub_done, 1)
            i = s - 2
            if 0 <= i < NI and self.stats:
                v.wait_ge(self.exp_done, b * NI + i + 1)
                v.tensor_reduce(self.sums[:, i, :], P[:, i, :, :], AX.X, ALU.add).then_inc(self.sum_done, 1)
                v.wait_ge(self.sum_done, b * NI + i + 1)
                v.reciprocal(self.rec[:, i, :], self.sums[:, i, :]).then_inc(self.rec_done, 1)
            i = s - 3
            if i >= 0 and self.stats:
                v.wait_ge(self.sq_done, b * NI + i + 1)
                v.tensor_reduce(self.row[:, 2, i, :], self.sq[:, i, :, :], AX.X, ALU.add).then_inc(self.rows_done, 1)
            if s == NI + 1:
                self.nrm.take_moments(v, b + 1)
            if s == NI + 2:
                self.nrm.norm_rows(v, b + 1)
            yield
        if self.stats:
            k = self.I0
            T.wait_filled(v, b, k)
            v.tensor_copy(g["hidden"][:, c, :], T.bank(k)[0:64, 0:H]).then_inc(T.free(k), 1)
            yield
        else:
            k = self.I0 + NI
            T.wait_filled(v, b, k + 1)
            v.reciprocal(self.over[:, :], T.bank(k + 1)[:, 0:S]).then_inc(T.free(k + 1), 1)
            T.wait_emptied(v, b, k + 1)
            v.tensor_tensor(self.OT[:, :], T.bank(k)[:, 0:S], self.over[:, :], ALU.mult).then_inc(T.free(k), 1)
            yield
            k += 2
            T.wait_filled(v, b, k)
            v.tensor_tensor(x[:, bass.ds(QT * c, QT), :], x[:, bass.ds(QT * c, QT), :],
                            T.bank(k)[:, 0:QT * 128].rearrange("p (t f) -> p t f", t=QT),
                            ALU.add).then_inc(T.free(k), 1)
            T.wait_emptied(v, b, k)
            v.tensor_tensor(x[:, bass.ds(QT * c, QT), :], x[:, bass.ds(QT * c, QT), :],
                            w("ob").unsqueeze(1).to_broadcast([128, QT, D]), ALU.add).then_inc(self.added, 1)
            yield

    SCALE = {"plain": (D // H) ** -0.5, "stats": (D // H) ** -0.5, "tempered": 1.0}


def cross_attention(nc, g, name, wts, mode):
    LANES = 2
    SCALE = CrossLane.SCALE[mode]
    st = Stage(nc, name)
    w, loaded = wts.of, wts.loaded
    kT = st.sb("kT", [128, B, SC])
    qbias = st.sb("qbias", [128, 1])
    w1s = st.sb("w1s", [128, 3 * 64]) if mode == "stats" else None
    set_up, w1s_done = st.sem("set_up"), st.sem("w1s_done")
    kT_filled, kT_done = st.sem("kT_filled"), st.sem("kT_done")

    ksum = st.sb("ksum", [128, B]) if mode == "stats" else None
    ksum_done = st.sem("ksum_done")
    lanes = [CrossLane(st, n, LANES, g, w, kT, ksum, qbias, w1s, mode) for n in range(LANES)]
    kps = lanes[0].scores[0]

    with nc.Block(f"{name}_block") as block:
        @block.sync
        def _(sp):
            for ln in lanes:
                ln.sync_setup(sp)

        @block.gpsimd
        def _(pool):
            for ln in lanes:
                ln.pool_setup(pool)
            for ln in lanes:
                ln.nrm.pool(pool, 0)
            pool.wait_ge(kT_done, 1)
            with pool.Fori(0, B // LANES) as i:
                in_turn(*(ln.pool(pool, i) for ln in lanes))

        @block.tensor
        def _(pe):
            pe.wait_ge(loaded, 16)
            pe.matmul(kps[:, :], w("k"), g["ctxT"][:, :, :], start=True, stop=True).then_inc(kT_filled, 1)
            pe.wait_ge(kT_done, 1)
            if mode == "stats":
                pe.wait_ge(w1s_done, 3)
            with pe.Fori(0, B // LANES) as i:
                in_turn(*(ln.tensor(pe, i) for ln in lanes))

        @block.scalar
        def _(act):
            act.wait_ge(loaded, 16)
            act.activation(qbias[:, :], w("qb"), ACT.Copy, scale=SCALE).then_inc(set_up, 1)
            act.wait_ge(kT_filled, 1)
            act.activation(kT[:, :, :], kps[:, :].rearrange("p (b k) -> p b k", b=B), ACT.Identity, bias=w("kb"))\
                .then_inc(kT_done, 1)
            act.wait_ge(set_up, 1)
            with act.Fori(0, B // LANES) as i:
                in_turn(*(ln.scalar(act, i) for ln in lanes))

        @block.vector
        def _(v):
            v.wait_ge(loaded, 16)
            if mode == "stats":
                for f, n in enumerate((SC * S, S, (SC - 1) * S)):
                    v.tensor_scalar(w1s[:, f * 64:f * 64 + 64], w("w1")[:, f * 64:f * 64 + 64], 1.0 / n, None,
                                    ALU.mult).then_inc(w1s_done, 1)
            for ln in lanes:
                v.wait_ge(ln.v_set, 1)
                ln.nrm.take_moments(v, 0)
            for ln in lanes:
                ln.nrm.norm_rows(v, 0)
            v.wait_ge(kT_done, 1)
            if mode == "stats":
                v.tensor_reduce(ksum[:, :], kT[:, :, :], AX.X, ALU.add).then_inc(ksum_done, 1)
                v.wait_ge(ksum_done, 1)
            with v.Fori(0, B // LANES) as i:
                in_turn(*(ln.vector(v, i) for ln in lanes))
    st.close()


def temperature(nc, g, wts):
    st = Stage(nc, "temp")
    loaded = wts.loaded
    ps = st.ps("ps")
    N = B * H
    h1 = st.sb("h1", [64, N])
    h2 = st.sb("h2", [64, N])
    lt = st.sb("lt", [128, N])
    product = st.sem("product")
    gelu = st.sem("gelu")
    clipped = st.sem("clipped")
    done = st.sem("done")

    def w(key, rows=64):
        return wts.of(key)[0:rows, :]

    with nc.Block("temp_block") as block:
        @block.scalar
        def _(act):
            act.wait_ge(loaded, 16)
            act.activation(h1[:, :], g["hidden"][:, :, :].rearrange("p b h -> p (b h)"), ACT.Gelu, bias=w("b1"))\
                .then_inc(gelu, 1)
            act.wait_ge(product, 1)
            act.activation(h2[:, :], ps[0:64, 0:N], ACT.Gelu, bias=w("b2")).then_inc(gelu, 1)
            act.wait_ge(clipped, 2)
            act.activation(lt[:, :], lt[:, :], ACT.Exp, scale=-1.0).then_inc(clipped, 1)

        @block.tensor
        def _(pe):
            pe.wait_ge(loaded, 16)
            pe.wait_ge(gelu, 1)
            pe.matmul(ps[0:64, 0:N], w("w2"), h1[:, :], start=True, stop=True).then_inc(product, 1)
            pe.wait_ge(gelu, 2)
            pe.matmul(ps[:, N:2 * N], w("w3"), h2[:, :], start=True, stop=True).then_inc(product, 1)

        @block.vector
        def _(v):
            v.wait_ge(loaded, 16)
            v.wait_ge(product, 2)
            v.tensor_scalar(lt[:, :], ps[:, N:2 * N], w("b3", 128), float(np.log(10.0)), ALU.add, ALU.min)\
                .then_inc(clipped, 1)
            v.wait_ge(clipped, 1)
            v.tensor_scalar(lt[:, :], lt[:, :], float(np.log(0.1)), None, ALU.max).then_inc(clipped, 1)
            v.wait_ge(clipped, 3)
            v.tensor_scalar(g["factor"][:, :, :].rearrange("p b h -> p (b h)"), lt[:, :], 0.5, None, ALU.mult)\
                .then_inc(done, 1)
    st.close()


def L2_xattn(nc, g, wts):
    with nc.sbuf_tensor("hidden", [64, B, H], F32) as hidden, nc.sbuf_tensor("factor", [128, B, H], F32) as factor:
        g["hidden"], g["factor"] = hidden, factor
        cross_attention(nc, g, "l2xs", wts, "stats")
        temperature(nc, g, wts)
        cross_attention(nc, g, "l2x", wts, "tempered")


class L0_xattn_lane:
    XT, Q, V, SCORES, PTURNED, OUT = 0, 1, 2, 3, 4, 5

    def __init__(self, st, lane, lanes, g, w, kT, qbias, keep, fill):
        self.g, self.w, self.kT, self.qbias, self.keep, self.fill = g, w, kT, qbias, keep, fill
        st = Lane(st, lane, lanes)
        self.batch = st.batch
        self.T = Ring(st, "t", 2, self.OUT + QT)
        self.nrm = Norm(st, g["x"])
        self.xnT = st.sb("xnT", [128, S])
        self.q_sb = st.sb("q", [128, S])
        self.ctx1 = st.sb("ctx1", [128, 2, SC])
        self.v_sb = st.sb("v", [2 * SC, D])
        self.P = st.sb("p", [128, QT, SC])
        self.P2 = st.sb("p2", [128, QT, SC])
        self.PT = st.sb("pt", [QT * SC, 128])
        self.top = st.sb("top", [128, QT])
        self.sums = st.sb("sums", [128, QT])
        self.rec = st.sb("rec", [128, QT])
        self.ctx1_done, self.masked, self.top_done = st.sem("ctx1_done"), st.sem("masked"), st.sem("top_done")
        self.less_top, self.exp_done, self.sum_done = st.sem("less_top"), st.sem("exp_done"), st.sem("sum_done")
        self.rec_done, self.p_done = st.sem("rec_done"), st.sem("p_done")

    def pool(self, pool, b):
        self.nrm.pool(pool, b + 1)
        yield

    def tensor(self, pe, b):
        T, w = self.T, self.w
        self.nrm.wait(pe, b)
        T.wait_free(pe, b, self.XT)
        for t in range(QT):
            mm = pe.transpose(T.bank(self.XT)[:, t * 128:t * 128 + 128], self.nrm.xn[:, t, :], self.g["ident"][:, :])
        mm.then_inc(T.full(self.XT), 1)
        yield
        T.wait_emptied(pe, b, self.XT)
        T.wait_free(pe, b, self.Q)
        pe.matmul(T.bank(self.Q)[:, 0:S], w("q"), self.xnT[:, :], start=True, stop=True).then_inc(T.full(self.Q), 1)
        pe.wait_ge(self.ctx1_done, b + 1)
        pe.matmul(T.bank(self.V)[:, 0:D], self.ctx1[:, :, :], w("v"), start=True, stop=True)\
            .then_inc(T.full(self.V), 1)
        yield
        T.wait_emptied(pe, b, self.Q)
        for t in range(QT):
            mm = pe.matmul(T.bank(self.SCORES)[:, t * SC:t * SC + SC], self.q_sb[:, t * 128:t * 128 + 128],
                           self.kT[:, self.batch(b), :], start=True, stop=True)
        mm.then_inc(T.full(self.SCORES), 1)
        yield
        yield
        yield
        pe.wait_ge(self.p_done, b + 1)
        T.wait_free(pe, b, self.PTURNED)
        pe.transpose(T.bank(self.PTURNED)[:, 0:128], self.P2[:, :, :], self.g["ident"][:, :])\
            .then_inc(T.full(self.PTURNED), 1)
        yield
        T.wait_emptied(pe, b, self.PTURNED)
        for t in range(QT):
            k = self.OUT + t
            T.wait_free(pe, b, k)
            pe.matmul(T.bank(k)[:, 0:128], self.PT[SC * t:SC * t + SC, :], self.v_sb[SC * t:SC * t + SC, :],
                      start=True, stop=True).then_inc(T.full(k), 1)
        yield

    def scalar(self, act, b):
        T = self.T
        T.wait_filled(act, b, self.XT)
        act.activation(self.xnT[:, :], T.bank(self.XT)[:, 0:S], ACT.Copy).then_inc(T.free(self.XT), 1)
        yield
        T.wait_filled(act, b, self.Q)
        act.activation(self.q_sb[:, :], T.bank(self.Q)[:, 0:S], ACT.Identity, scale=D ** -0.5,
                       bias=self.qbias[:, :]).then_inc(T.free(self.Q), 1)
        yield
        yield
        yield
        act.wait_ge(self.less_top, b + 1)
        act.activation(self.P[:, :, :], self.P[:, :, :], ACT.Exp).then_inc(self.exp_done, 1)
        yield
        T.wait_filled(act, b, self.PTURNED)
        act.activation(self.PT[:, :], T.bank(self.PTURNED)[:, 0:128], ACT.Copy).then_inc(T.free(self.PTURNED), 1)
        yield

    def vector(self, v, b):
        T, w, P, x, c = self.T, self.w, self.P, self.g["x"], self.batch(b)
        v.tensor_copy(self.ctx1[:, :, :], self.g["ctxT"][:, c, :].unsqueeze(1).to_broadcast([128, 2, SC]))\
            .then_inc(self.ctx1_done, 1)
        yield
        T.wait_filled(v, b, self.V)
        v.tensor_tensor(self.v_sb[:, :], T.bank(self.V)[:, 0:D], w("vb"), ALU.add).then_inc(T.free(self.V), 1)
        yield
        T.wait_filled(v, b, self.SCORES)
        v.tensor_tensor(P[:, :, :], T.bank(self.SCORES)[:, 0:QT * SC].rearrange("p (t k) -> p t k", t=QT),
                        self.keep[:, :, :], ALU.mult).then_inc(T.free(self.SCORES), 1)
        yield
        T.wait_emptied(v, b, self.SCORES)
        v.tensor_tensor(P[:, :, :], P[:, :, :], self.fill[:, :, :], ALU.add).then_inc(self.masked, 1)
        v.wait_ge(self.masked, b + 1)
        v.tensor_reduce(self.top[:, :], P[:, :, :], AX.X, ALU.max).then_inc(self.top_done, 1)
        v.wait_ge(self.top_done, b + 1)
        v.tensor_tensor(P[:, :, :], P[:, :, :], self.top[:, :].unsqueeze(2).to_broadcast([128, QT, SC]),
                        ALU.subtract).then_inc(self.less_top, 1)
        yield
        self.nrm.take_moments(v, b + 1)
        yield
        v.wait_ge(self.exp_done, b + 1)
        v.tensor_reduce(self.sums[:, :], P[:, :, :], AX.X, ALU.add).then_inc(self.sum_done, 1)
        v.wait_ge(self.sum_done, b + 1)
        v.reciprocal(self.rec[:, :], self.sums[:, :]).then_inc(self.rec_done, 1)
        v.wait_ge(self.rec_done, b + 1)
        v.tensor_tensor(self.P2[:, :, :], P[:, :, :], self.rec[:, :].unsqueeze(2).to_broadcast([128, QT, SC]),
                        ALU.mult).then_inc(self.p_done, 1)
        yield
        self.nrm.norm_rows(v, b + 1)
        yield
        for t in range(QT):
            T.wait_filled(v, b, self.OUT + t)
            v.tensor_tensor(x[:, QT * c + t, :], x[:, QT * c + t, :], T.bank(self.OUT + t)[:, 0:128], ALU.add)\
                .then_inc(T.free(self.OUT + t), 1)
        yield


def L0_xattn(nc, g, wts):
    LANES = 4
    st = Stage(nc, "l0x")
    w, loaded = wts.of, wts.loaded
    qbias = st.sb("qbias", [128, 1])
    kT = st.sb("kT", [128, B, SC])
    mask8 = g["mask8"]
    keep = st.sb("keep", [128, QT, SC])
    fill = st.sb("fill", [128, QT, SC])
    set_up, masks_done = st.sem("set_up"), st.sem("masks_done")
    kT_filled, kT_done = st.sem("kT_filled"), st.sem("kT_done")

    lanes = [L0_xattn_lane(st, n, LANES, g, w, kT, qbias, keep, fill) for n in range(LANES)]
    kps = lanes[0].T.bank(0)

    with nc.Block("l0x_block") as block:
        @block.sync
        def _(sp):
            for ln in lanes:
                ln.T.credit(sp)

        @block.gpsimd
        def _(pool):
            for ln in lanes:
                ln.nrm.pool_setup(pool)
            for ln in lanes:
                ln.nrm.pool(pool, 0)
            with pool.Fori(0, B // LANES) as i:
                in_turn(*(ln.pool(pool, i) for ln in lanes))

        @block.tensor
        def _(pe):
            pe.wait_ge(loaded, 16)
            pe.matmul(kps[:, :], w("k"), g["ctxT"][:, :, :], start=True, stop=True).then_inc(kT_filled, 1)
            pe.wait_ge(kT_done, 1)
            with pe.Fori(0, B // LANES) as i:
                in_turn(*(ln.tensor(pe, i) for ln in lanes))

        @block.scalar
        def _(act):
            act.wait_ge(loaded, 16)
            act.activation(qbias[:, :], w("qb"), ACT.Copy, scale=D ** -0.5).then_inc(set_up, 1)
            act.wait_ge(kT_filled, 1)
            act.activation(kT[:, :, :], kps[:, :].rearrange("p (b k) -> p b k", b=B), ACT.Identity, bias=w("kb"))\
                .then_inc(kT_done, 1)
            act.wait_ge(set_up, 1)
            with act.Fori(0, B // LANES) as i:
                in_turn(*(ln.scalar(act, i) for ln in lanes))

        @block.vector
        def _(v):
            v.wait_ge(loaded, 16)
            v.tensor_scalar(keep[:, :, :], mask8[:, :, :], -1.0, 1.0, ALU.mult, ALU.add).then_inc(masks_done, 1)
            v.tensor_scalar(fill[:, :, :], mask8[:, :, :], -1e9, None, ALU.mult).then_inc(masks_done, 1)
            v.wait_ge(masks_done, 2)
            for ln in lanes:
                ln.nrm.take_moments(v, 0)
            for ln in lanes:
                ln.nrm.norm_rows(v, 0)
            with v.Fori(0, B // LANES) as i:
                in_turn(*(ln.vector(v, i) for ln in lanes))
    st.close()


ROUND = 1.5 * 2 ** 23


class L1_ffn_lane:
    F = 512
    FC = F // 128
    XS, HS = 6, 6

    def __init__(self, st, lane, lanes, g, wq, wmean):
        self.g, self.wq, self.wmean = g, wq, wmean
        F, FC = self.F, self.FC
        st = Lane(st, lane, lanes)
        self.batch = st.batch
        self.nrm = Norm(st, g["x"])
        self.amax = st.sb("amax", [128, QT])
        self.ascale = st.sb("ascale", [128, QT])
        self.xr = st.sb("xr", [128, QT, D])
        self.xr2 = st.sb("xr2", [128, QT, D])
        self.xq = st.sb("xq", [128, QT, D], BF16)
        self.xqT = st.sb("xqT", [128, S], BF16)
        self.back = st.sb("back", [128, QT, 3])
        self.gate = st.sb("gate", [128, QT, F])
        self.h = st.sb("h", [128, QT, F])
        self.hr = st.sb("hr", [128, QT, F])
        self.hq = st.sb("hq", [128, QT, F], BF16)
        self.hqT = st.sb("hqT", [128, QT, FC, 128], BF16)
        self.hmax = st.sb("hmax", [128, QT])
        self.hscale = st.sb("hscale", [128, QT])
        self.tps = st.ps("tps", (128, 1024), BF16)
        self.gps, self.ups, self.yps = st.ps("gps"), st.ps("ups"), st.ps("yps")
        self.xstep, self.xq_done = st.sem("xstep"), st.sem("xq_done")
        self.xT_filled, self.xT_done = st.sem("xT_filled"), st.sem("xT_done")
        self.g_filled, self.u_filled = st.sem("g_filled"), st.sem("u_filled")
        self.gate_done, self.h_done = st.sem("gate_done"), st.sem("h_done")
        self.hstep, self.hq_done = st.sem("hstep"), st.sem("hq_done")
        self.hT_filled, self.hT_done = st.sem("hT_filled"), st.sem("hT_done")
        self.y_filled, self.y_done = st.sem("y_filled"), st.sem("y_done")

    def pool(self, pool, b):
        self.nrm.pool(pool, b + 1)
        yield

    def first_products(self, pe, b, t):
        pe.wait_ge(self.h_done, QT * b + t + 1)
        for bank, n, sem in ((self.gps, 0, self.g_filled), (self.ups, 1, self.u_filled)):
            pe.matmul(bank[:, :], self.xqT[:, t * 128:t * 128 + 128], self.wq[:, n, :], start=True, stop=True)\
                .then_inc(sem, 1)

    def tensor(self, pe, b):
        FC, F, identb = self.FC, self.F, self.g["identb"]
        yield
        pe.wait_ge(self.xq_done, b + 1)
        pe.wait_ge(self.hT_done, QT * b + QT)
        for t in range(QT):
            mm = pe.transpose(self.tps[:, F + t * 128:F + t * 128 + 128], self.xq[:, t, :], identb[:, :])
        mm.then_inc(self.xT_filled, 1)
        yield
        pe.wait_ge(self.xT_done, b + 1)
        self.first_products(pe, b, 0)
        yield
        for t in range(QT):
            if t + 1 < QT:
                self.first_products(pe, b, t + 1)
            pe.wait_ge(self.hq_done, QT * b + t + 1)
            if t > 0:
                pe.wait_ge(self.hT_done, QT * b + t + QT)
            for c in range(FC):
                mm = pe.transpose(self.tps[:, c * 128:c * 128 + 128], self.hq[:, t, c * 128:c * 128 + 128], identb[:, :])
            mm.then_inc(self.hT_filled, 1)
            yield
        pe.wait_ge(self.y_done, QT * b + QT)
        for t in range(QT):
            pe.wait_ge(self.hT_done, QT * b + t + 1 + QT)
            for c in range(FC):
                mm = pe.matmul(self.yps[:, t * 128:t * 128 + 128], self.hqT[:, t, c, :],
                               self.wq[:, 2, c * 128:c * 128 + 128], start=(c == 0), stop=(c == FC - 1))
        mm.then_inc(self.y_filled, 1)
        yield

    def scalar(self, act, b):
        FC, F = self.FC, self.F
        yield
        act.wait_ge(self.xT_filled, b + 1)
        act.activation(self.xqT[:, :], self.tps[:, F:F + S], ACT.Copy).then_inc(self.xT_done, 1)
        yield
        act.wait_ge(self.xstep, self.XS * b + self.XS)
        for t in range(QT + 1):
            if t > 0:
                act.wait_ge(self.hT_filled, QT * b + t)
                act.activation(self.hqT[:, t - 1, :, :], self.tps[:, 0:F].rearrange("p (c q) -> p c q", c=FC),
                               ACT.Copy).then_inc(self.hT_done, 1)
            if t < QT:
                act.wait_ge(self.g_filled, QT * b + t + 1)
                act.activation(self.gate[:, t, :], self.gps[:, :], ACT.Silu, scale=self.back[:, t, 0:1])\
                    .then_inc(self.gate_done, 1)
            yield

    def vector(self, v, b):
        nrm, xstep, hstep, x, wmean, back = self.nrm, self.xstep, self.hstep, self.g["x"], self.wmean, self.back
        XS, HS, c = self.XS, self.HS, self.batch(b)
        nrm.wait(v, b)
        v.tensor_reduce(self.amax[:, :], nrm.xn[:, :, :], AX.X, ALU.max, apply_absolute_value=True).then_inc(xstep, 1)
        yield
        v.wait_ge(xstep, XS * b + 1)
        v.tensor_scalar(self.amax[:, :], self.amax[:, :], 1e-5, 1.0 / 127.0, ALU.max, ALU.mult).then_inc(xstep, 1)
        yield
        v.wait_ge(xstep, XS * b + 2)
        v.reciprocal(self.ascale[:, :], self.amax[:, :]).then_inc(xstep, 1)
        yield
        v.wait_ge(xstep, XS * b + 3)
        v.tensor_tensor(self.xr[:, :, :], nrm.xn[:, :, :], self.ascale[:, :].unsqueeze(2).to_broadcast([128, QT, D]),
                        ALU.mult).then_inc(xstep, 1)
        yield
        v.wait_ge(xstep, XS * b + 4)
        v.tensor_scalar(self.xr2[:, :, :], self.xr[:, :, :], 127.0, -128.0, ALU.min, ALU.max).then_inc(xstep, 1)
        yield
        v.wait_ge(xstep, XS * b + 5)
        v.tensor_scalar(self.xq[:, :, :], self.xr2[:, :, :], ROUND, -ROUND, ALU.add, ALU.add).then_inc(self.xq_done, 1)
        v.tensor_tensor(back[:, :, 0:2], self.amax[:, :].unsqueeze(2).to_broadcast([128, QT, 2]),
                        wmean[:, 0:2].unsqueeze(1).to_broadcast([128, QT, 2]), ALU.mult).then_inc(xstep, 1)
        yield
        v.wait_ge(xstep, XS * b + 6)
        yield
        nrm.take_moments(v, b + 1)
        yield
        h, hr, hmax = self.h, self.hr, self.hmax
        for t in range(QT):
            hs = HS * (QT * b + t)
            v.wait_ge(self.u_filled, QT * b + t + 1)
            v.wait_ge(self.gate_done, QT * b + t + 1)
            v.scalar_tensor_tensor(h[:, t, :], self.ups[:, :], back[:, t, 1:2], self.gate[:, t, :],
                                   ALU.mult, ALU.mult).then_inc(self.h_done, 1)
            yield
            v.wait_ge(self.h_done, QT * b + t + 2)
            v.tensor_reduce(hmax[:, t:t + 1], h[:, t, :], AX.X, ALU.max, apply_absolute_value=True)\
                .then_inc(hstep, 1)
            yield
            v.wait_ge(hstep, hs + 1)
            v.tensor_scalar(hmax[:, t:t + 1], hmax[:, t:t + 1], 1e-5, 1.0 / 127.0, ALU.max, ALU.mult)\
                .then_inc(hstep, 1)
            yield
            v.wait_ge(hstep, hs + 2)
            v.reciprocal(self.hscale[:, t:t + 1], hmax[:, t:t + 1]).then_inc(hstep, 1)
            v.tensor_tensor(back[:, t, 2:3], hmax[:, t:t + 1], wmean[:, 2:3], ALU.mult).then_inc(hstep, 1)
            yield
            v.wait_ge(hstep, hs + 4)
            v.tensor_scalar(hr[:, t, :], h[:, t, :], self.hscale[:, t:t + 1], 127.0, ALU.mult, ALU.min)\
                .then_inc(hstep, 1)
            yield
            v.wait_ge(hstep, hs + 5)
            v.tensor_scalar(hr[:, t, :], hr[:, t, :], -128.0, ROUND, ALU.max, ALU.add).then_inc(hstep, 1)
            yield
            v.wait_ge(hstep, hs + 6)
            v.tensor_scalar(self.hq[:, t, :], hr[:, t, :], -ROUND, None, ALU.add).then_inc(self.hq_done, 1)
            yield
        nrm.norm_rows(v, b + 1)
        yield
        v.wait_ge(self.y_filled, b + 1)
        for t in range(QT):
            v.scalar_tensor_tensor(x[:, QT * c + t, :], self.yps[:, t * 128:t * 128 + 128], back[:, t, 2:3],
                                   x[:, QT * c + t, :], ALU.mult, ALU.add).then_inc(self.y_done, 1)
        yield


def L1_ffn(nc, g, wts):
    LANES = 2
    F = L1_ffn_lane.F
    st = Stage(nc, "l1f")
    wf, loaded = wts.sb, wts.loaded
    wq = st.sb("wq", [128, 3, F], BF16)
    ones = st.sb("ones", [128, 128])
    wabs = st.sb("wabs", [128, 3])
    wmean = st.sb("wmean", [128, 3])
    wscale = st.sb("wscale", [128, 3])
    ones_set, wabs_done, wsum_done = st.sem("ones_set"), st.sem("wabs_done"), st.sem("wsum_done")
    wstep = st.sem("wstep")
    lanes = [L1_ffn_lane(st, n, LANES, g, wq, wmean) for n in range(LANES)]
    yps = lanes[0].yps

    with nc.Block("l1f_block") as block:
        @block.sync
        def _(sp):
            for ln in lanes:
                sp.sem_inc(ln.h_done, 1)
                sp.sem_inc(ln.hT_done, QT)
                sp.sem_inc(ln.y_done, QT)

        @block.gpsimd
        def _(pool):
            pool.memset(ones[:, :], 1.0).then_inc(ones_set, 1)
            for ln in lanes:
                ln.nrm.pool_setup(pool)
            for ln in lanes:
                ln.nrm.pool(pool, 0)
            with pool.Fori(0, B // LANES) as i:
                in_turn(*(ln.pool(pool, i) for ln in lanes))

        @block.tensor
        def _(pe):
            pe.wait_ge(ones_set, 1)
            pe.wait_ge(wabs_done, 1)
            pe.matmul(yps[:, 0:3], ones[:, :], wabs[:, :], start=True, stop=True).then_inc(wsum_done, 1)
            pe.wait_ge(wstep, 12)
            with pe.Fori(0, B // LANES) as i:
                in_turn(*(ln.tensor(pe, i) for ln in lanes))

        @block.scalar
        def _(act):
            with act.Fori(0, B // LANES) as i:
                in_turn(*(ln.scalar(act, i) for ln in lanes))

        @block.vector
        def _(v):
            v.wait_ge(loaded, 16)
            v.tensor_reduce(wabs[:, :], wf[:, :].rearrange("p (a f) -> p a f", a=3), AX.X, ALU.add, apply_absolute_value=True).then_inc(wabs_done, 1)
            v.wait_ge(wsum_done, 1)
            v.tensor_scalar(wmean[:, :], yps[:, 0:3], 1.0 / (F * D), 1e-5, ALU.mult, ALU.max).then_inc(wstep, 1)
            v.wait_ge(wstep, 1)
            v.reciprocal(wscale[:, :], wmean[:, :]).then_inc(wstep, 2)
            v.wait_ge(wstep, 3)
            for n in range(3):
                v.tensor_scalar(wf[:, n * F:(n + 1) * F], wf[:, n * F:(n + 1) * F], wscale[:, n:n + 1], ROUND, ALU.mult, ALU.add).then_inc(wstep, 1)
                v.wait_ge(wstep, 3 * n + 4)
                v.tensor_scalar(wf[:, n * F:(n + 1) * F], wf[:, n * F:(n + 1) * F], -ROUND, 1.0, ALU.add, ALU.min).then_inc(wstep, 1)
                v.wait_ge(wstep, 3 * n + 5)
                v.tensor_scalar(wq[:, n, :], wf[:, n * F:(n + 1) * F], -1.0, None, ALU.max).then_inc(wstep, 1)
            for ln in lanes:
                ln.nrm.take_moments(v, 0)
            for ln in lanes:
                ln.nrm.norm_rows(v, 0)
            with v.Fori(0, B // LANES) as i:
                in_turn(*(ln.vector(v, i) for ln in lanes))
    st.close()


def L1_attn(nc, g, wts):
    x, ident = g["x"], g["ident"]
    NS = 16
    HB = B // 2
    LANES = 4
    AHEAD = 2
    NB = 4
    YB = NT * D // 512
    st = Stage(nc, "l1a")
    w, loaded = wts.of, wts.loaded
    u = st.sb("u", [128, B, S])
    dt = st.sb("dt", [128, B, S])
    A = st.sb("A", [128, NS])
    BA = st.sb("BA", [128, NS])
    CBA = st.sb("CBA", [128, NS])
    cols = st.sb("cols", [128, NS, 3])
    cur = [st.sb(f"cur{i}", [128, 3]) for i in range(NB)]
    diag = [st.sb(f"diag{i}", [128, 128]) for i in range(NB)]
    diag_D = st.sb("diag_D", [128, 128])
    decay = [st.sb(f"decay{i}", [128, HB, S]) for i in range(NB)]
    th = [st.sb(f"th{i}", [128, HB, S]) for i in range(NB)]
    state = [st.sb(f"state{i}", [128, HB, S]) for i in range(2)]
    lanes = [Lane(st, n, LANES) for n in range(LANES)]
    norms = [Norm(ln, x) for ln in lanes]
    turn_ps = [ln.ps("ps") for ln in lanes]
    t_filled = [ln.sem("t_filled") for ln in lanes]
    u_done = [ln.sem("u_done") for ln in lanes]
    d_filled = [ln.sem("d_filled") for ln in lanes]
    d_left = [ln.sem("d_left") for ln in lanes]
    yps = [st.ps(f"y{i}") for i in range(YB)]
    aset, dt_exp, dt_done = st.sem("aset"), st.sem("dt_exp"), st.sem("dt_done")
    decay_done, th_done, coef_done = st.sem("decay_done"), st.sem("th_done"), st.sem("coef_done")
    drive_done, reset_done, state_done = st.sem("drive_done"), st.sem("reset_done"), st.sem("state_done")
    summed, cols_done, cur_done, diag_done = st.sem("summed"), st.sem("cols_done"), st.sem("cur_done"), st.sem("diag_done")
    added = st.sem("added")

    def y_of(batch, t):
        n = QT * batch + t
        return yps[n // 4][:, n % 4 * 128:n % 4 * 128 + 128]

    def all_units(eng, unit):
        with eng.Fori(0, NS // NB) as m:
            for s in range(NB):
                for hf in range(2):
                    unit(NB * m + s, s, hf)

    with nc.Block("l1a_block") as block:
        @block.sync
        def _(sp):
            sp.sem_inc(state_done, NB)
            sp.sem_inc(summed, 2)
            for ln in range(LANES):
                sp.sem_inc(d_left[ln], 1)

        @block.gpsimd
        def _(pool):
            for nrm in norms:
                nrm.pool_setup(pool)
            with pool.Fori(0, B // LANES) as b:
                for nrm in norms:
                    nrm.pool(pool, b)
            for ln in range(LANES):
                pool.wait_ge(u_done[ln], B // LANES)

            def unit(n, s, hf):
                i = 2 * n + hf
                buf = th[(2 * s + hf) % NB]
                pool.wait_ge(coef_done, i + 1)
                pool.tensor_tensor(buf[:, :, :], buf[:, :, :], u[:, HB * hf:HB * hf + HB, :], ALU.mult)\
                    .then_inc(drive_done, 1)

            all_units(pool, unit)

        @block.tensor
        def _(pe):
            pe.wait_ge(loaded, 16)
            with pe.Fori(0, B // LANES) as b:
                for ln in range(LANES):
                    norms[ln].wait(pe, b)
                    pe.wait_ge(d_left[ln], b + 1)
                    for t in range(QT):
                        mm = pe.transpose(turn_ps[ln][:, t * 128:t * 128 + 128], norms[ln].xn[:, t, :], ident[:, :])
                    mm.then_inc(t_filled[ln], 1)
                for ln in range(LANES):
                    pe.wait_ge(u_done[ln], b + 1)
                    pe.matmul(turn_ps[ln][:, S:2 * S], w("dt"), u[:, lanes[ln].batch(b), :], start=True, stop=True)\
                        .then_inc(d_filled[ln], 1)
            pe.wait_ge(cols_done, 3)
            for batch in range(B):
                for t in range(QT):
                    mm = pe.matmul(y_of(batch, t), u[:, batch, t * 128:t * 128 + 128], diag_D[:, :],
                                   start=(QT * batch + t) % 4 == 0, stop=False, skip_group_check=True)

            def unit(n, s, hf):
                i = 2 * n + hf
                pe.wait_ge(state_done, i + 1 + NB)
                pe.wait_ge(diag_done, n + 1)
                for bb in range(HB):
                    for t in range(QT):
                        mm = pe.matmul(y_of(HB * hf + bb, t), state[hf][:, bb, t * 128:t * 128 + 128], diag[s][:, :],
                                       start=False, stop=True, skip_group_check=True)
                mm.then_inc(summed, 1)

            all_units(pe, unit)

        @block.scalar
        def _(act):
            act.wait_ge(aset, 1)
            act.activation(A[:, :], A[:, :], ACT.Exp).then_inc(aset, 1)
            for ln in range(LANES):
                act.wait_ge(d_left[ln], B // LANES + 1)
            act.activation(dt[:, :, :], dt[:, :, :], ACT.Exp).then_inc(dt_exp, 1)
            act.wait_ge(dt_done, 1)

            def unit(n, s, hf):
                i = 2 * n + hf
                rows = dt[:, HB * hf:HB * hf + HB, :]
                act.wait_ge(cur_done, n + 1)
                act.wait_ge(state_done, i + 1)
                k = (2 * s + hf) % NB
                act.activation(decay[k][:, :, :], rows, ACT.Exp, scale=cur[s][:, 0:1]).then_inc(decay_done, 1)
                act.activation(th[k][:, :, :], rows, ACT.Tanh, scale=cur[s][:, 1:2]).then_inc(th_done, 1)

            all_units(act, unit)

        @block.vector
        def _(v):
            v.wait_ge(loaded, 16)
            v.tensor_scalar(A[:, :], w("A"), 88.5, None, ALU.min).then_inc(aset, 1)
            v.wait_ge(aset, 2)
            v.tensor_scalar(A[:, :], A[:, :], -1.0, None, ALU.mult).then_inc(aset, 1)
            v.wait_ge(aset, 3)
            v.reciprocal(BA[:, :], A[:, :]).then_inc(aset, 1)
            v.wait_ge(aset, 4)
            v.tensor_tensor(BA[:, :], BA[:, :], w("B"), ALU.mult).then_inc(aset, 1)
            v.wait_ge(aset, 5)
            v.tensor_tensor(CBA[:, :], BA[:, :], w("C"), ALU.mult).then_inc(aset, 1)
            v.tensor_copy(cols[:, :, 0], A[:, :]).then_inc(cols_done, 1)
            v.tensor_scalar(cols[:, :, 1], A[:, :], 0.5, None, ALU.mult)
            v.tensor_scalar(diag_D[:, :], ident[:, :], w("D"), None, ALU.mult).then_inc(cols_done, 1)
            v.wait_ge(aset, 6)
            v.tensor_copy(cols[:, :, 2], CBA[:, :]).then_inc(cols_done, 1)
            v.wait_ge(cols_done, 3)
            for n in range(NB - 1):
                v.tensor_copy(cur[n][:, :], cols[:, n, :]).then_inc(cur_done, 1)
            v.wait_ge(cur_done, NB - 1)
            for n in range(NB - 1):
                v.tensor_scalar(diag[n][:, :], ident[:, :], cur[n][:, 2:3], None, ALU.mult).then_inc(diag_done, 1)
            with v.Fori(0, B // LANES) as b:
                for nrm in norms:
                    nrm.take_moments(v, b)
                for nrm in norms:
                    nrm.norm_rows(v, b)
                for ln in range(LANES):
                    v.wait_ge(t_filled[ln], b + 1)
                    v.tensor_scalar(u[:, lanes[ln].batch(b), :], turn_ps[ln][:, 0:S], 1.0, None, ALU.mult)\
                        .then_inc(u_done[ln], 1)
                for ln in range(LANES):
                    v.wait_ge(d_filled[ln], b + 1)
                    v.tensor_scalar(dt[:, lanes[ln].batch(b), :], turn_ps[ln][:, S:2 * S], w("bdt"), 0.0, ALU.add, ALU.min)\
                        .then_inc(d_left[ln], 1)
            v.wait_ge(dt_exp, 1)
            v.tensor_scalar(dt[:, :, :], dt[:, :, :], 0.001, 0.02, ALU.max, ALU.min).then_inc(dt_done, 1)

            def coefficient(i, k):
                v.wait_ge(decay_done, i + 1)
                v.wait_ge(th_done, i + 1)
                v.scalar_tensor_tensor(th[k][:, :, :], decay[k][:, :, :], 1.0, th[k][:, :, :],
                                       ALU.add, ALU.mult).then_inc(coef_done, 1)

            def reset(i, k):
                v.wait_ge(coef_done, i + 1)
                v.memset(decay[k][:, :, 0:1], 0.0).then_inc(reset_done, 1)

            def four_states(m, last):
                for s in range(NB):
                    n = NB * m + s
                    for hf in range(2):
                        i, k = 2 * n + hf, (2 * s + hf) % NB
                        more = not last or 2 * s + hf + AHEAD < 2 * NB
                        if more:
                            coefficient(i + AHEAD, (k + AHEAD) % NB)
                        v.wait_ge(summed, i + 1)
                        v.wait_ge(drive_done, i + 1)
                        v.wait_ge(reset_done, i + 1)
                        v.tensor_tensor_scan(state[hf][:, :, :].rearrange("p b s -> p (b s)"),
                                             decay[k][:, :, :].rearrange("p b s -> p (b s)"),
                                             th[k][:, :, :].rearrange("p b s -> p (b s)"), 0.0, ALU.mult, ALU.add)\
                            .then_inc(state_done, 1)
                        if more:
                            reset(i + AHEAD, (k + AHEAD) % NB)
                        if not last or s + NB - 1 < NB:
                            c = (s + NB - 1) % NB
                            if hf == 0:
                                v.tensor_scalar(cur[c][:, :], cols[:, n + NB - 1, :], 1.0, None, ALU.mult)\
                                    .then_inc(cur_done, 1)
                            else:
                                v.wait_ge(cur_done, n + NB)
                                v.wait_ge(summed, 2 * n + 2)
                                v.tensor_scalar(diag[c][:, :], ident[:, :], cur[c][:, 2:3], None, ALU.mult)\
                                    .then_inc(diag_done, 1)

            for i in range(AHEAD):
                coefficient(i, i)
                reset(i, i)
            with v.Fori(0, NS // NB - 1) as m:
                four_states(m, False)
            four_states(NS // NB - 1, True)
            v.wait_ge(summed, 2 * NS + 2)
            for n in range(YB):
                v.tensor_tensor(x[:, 4 * n:4 * n + 4, :], x[:, 4 * n:4 * n + 4, :],
                                yps[n][:, :].rearrange("p (t f) -> p t f", t=4), ALU.add).then_inc(added, 1)
    st.close()




class L2_ffn_lane:
    C, HI = S // 2, 4
    NI = H // HI
    SR = 2
    XT, GATE, PICK, QK, V, SELT, ITEM = 0, 1, 2, 3, 4, 5, 6
    AV, SUM, PROJ, BACK = ITEM + NI, ITEM + NI + 1, ITEM + NI + 2, ITEM + NI + 3
    GS = 5

    def __init__(self, st, lane, lanes, g, w):
        self.g, self.w = g, w
        C, NI, HI = self.C, self.NI, self.HI
        st = Lane(st, lane, lanes)
        self.batch = st.batch
        self.T = Ring(st, "t", 2, self.BACK + 1)
        self.scores = [st.ps(f"s{i}") for i in range(self.SR)]
        self.nrm = Norm(st, g["x"])
        self.xnT = st.sb("xnT", [128, S])
        self.gates = st.sb("gates", [128, S])
        self.junk = st.sb("junk", [128, 3 * QT, S])
        self.own = st.sb("own", [128, QT])
        self.above = st.sb("above", [128, QT])
        self.equal = st.sb("equal", [128, QT])
        self.rank = st.sb("rank", [128, QT])
        self.sel = st.sb("sel", [128, QT, C])
        self.selT = st.sb("selT", [C, S])
        self.picked = st.sb("picked", [128, C])
        self.q_sb = st.sb("q", [128, C])
        self.k_sb = st.sb("k", [128, C])
        self.kbd = st.sb("kbd", [128, H, C])
        self.v_sb = st.sb("v", [C, 4, 160])
        self.P = st.sb("p", [128, NI, HI, C])
        self.PT = st.sb("pt", [C, NI, HI, C])
        self.OT = st.sb("ot", [128, C])
        self.o_sb = st.sb("o_sb", [C, D])
        self.top = st.sb("top", [128, NI, HI])
        self.over = st.sb("over", [128, C])
        self.v_set, self.gstep, self.sel_done = st.sem("v_set"), st.sem("gstep"), st.sem("sel_done")
        self.kbd_vector, self.kbd_pool = st.sem("kbd_vector"), st.sem("kbd_pool")
        self.s_filled, self.top_done = st.sem("s_filled"), st.sem("top_done")
        self.sub_done, self.exp_done = st.sem("sub_done"), st.sem("exp_done")

    def lone_keys(self, eng, i):
        h, n = self.HI * i, self.HI
        return eng.tensor_tensor(self.kbd[:, h:h + n, :], self.k_sb[:, :].unsqueeze(1).to_broadcast([128, n, self.C]),
                                 self.w("kmask")[:, h:h + n].unsqueeze(2).to_broadcast([128, n, self.C]), ALU.mult)

    def pool(self, pool, b):
        T, NI = self.T, self.NI
        for _ in range(4):
            yield
        T.wait_emptied(pool, b, self.QK)
        for i in (2, 3):
            self.lone_keys(pool, i).then_inc(self.kbd_pool, 1)
        yield
        for s in range(NI + 2):
            if s == NI:
                self.nrm.pool(pool, b + 1)
            yield

    def tensor(self, pe, b):
        T, C, HI, NI, w, ident, sel = self.T, self.C, self.HI, self.NI, self.w, self.g["ident"], self.sel
        XT, GATE, PICK, QK, V, SELT, ITEM = self.XT, self.GATE, self.PICK, self.QK, self.V, self.SELT, self.ITEM
        self.nrm.wait(pe, b)
        T.wait_free(pe, b, XT)
        for t in range(QT):
            mm = pe.transpose(T.bank(XT)[:, t * 128:t * 128 + 128], self.nrm.xn[:, t, :], ident[:, :])
        mm.then_inc(T.full(XT), 1)
        yield
        T.wait_emptied(pe, b, XT)
        T.wait_free(pe, b, GATE)
        pe.matmul(T.bank(GATE)[:, 0:S], w("gate"), self.xnT[:, :], start=True, stop=True).then_inc(T.full(GATE), 1)
        yield
        yield
        pe.wait_ge(self.sel_done, QT * b + QT)
        for t in range(QT):
            mm = pe.matmul(T.bank(PICK)[:, 0:C], self.nrm.xn[:, t, :], sel[:, t, :], start=(t == 0),
                           stop=(t == QT - 1))
        mm.then_inc(T.full(PICK), 1)
        yield
        T.wait_emptied(pe, b, PICK)
        T.wait_free(pe, b, QK)
        for n, key in enumerate("qk"):
            mm = pe.matmul(T.bank(QK)[:, n * C:(n + 1) * C], w(key), self.picked[:, :], start=True, stop=True)
        mm.then_inc(T.full(QK), 1)
        pe.matmul(T.bank(V)[:, 0:D], self.picked[:, :], w("v"), start=True, stop=True).then_inc(T.full(V), 1)
        T.wait_free(pe, b, SELT)
        for t in range(QT):
            mm = pe.transpose(T.bank(SELT)[:, t * 128:t * 128 + 128], sel[:, t, :], ident[:, :])
        mm.then_inc(T.full(SELT), 1)
        yield
        for s in range(NI + 2):
            if s < NI:
                pe.wait_ge(self.kbd_vector if s < 2 else self.kbd_pool, 2 * b + s % 2 + 1)
                pe.wait_ge(self.sub_done, b * NI + s + 1)
                pe.matmul(self.scores[s % self.SR][:, :], self.q_sb[:, :], self.kbd[:, s * HI:s * HI + HI, :],
                          start=True, stop=True).then_inc(self.s_filled, 1)
            i = s - 2
            if i >= 0:
                pe.wait_ge(self.exp_done, b * NI + i + 1)
                T.wait_free(pe, b, ITEM + i)
                for m in range(HI):
                    mm = pe.transpose(T.bank(ITEM + i)[:, m * C:m * C + C], self.P[:, i, m, :], ident[:, :])
                mm.then_inc(T.full(ITEM + i), 1)
            yield
        T.wait_emptied(pe, b, self.AV - 2)
        T.wait_emptied(pe, b, self.AV - 1)
        for k, left in ((self.AV, lambda i: self.v_sb[:, i, :]), (self.SUM, lambda i: w("ones"))):
            T.wait_free(pe, b, k)
            for i in range(NI):
                for m in range(HI):
                    mm = pe.matmul(T.bank(k)[32 * i:32 * i + 32, 0:C], left(i)[:, 32 * m:32 * m + 32],
                                   self.PT[:, i, m, :], start=(m == 0), stop=(m == HI - 1),
                                   tile_position=(0, 32 * i))
            mm.then_inc(T.full(k), 1)
        yield
        T.wait_emptied(pe, b, self.AV)
        T.wait_free(pe, b, self.PROJ)
        pe.matmul(T.bank(self.PROJ)[:, 0:D], self.OT[:, :], w("o"), start=True, stop=True)\
            .then_inc(T.full(self.PROJ), 1)
        yield
        T.wait_emptied(pe, b, self.PROJ)
        for t in range(QT):
            mm = pe.matmul(T.bank(self.BACK)[:, t * D:t * D + D], self.selT[:, t * 128:t * 128 + 128], self.o_sb[:, :],
                           start=True, stop=True)
        mm.then_inc(T.full(self.BACK), 1)
        yield

    def scalar(self, act, b):
        T, C, HI, NI = self.T, self.C, self.HI, self.NI
        XT, GATE, PICK, QK, SELT, ITEM = self.XT, self.GATE, self.PICK, self.QK, self.SELT, self.ITEM
        T.wait_filled(act, b, XT)
        act.activation(self.xnT[:, :], T.bank(XT)[:, 0:S], ACT.Copy).then_inc(T.free(XT), 1)
        yield
        T.wait_filled(act, b, GATE)
        act.activation(self.gates[:, :], T.bank(GATE)[:, 0:S], ACT.Exp, scale=-1.0).then_inc(T.free(GATE), 1)
        yield
        yield
        T.wait_filled(act, b, PICK)
        act.activation(self.picked[:, :], T.bank(PICK)[:, 0:C], ACT.Copy).then_inc(T.free(PICK), 1)
        yield
        T.wait_filled(act, b, QK)
        act.activation(self.q_sb[:, :], T.bank(QK)[:, 0:C], ACT.Copy, scale=(D // H) ** -0.5)
        act.activation(self.k_sb[:, :], T.bank(QK)[:, C:2 * C], ACT.Copy).then_inc(T.free(QK), 1)
        T.wait_filled(act, b, SELT)
        act.activation(self.selT[:, :], T.bank(SELT)[:, 0:S], ACT.Copy).then_inc(T.free(SELT), 1)
        yield
        for s in range(NI + 2):
            i = s - 2
            if i >= 0:
                T.wait_filled(act, b, ITEM + i)
                act.activation(self.PT[:, i, :, :], T.bank(ITEM + i)[:, :].rearrange("p (m q) -> p m q", m=HI), ACT.Copy)\
                    .then_inc(T.free(ITEM + i), 1)
            i = s - 1
            if 0 <= i < NI:
                act.wait_ge(self.sub_done, b * NI + i + 1 + self.SR)
                act.activation(self.P[:, i, :, :], self.P[:, i, :, :], ACT.Exp).then_inc(self.exp_done, 1)
            yield
        yield
        T.wait_filled(act, b, self.PROJ)
        act.activation(self.o_sb[:, :], T.bank(self.PROJ)[:, 0:D], ACT.Copy).then_inc(T.free(self.PROJ), 1)
        yield
        yield

    def vector(self, v, b):
        T, C, HI, NI, GS, w, ident = self.T, self.C, self.HI, self.NI, self.GS, self.w, self.g["ident"]
        gates, gstep, own, junk = self.gates, self.gstep, self.own, self.junk
        x, c, d = self.g["x"], self.batch(b), D // H
        yield
        yield
        T.wait_emptied(v, b, self.GATE)
        v.tensor_scalar(gates[:, :], gates[:, :], 1.0, None, ALU.add).then_inc(gstep, 1)
        v.wait_ge(gstep, GS * b + 1)
        v.reciprocal(gates[:, :], gates[:, :]).then_inc(gstep, 1)
        v.wait_ge(gstep, GS * b + 2)
        for t in range(QT):
            o = v.scalar_tensor_tensor(junk[:, t, 0:128], gates[:, t * 128:t * 128 + 128], 1.0, ident[:, :],
                                       ALU.mult, ALU.mult, accum_out=own[:, t:t + 1])
        o.then_inc(gstep, 1)
        v.wait_ge(gstep, GS * b + 3)
        for t in range(QT):
            v.tensor_scalar(junk[:, QT + t, :], gates[:, :], own[:, t:t + 1], 0.0, ALU.is_gt, ALU.add,
                            accum_out=self.above[:, t:t + 1])
            e = v.scalar_tensor_tensor(junk[:, 2 * QT + t, :], gates[:, :], own[:, t:t + 1],
                                       w("before")[:, t * S:t * S + S], ALU.is_equal, ALU.mult,
                                       accum_out=self.equal[:, t:t + 1])
        e.then_inc(gstep, 1)
        v.wait_ge(gstep, GS * b + 4)
        v.tensor_tensor(self.rank[:, :], self.above[:, :], self.equal[:, :], ALU.add).then_inc(gstep, 1)
        v.wait_ge(gstep, GS * b + 5)
        for t in range(QT):
            v.tensor_scalar(self.sel[:, t, :], w("iota"), self.rank[:, t:t + 1], None, ALU.is_equal)\
                .then_inc(self.sel_done, 1)
        yield
        yield
        T.wait_emptied(v, b, self.QK)
        for i in (0, 1):
            self.lone_keys(v, i).then_inc(self.kbd_vector, 1)
        T.wait_filled(v, b, self.V)
        v.tensor_copy(self.v_sb[:, :, :].rearrange("p w (j c) -> p w j c", c=40)[:, :, :, 0:d],
                      T.bank(self.V)[:, 0:D].rearrange("p (w j d) -> p w j d", w=4, d=d))\
            .then_inc(T.free(self.V), 1)
        yield
        for s in range(NI + 2):
            i = s
            if i < NI:
                v.wait_ge(self.s_filled, b * NI + i + 1)
                v.tensor_reduce(self.top[:, i, :], self.scores[i % self.SR][:, :].rearrange("p (h k) -> p h k", h=HI),
                                AX.X, ALU.max).then_inc(self.top_done, 1)
            i = s - 1
            if 0 <= i < NI:
                v.wait_ge(self.top_done, b * NI + i + 1)
                v.tensor_tensor(self.P[:, i, :, :], self.scores[i % self.SR][:, :].rearrange("p (h k) -> p h k", h=HI),
                                self.top[:, i, :].unsqueeze(2).to_broadcast([128, HI, C]),
                                ALU.subtract).then_inc(self.sub_done, 1)
            if s == NI:
                self.nrm.take_moments(v, b + 1)
            if s == NI + 1:
                self.nrm.norm_rows(v, b + 1)
            yield
        T.wait_filled(v, b, self.SUM)
        v.reciprocal(self.over[:, :], T.bank(self.SUM)[:, 0:C]).then_inc(T.free(self.SUM), 1)
        T.wait_emptied(v, b, self.SUM)
        v.tensor_tensor(self.OT[:, :], T.bank(self.AV)[:, 0:C], self.over[:, :], ALU.mult).then_inc(T.free(self.AV), 1)
        yield
        yield
        T.wait_filled(v, b, self.BACK)
        for t in range(QT):
            f = v.scalar_tensor_tensor(x[:, QT * c + t, :], T.bank(self.BACK)[:, t * D:t * D + D], own[:, t:t + 1],
                                       x[:, QT * c + t, :], ALU.mult, ALU.add)
        f.then_inc(T.free(self.BACK), 1)
        yield


def L2_ffn(nc, g, wts):
    LANES = 2
    st = Stage(nc, "l2f")
    w, loaded = wts.of, wts.loaded

    lanes = [L2_ffn_lane(st, n, LANES, g, w) for n in range(LANES)]

    with nc.Block("l2f_block") as block:
        @block.sync
        def _(sp):
            for ln in lanes:
                ln.T.credit(sp)
                sp.sem_inc(ln.sub_done, ln.SR)

        @block.gpsimd
        def _(pool):
            for ln in lanes:
                ln.nrm.pool_setup(pool)
                pool.memset(ln.v_sb[:, :, :], 0.0).then_inc(ln.v_set, 1)
            for ln in lanes:
                ln.nrm.pool(pool, 0)
            pool.wait_ge(loaded, 16)
            with pool.Fori(0, B // LANES) as i:
                in_turn(*(ln.pool(pool, i) for ln in lanes))

        @block.tensor
        def _(pe):
            pe.wait_ge(loaded, 16)
            with pe.Fori(0, B // LANES) as i:
                in_turn(*(ln.tensor(pe, i) for ln in lanes))

        @block.scalar
        def _(act):
            with act.Fori(0, B // LANES) as i:
                in_turn(*(ln.scalar(act, i) for ln in lanes))

        @block.vector
        def _(v):
            v.wait_ge(loaded, 16)
            for ln in lanes:
                v.wait_ge(ln.v_set, 1)
                ln.nrm.take_moments(v, 0)
            for ln in lanes:
                ln.nrm.norm_rows(v, 0)
            with v.Fori(0, B // LANES) as i:
                in_turn(*(ln.vector(v, i) for ln in lanes))
    st.close()


class L3_xattn_lane:
    d, NP = 64, H // 2
    NI = NP * QT
    K = SC + S
    LAG, PR = 2, 3
    XT, Q0 = 0, 1
    K0 = Q0 + 4
    V0 = K0 + NP
    VC0 = V0 + 2 * QT
    I0 = VC0 + 2
    OUT = I0 + 4 * NP

    def __init__(self, st, lane, lanes, g, w, cnT):
        self.g, self.w, self.cnT = g, w, cnT
        NP, K = self.NP, self.K
        st = Lane(st, lane, lanes)
        self.batch = st.batch
        self.T = Ring(st, "t", 2, self.OUT + 1)
        self.scores = st.ps("s", (128, 1024))
        self.nrm = Norm(st, g["x"])
        self.nrm2 = Norm(st, g["x"], of=self.nrm)
        self.xnT = st.sb("xnT", [128, S])
        self.ctx2 = st.sb("ctx2", [128, 2, SC])
        self.q_sb = st.sb("q", [128, NP, S])
        self.k_sb = st.sb("k", [128, NP, K])
        self.v_sb = st.sb("v", [128, QT, H, self.d])
        self.vc = st.sb("vc", [128, NP, 128])
        self.P = [st.sb(f"p{i}", [128, 2, K]) for i in range(self.PR)]
        self.Pc = [st.sb(f"pc{i}", [128, 2, SC]) for i in range(self.PR)]
        self.PT = [st.sb(f"pt{i}", [128, 2, QT, S]) for i in range(2)]
        self.PTc = [st.sb(f"ptc{i}", [128, S]) for i in range(2)]
        self.OT = st.sb("ot", [128, NP, S])
        self.nmax = st.sb("nmax", [128, self.PR, 2])
        self.sums = st.sb("sums", [128, self.PR, 2])
        self.rec = st.sb("rec", [128, self.PR, 2])
        self.ctx2_done, self.vc_half, self.v_set = st.sem("ctx2_done"), st.sem("vc_half"), st.sem("v_set")
        self.s_filled, self.max_done, self.exp_done = st.sem("s_filled"), st.sem("max_done"), st.sem("exp_done")
        self.rec_done, self.p_done, self.added = st.sem("rec_done"), st.sem("p_done"), st.sem("added")

    def keys_of(self, qt):
        return SC + 128 * (qt + 1)

    def use_of(self, u, n):
        return self.I0 + 4 * u + n

    def sync_setup(self, sp):
        self.T.credit(sp)
        sp.sem_inc(self.exp_done, 1)

    def pool_setup(self, pool):
        self.nrm.pool_setup(pool)
        self.nrm2.pool_setup(pool)
        pool.memset(self.vc[:, :, :], 0.0).then_inc(self.v_set, 1)

    def pool(self, pool, b):
        for _ in range(self.I0):
            yield
        for s in range(self.NI + self.LAG + 1):
            i = s - 1
            if 0 <= i < self.NI:
                n, m = self.keys_of(i % QT), i % self.PR
                P, by = self.P[m], self.rec[:, m, :].unsqueeze(2)
                pool.wait_ge(self.rec_done, b * self.NI + i + 1)
                pool.tensor_tensor(self.Pc[m][:, :, :], P[:, :, 0:SC], by.to_broadcast([128, 2, SC]), ALU.mult)
                pool.tensor_tensor(P[:, :, SC:n], P[:, :, SC:n], by.to_broadcast([128, 2, n - SC]),
                                   ALU.mult).then_inc(self.p_done, 1)
            if s == self.NI - 1:
                self.nrm.pool(pool, b + 1)
            if s == self.NI + 1:
                self.nrm2.pool(pool, b + 1)
            yield

    def tensor(self, pe, b):
        T, w, g, xnT, NI, NP, LAG, K = self.T, self.w, self.g, self.xnT, self.NI, self.NP, self.LAG, self.K
        ident, c0 = g["ident"], self.batch(b)
        self.nrm2.wait(pe, b)
        T.wait_free(pe, b, self.XT)
        for t in range(QT):
            mm = pe.transpose(T.bank(self.XT)[:, t * 128:t * 128 + 128], self.nrm2.xn[:, t, :], ident[:, :])
        mm.then_inc(T.full(self.XT), 1)
        yield
        T.wait_emptied(pe, b, self.XT)
        for n in range(4):
            k = self.Q0 + n
            T.wait_free(pe, b, k)
            for j in range(2):
                c = 2 * n + j
                mm = pe.matmul(T.bank(k)[:, j * S:(j + 1) * S], w("q")[:, c * 128:c * 128 + 128],
                               xnT[:, :], start=True, stop=True)
            mm.then_inc(T.full(k), 1)
            yield
        for c in range(NP):
            k = self.K0 + c
            T.wait_free(pe, b, k)
            wk = w("k")[:, c * 128:c * 128 + 128]
            pe.matmul(T.bank(k)[:, 0:SC], wk, self.cnT[:, c0, :], start=True, stop=True)
            pe.matmul(T.bank(k)[:, SC:K], wk, xnT[:, :], start=True, stop=True).then_inc(T.full(k), 1)
            yield
        for n in range(2 * QT):
            t, hf = divmod(n, 2)
            k = self.V0 + n
            T.wait_free(pe, b, k)
            pe.matmul(T.bank(k)[:, :], xnT[:, t * 128:t * 128 + 128], w("v")[:, hf * 512:hf * 512 + 512],
                      start=True, stop=True).then_inc(T.full(k), 1)
            yield
        pe.wait_ge(self.ctx2_done, b + 1)
        for hf in range(2):
            k = self.VC0 + hf
            T.wait_free(pe, b, k)
            pe.matmul(T.bank(k)[:, :], self.ctx2[:, :, :], w("v")[:, hf * 512:hf * 512 + 512],
                      start=True, stop=True).then_inc(T.full(k), 1)
            yield
        T.wait_emptied(pe, b, self.VC0 - 2)
        T.wait_emptied(pe, b, self.VC0 - 1)
        for i in range(NI + LAG + 1):
            if i < NI:
                u, qt = divmod(i, QT)
                n = self.keys_of(qt)
                pe.wait_ge(self.exp_done, b * NI + i + 1)
                for j in range(2):
                    so = self.scores[:, j * 512:j * 512 + n]
                    lo = self.d * j
                    pe.matmul(so, self.q_sb[lo:lo + 64, u, qt * 128:qt * 128 + 128], self.k_sb[lo:lo + 64, u, 0:n],
                              start=True, stop=False, tile_position=(lo, 0))
                    pe.matmul(so[:, n - 128:n], g["identb"][:, :], g["tri"][:, :], start=False, stop=False)
                    mm = pe.matmul(so[:, 0:SC], g["onesb"][:, :], g["hide"][:, c0, :], start=False, stop=True)
                mm.then_inc(self.s_filled, 1)
            j = i - LAG - 1
            if j >= 0 and j % QT == QT - 1:
                self.products(pe, b, j // QT)
            j = i - LAG
            if 0 <= j < NI:
                u, qt = divmod(j, QT)
                nb = qt + 1
                k = self.use_of(u, qt)
                pe.wait_ge(self.p_done, b * NI + j + 1)
                T.wait_free(pe, b, k)
                for hh in range(2):
                    for kt in range(nb):
                        at = (hh * nb + kt) * 128
                        mm = pe.transpose(T.bank(k)[:, at:at + 128],
                                          self.P[j % self.PR][:, hh, SC + kt * 128:SC + kt * 128 + 128], ident[:, :])
                if qt == 1:
                    mm.then_inc(T.full(k), 1)
                    k += 1
                    T.wait_free(pe, b, k)
                at = 256 if qt == 0 else 0
                pe.transpose(T.bank(k)[:, at:at + 128], self.Pc[j % self.PR][:, :, :].rearrange("p j k -> p (j k)"),
                             ident[:, :]).then_inc(T.full(k), 1)
            yield
        k = self.OUT
        T.wait_emptied(pe, b, k - 1)
        T.wait_free(pe, b, k)
        for t in range(QT):
            for u in range(NP):
                mm = pe.matmul(T.bank(k)[:, t * 128:t * 128 + 128], self.OT[:, u, t * 128:t * 128 + 128],
                               w("o")[:, u * 128:u * 128 + 128], start=(u == 0), stop=(u == NP - 1))
        mm.then_inc(T.full(k), 1)
        yield

    def products(self, pe, b, u):
        T, k = self.T, self.use_of(u, 3)
        T.wait_emptied(pe, b, k - 2)
        T.wait_emptied(pe, b, k - 1)
        T.wait_free(pe, b, k)
        o = T.bank(k)
        pe.matmul(o[:, 0:S], self.vc[:, u, :], self.PTc[u % 2][:, :], start=True, stop=False, skip_group_check=True)
        for hh in range(2):
            for kt in range(QT):
                mm = pe.matmul(o[64 * hh:64 * hh + 64, 128 * kt:S], self.v_sb[:, kt, 2 * u + hh, :],
                               self.PT[u % 2][:, hh, kt, 128 * kt:S], start=False, stop=(kt == QT - 1),
                               tile_position=(0, 64 * hh), skip_group_check=True)
        mm.then_inc(T.full(k), 1)

    def scalar(self, act, b):
        T, w, NI, LAG, K = self.T, self.w, self.NI, self.LAG, self.K
        T.wait_filled(act, b, self.XT)
        act.activation(self.xnT[:, :], T.bank(self.XT)[:, 0:S], ACT.Identity, scale=w("g1"), bias=w("b1"))\
            .then_inc(T.free(self.XT), 1)
        yield
        for n in range(4):
            k = self.Q0 + n
            T.wait_filled(act, b, k)
            act.activation(self.q_sb[:, 2 * n:2 * n + 2, :], T.bank(k)[:, :].rearrange("p (c q) -> p c q", c=2),
                           ACT.Copy, scale=self.d ** -0.5).then_inc(T.free(k), 1)
            yield
        for c in range(self.NP):
            if c % 2:
                T.wait_filled(act, b, self.K0 + c)
                act.activation(self.k_sb[:, c, :], T.bank(self.K0 + c)[:, 0:K], ACT.Copy).then_inc(T.free(self.K0 + c), 1)
            yield
        for n in range(2 * QT):
            t, hf = divmod(n, 2)
            k = self.V0 + n
            T.wait_filled(act, b, k)
            act.activation(self.v_sb[:, t, 8 * hf:8 * hf + 8, :],
                           T.bank(k)[:, :].rearrange("p (h d) -> p h d", d=self.d), ACT.Copy).then_inc(T.free(k), 1)
            yield
        yield
        yield
        for i in range(NI + LAG + 1):
            if i < NI:
                n, m = self.keys_of(i % QT), i % self.PR
                act.wait_ge(self.max_done, b * NI + i + 1)
                if i >= self.PR:
                    u, qt = divmod(i - self.PR, QT)
                    T.wait_filled(act, b, self.use_of(u, 2 * qt))
                for hh in range(2):
                    e = act.activation(self.P[m][:, hh, 0:n], self.scores[:, hh * 512:hh * 512 + n], ACT.Exp,
                                       bias=self.nmax[:, m, hh:hh + 1], accum_out=self.sums[:, m, hh:hh + 1])
                e.then_inc(self.exp_done, 1)
            j = i - LAG
            if 0 <= j < NI and j % QT == 1:
                self.pt_copy(act, lambda dst, src: act.activation(dst, src, ACT.Copy), b, j // QT, 1)
            yield
        yield

    def pt_copy(self, eng, copy, b, u, qt):
        T, k, nb = self.T, self.use_of(u, qt), qt + 1
        T.wait_filled(eng, b, k)
        if u >= 2:
            T.wait_filled(eng, b, self.use_of(u - 2, 3))
        c = copy(self.PT[u % 2][:, :, 0:nb, qt * 128:qt * 128 + 128],
                 T.bank(k)[:, 0:2 * nb * 128].rearrange("p (j t q) -> p j t q", j=2, t=nb))
        if qt == 1:
            c.then_inc(T.free(k), 1)

    def vector(self, v, b):
        T, w, x, NI, LAG, K, c0 = self.T, self.w, self.g["x"], self.NI, self.LAG, self.K, self.batch(b)
        v.tensor_copy(self.ctx2[:, :, :], self.cnT[:, c0, :].unsqueeze(1).to_broadcast([128, 2, SC]))\
            .then_inc(self.ctx2_done, 1)
        yield
        for n in range(4):
            yield
        for c in range(self.NP):
            if c % 2 == 0:
                T.wait_filled(v, b, self.K0 + c)
                v.tensor_copy(self.k_sb[:, c, :], T.bank(self.K0 + c)[:, 0:K]).then_inc(T.free(self.K0 + c), 1)
            yield
        for n in range(2 * QT):
            yield
        for hf in range(2):
            k = self.VC0 + hf
            T.wait_filled(v, b, k)
            for j in range(2):
                cc = v.tensor_copy(self.vc[64 * j:64 * j + 64, 4 * hf:4 * hf + 4, 64 * j:64 * j + 64],
                                   T.bank(k)[64 * j:64 * j + 64, :]
                                   .rearrange("p (m j e) -> p m j e", j=2, e=self.d)[:, :, j, :])
                if j == 0:
                    cc.then_inc(self.vc_half, 1)
                    v.wait_ge(self.vc_half, 2 * b + hf + 1)
            cc.then_inc(T.free(k), 1)
            yield
        for i in range(NI + LAG + 1):
            j = i - LAG - 1
            if j >= 0 and j % QT == QT - 1:
                u = j // QT
                k = self.use_of(u, 3)
                T.wait_filled(v, b, k)
                v.tensor_copy(self.OT[:, u, :], T.bank(k)[:, 0:S]).then_inc(T.free(k), 1)
            if i < NI:
                n = self.keys_of(i % QT)
                v.wait_ge(self.s_filled, b * NI + i + 1)
                v.tensor_reduce(self.nmax[:, i % self.PR, :],
                                self.scores[:, :].rearrange("p (j k) -> p j k", j=2)[:, :, 0:n],
                                AX.X, ALU.max, negate=True).then_inc(self.max_done, 1)
            j = i - 1
            if 0 <= j < NI:
                v.wait_ge(self.exp_done, b * NI + j + 2)
                v.reciprocal(self.rec[:, j % self.PR, :], self.sums[:, j % self.PR, :]).then_inc(self.rec_done, 1)
            j = i - LAG
            if 0 <= j < NI:
                u, qt = divmod(j, QT)
                if qt == 0:
                    self.pt_copy(v, v.tensor_copy, b, u, qt)
                    k, at = self.use_of(u, 0), 256
                else:
                    k, at = self.use_of(u, 2), 0
                    T.wait_filled(v, b, k)
                v.tensor_copy(self.PTc[u % 2][:, qt * 128:qt * 128 + 128], T.bank(k)[:, at:at + 128])\
                    .then_inc(T.free(k), 1)
            if i == NI - 1:
                self.nrm.take_moments(v, b + 1)
            if i == NI:
                self.nrm.norm_rows(v, b + 1)
            if i == NI + 1:
                self.nrm2.take_moments(v, b + 1)
            if i == NI + 2:
                self.nrm2.norm_rows(v, b + 1)
            yield
        k = self.OUT
        T.wait_filled(v, b, k)
        v.tensor_tensor(x[:, bass.ds(QT * c0, QT), :], x[:, bass.ds(QT * c0, QT), :],
                        T.bank(k)[:, 0:QT * 128].rearrange("p (t f) -> p t f", t=QT),
                        ALU.add).then_inc(T.free(k), 1)
        T.wait_emptied(v, b, k)
        v.tensor_tensor(x[:, bass.ds(QT * c0, QT), :], x[:, bass.ds(QT * c0, QT), :],
                        w("ob").unsqueeze(1).to_broadcast([128, QT, D]), ALU.add).then_inc(self.added, 1)
        yield


def L3_xattn(nc, g, wts):
    LANES = 2
    CT = B * SC // 128
    st = Stage(nc, "l3x")
    w, loaded = wts.of, wts.loaded
    raw = st.sb("raw", [128, CT, D])
    cstats = st.sb("cstats", [128, CT, 6])
    cmv = st.sb("cmv", [128, CT, 2])
    cveps = st.sb("cveps", [128, CT])
    crstd = st.sb("crstd", [128, CT])
    chalf = st.sb("chalf", [128, CT])
    cnT = st.sb("cnT", [128, B, SC])
    raw_in, half_set = st.sem("raw_in"), st.sem("half_set")
    cstep, cfilled, cn_done = st.sem("cstep"), st.sem("cfilled"), st.sem("cn_done")

    lanes = [L3_xattn_lane(st, n, LANES, g, w, cnT) for n in range(LANES)]
    cps = lanes[0].scores

    with nc.Block("l3x_block") as block:
        @block.sync
        def _(sp):
            sp.dma_start(raw[:, :, :], g["dram"]["ctx"].rearrange("(t p) d -> p t d", p=128)).then_inc(raw_in, 16)
            for ln in lanes:
                ln.sync_setup(sp)

        @block.gpsimd
        def _(pool):
            pool.memset(chalf[:, :], -0.5).then_inc(half_set, 1)
            for ln in lanes:
                ln.pool_setup(pool)
            pool.wait_ge(half_set, 1)
            pool.wait_ge(cstep, CT + 1)
            pool.tensor_tensor(crstd[:, :], cveps[:, :], chalf[:, :], ALU.pow).then_inc(cstep, 1)
            for ln in lanes:
                ln.nrm.pool(pool, 0)
            for ln in lanes:
                ln.nrm2.pool(pool, 0)
            with pool.Fori(0, B // LANES) as i:
                in_turn(*(ln.pool(pool, i) for ln in lanes))

        @block.tensor
        def _(pe):
            pe.wait_ge(loaded, 16)
            pe.wait_ge(cstep, 2 * CT + 2)
            for t in range(CT):
                mm = pe.transpose(cps[:, t * 128:t * 128 + 128], raw[:, t, :], g["ident"][:, :])
            mm.then_inc(cfilled, 1)
            pe.wait_ge(cn_done, 1)
            with pe.Fori(0, B // LANES) as i:
                in_turn(*(ln.tensor(pe, i) for ln in lanes))

        @block.scalar
        def _(act):
            act.wait_ge(loaded, 16)
            act.wait_ge(cfilled, 1)
            act.activation(cnT[:, :, :], cps[:, 0:CT * 128].rearrange("p (b k) -> p b k", b=B), ACT.Identity,
                           scale=w("g2"), bias=w("b2")).then_inc(cn_done, 1)
            with act.Fori(0, B // LANES) as i:
                in_turn(*(ln.scalar(act, i) for ln in lanes))

        @block.vector
        def _(v):
            v.wait_ge(loaded, 16)
            v.wait_ge(raw_in, 16)
            for t in range(CT):
                v.bn_stats(cstats[:, t, :], raw[:, t, :])
            v.drain()
            for t in range(CT):
                v.bn_aggr(cmv[:, t, :], cstats[:, t, :]).then_inc(cstep, 1)
            v.wait_ge(cstep, CT)
            v.tensor_scalar(cveps[:, :], cmv[:, :, 1], EPS, None, ALU.add).then_inc(cstep, 1)
            v.wait_ge(cstep, CT + 2)
            for t in range(CT):
                v.tensor_scalar(raw[:, t, :], raw[:, t, :], cmv[:, t, 0:1], crstd[:, t:t + 1], ALU.subtract, ALU.mult)\
                    .then_inc(cstep, 1)
            v.wait_ge(cn_done, 1)
            for ln in lanes:
                v.wait_ge(ln.v_set, 1)
                ln.nrm.take_moments(v, 0)
            for ln in lanes:
                ln.nrm.norm_rows(v, 0)
            for ln in lanes:
                ln.nrm2.take_moments(v, 0)
            for ln in lanes:
                ln.nrm2.norm_rows(v, 0)
            with v.Fori(0, B // LANES) as i:
                in_turn(*(ln.vector(v, i) for ln in lanes))
    st.close()


def L3_ffn(nc, g, wts):
    name = "l3f"
    x, ident = g["x"], g["ident"]
    E, F = 8, 512
    CAP = B * S // E
    FC, ST = F // 128, CAP // 128
    W1, W2 = g["dram"]["L3_ffn_W1"], g["dram"]["L3_ffn_W2"]
    slots = nc.dram_tensor("slots", [E * CAP, D], F32, kind="Internal").ap()
    outs = nc.dram_tensor("outs", [E * CAP, D], F32, kind="Internal").ap()
    st = Stage(nc, name)
    w, loaded = wts.of, wts.loaded
    LANES = 4
    lanes = [Lane(st, n, LANES) for n in range(LANES)]
    norms = [Norm(ln, x) for ln in lanes]
    xn = st.sb("xn_all", [128, NT, D])
    xnT = [ln.sb("xnT", [128, S]) for ln in lanes]
    zeros = st.sb("zeros", [128, NT, D])
    logit = st.sb("logit", [128, NT, E])
    work = st.sb("work", [128, NT, E])
    cand = st.sb("cand", [128, NT, E])
    first = st.sb("first", [128, NT])
    lmax = st.sb("lmax", [128, NT])
    esum = st.sb("esum", [128, NT])
    prob = st.sb("prob", [128, NT])
    hot = st.sb("hot", [128, NT, E])
    hotb = st.sb("hotb", [128, NT, E], BF16)
    below_b = st.sb("below_b", [128, 128], BF16)
    rank = st.sb("rank", [128, NT])
    keep = st.sb("keep", [128, NT])
    weight = st.sb("weight", [128, NT])
    slotf = st.sb("slotf", [128, NT])
    slot = st.sb("slot", [128, NT])
    to_f = st.sb("to_f", [128, NT])
    to_u = st.sb("to_u", [128, NT], U32)
    from_u = st.sb("from_u", [128, NT], U32)
    NB = 4
    w1 = [st.sb(f"w1_{i}", [128, F]) for i in range(NB)]
    w2 = [st.sb(f"w2_{i}", [128, FC, D]) for i in range(NB)]
    xe = [st.sb(f"xe{i}", [128, ST, D]) for i in range(NB)]
    xeT = [st.sb(f"xeT{i}", [128, CAP]) for i in range(2)]
    hT = [st.sb(f"hT{i}", [128, FC, CAP]) for i in range(2)]
    ye = [st.sb(f"ye{i}", [128, ST, D]) for i in range(2)]
    yg = st.sb("yg", [128, NT, D])
    rps = st.ps("rps")
    eps_ = [st.ps(f"x{i}") for i in range(2)]
    hps = [st.ps(f"h{i}") for i in range(2)]
    yps = [st.ps(f"y{i}") for i in range(2)]
    turn_ps = [*eps_, *yps]
    set_up = st.sem("set_up")
    t_filled, xnT_done = [ln.sem("t_filled") for ln in lanes], [ln.sem("xnT_done") for ln in lanes]
    l_filled, l_left = [ln.sem("l_filled") for ln in lanes], [ln.sem("l_left") for ln in lanes]
    rstep, exped, hot_done, r_filled = st.sem("rstep"), st.sem("exped"), st.sem("hot_done"), st.sem("r_filled")
    zeroed, indexed, scattered = st.sem("zeroed"), st.sem("indexed"), st.sem("scattered")
    w_in = [st.sem(f"w_in{i}") for i in range(NB)]
    x_in = [st.sem(f"x_in{i}") for i in range(NB)]
    xe_filled, xeT_done, h_filled, h_done = st.sem("xe_filled"), st.sem("xeT_done"), st.sem("h_filled"), st.sem("h_done")
    y_filled, ye_done = st.sem("y_filled"), st.sem("ye_done")
    ye_out = [st.sem(f"ye_out{i}") for i in range(2)]
    gathered, added = st.sem("gathered"), st.sem("added")

    with nc.Block(f"{name}_block") as block:
        @block.sync
        def _(sp):
            sp.wait_ge(set_up, 1)
            sp.dma_start(slots.rearrange("(t p) d -> p t d", p=128), zeros[:, :, :]).then_inc(zeroed, 16)
            sp.sem_inc(y_filled, NB)
            sp.sem_inc(xe_filled, NB)

            def weights(e, p):
                sp.wait_ge(y_filled, e + 1)
                sp.dma_start(w1[p][:, :], W1[e, :, :]).then_inc(w_in[p], 16)
                sp.dma_start(w2[p][:, :, :], W2[e, :, :].rearrange("(c p) d -> p c d", p=128)).then_inc(w_in[p], 16)

            def rows(e, p):
                sp.wait_ge(xe_filled, e + 1)
                sp.dma_start(xe[p][:, :, :], slots[bass.ds(CAP * e, CAP), :].rearrange("(t p) d -> p t d", p=128))\
                    .then_inc(x_in[p], 16)

            for e in range(NB):
                weights(e, e)
            sp.wait_ge(scattered, 16 * NT)
            for e in range(NB):
                rows(e, e)
            for e in range(NB, E):
                weights(e, e % NB)
                rows(e, e % NB)

        @block.gpsimd
        def _(pool):
            for nrm in norms:
                nrm.pool_setup(pool)
            pool.memset(zeros[:, :, :], 0.0).then_inc(set_up, 1)
            with pool.Fori(0, B // LANES) as b:
                for nrm in norms:
                    nrm.pool(pool, b)
            pool.wait_ge(zeroed, 16)
            pool.wait_ge(indexed, 2)
            for t in range(NT):
                pool.indirect_dma_start(slots, bass.IndirectOffsetOnAxis(ap=to_u[:, t:t + 1], axis=0), xn[:, t, :], None,
                                        bounds_check=E * CAP - 1, oob_is_err=False).then_inc(scattered, 16)
            for p in range(2):
                pool.wait_ge(ye_out[p], 16 * E // 2 + 16)
            for t in range(NT):
                pool.indirect_dma_start(yg[:, t, :], None, outs, bass.IndirectOffsetOnAxis(ap=from_u[:, t:t + 1], axis=0))\
                    .then_inc(gathered, 16)

        @block.tensor
        def _(pe):
            pe.wait_ge(loaded, 16)
            with pe.Fori(0, B // LANES) as b:
                for ln in range(LANES):
                    norms[ln].wait(pe, b)
                    pe.wait_ge(l_left[ln], b + 1)
                    for t in range(QT):
                        mm = pe.transpose(turn_ps[ln][:, t * 128:t * 128 + 128], norms[ln].xn[:, t, :], ident[:, :])
                    mm.then_inc(t_filled[ln], 1)
                for ln in range(LANES):
                    pe.wait_ge(xnT_done[ln], b + 1)
                    for t in range(QT):
                        mm = pe.matmul(turn_ps[ln][:, S + t * E:S + t * E + E], xnT[ln][:, t * 128:t * 128 + 128], w("r"),
                                       start=True, stop=True)
                    mm.then_inc(l_filled[ln], 1)
            pe.wait_ge(hot_done, 2)
            pe.matmul(rps[:, 0:NT * E], below_b[:, :], hotb[:, :, :], start=True, stop=False)
            for t in range(NT - 1):
                n = NT - 1 - t
                mm = pe.matmul(rps[:, (t + 1) * E:NT * E].rearrange("p (t e) -> p t e", e=E), g["onesb"][:, :],
                               hotb[:, t, :].unsqueeze(1).to_broadcast([128, n, E]), start=False, stop=(t == NT - 2))
            mm.then_inc(r_filled, 1)

            def turn(m, p):
                pe.wait_ge(x_in[p], 16 * m + 16)
                for t in range(ST):
                    mm = pe.transpose(eps_[p % 2][:, t * 128:t * 128 + 128], xe[p][:, t, :], ident[:, :])
                mm.then_inc(xe_filled, 1)

            def experts(m, last):
                for p in range(NB):
                    e = NB * m + p
                    if not (last and p == NB - 1):
                        turn(m + (p + 1) // NB, (p + 1) % NB)
                    pe.wait_ge(xeT_done, e + 1)
                    pe.wait_ge(w_in[p], 32 * m + 32)
                    for n in range(2):
                        pe.wait_ge(h_done, 2 * e + n + 1)
                        for j in range(2):
                            c = 2 * n + j
                            mm = pe.matmul(hps[n][:, j * CAP:(j + 1) * CAP], w1[p][:, c * 128:c * 128 + 128],
                                           xeT[p % 2][:, :], start=True, stop=True)
                        mm.then_inc(h_filled, 1)
                    pe.wait_ge(h_done, 2 * e + 2 + 2)
                    pe.wait_ge(ye_done, e + 1)
                    for t in range(ST):
                        for c in range(FC):
                            mm = pe.matmul(yps[p % 2][:, t * D:t * D + D], hT[p % 2][:, c, t * 128:t * 128 + 128],
                                           w2[p][:, c, :], start=(c == 0), stop=(c == FC - 1))
                    mm.then_inc(y_filled, 1)

            turn(0, 0)
            with pe.Fori(0, E // NB - 1) as m:
                experts(m, False)
            experts(E // NB - 1, True)

        @block.scalar
        def _(act):
            act.sem_inc(h_done, 2)
            act.sem_inc(ye_done, 2)
            for ln in range(LANES):
                act.sem_inc(l_left[ln], 1)
            with act.Fori(0, B // LANES) as b:
                for ln in range(LANES):
                    act.wait_ge(t_filled[ln], b + 1)
                    act.activation(xnT[ln][:, :], turn_ps[ln][:, 0:S], ACT.Copy).then_inc(xnT_done[ln], 1)
            act.wait_ge(rstep, 2)
            act.activation(work[:, :, :], work[:, :, :], ACT.Exp).then_inc(exped, 1)
            with act.Fori(0, E // 2) as m:
                for p in range(2):
                    e = 2 * m + p
                    act.wait_ge(xe_filled, e + 1 + NB)
                    act.activation(xeT[p][:, :], eps_[p][:, 0:CAP], ACT.Copy).then_inc(xeT_done, 1)
                    act.wait_ge(y_filled, e + NB - 1)
                    for n in range(2):
                        act.wait_ge(h_filled, 2 * e + n + 1)
                        act.activation(hT[p][:, 2 * n:2 * n + 2, :], hps[n][:, :].rearrange("p (c s) -> p c s", c=2),
                                       ACT.Relu).then_inc(h_done, 1)
                    act.wait_ge(ye_done, e + 1 + 2)
                    act.dma_start(outs[bass.ds(CAP * e, CAP), :].rearrange("(t p) d -> p t d", p=128), ye[p][:, :, :])\
                        .then_inc(ye_out[p], 16)

        @block.vector
        def _(v):
            v.wait_ge(loaded, 16)
            v.sem_inc(ye_out[0], 16)
            v.sem_inc(ye_out[1], 16)
            with v.Fori(0, B // LANES) as b:
                for nrm in norms:
                    nrm.take_moments(v, b)
                for nrm in norms:
                    nrm.norm_rows(v, b)
                for ln in range(LANES):
                    norms[ln].wait(v, b)
                    v.tensor_scalar(xn[:, bass.ds(QT * lanes[ln].batch(b), QT), :], norms[ln].xn[:, :, :], 1.0, None,
                                    ALU.mult)
                for ln in range(LANES):
                    v.wait_ge(l_filled[ln], b + 1)
                    v.tensor_scalar(logit[:, bass.ds(QT * lanes[ln].batch(b), QT), :],
                                    turn_ps[ln][:, S:S + QT * E].rearrange("p (t e) -> p t e", e=E), 1.0,
                                    None, ALU.mult).then_inc(l_left[ln], 1)
            for ln in range(LANES):
                v.wait_ge(l_left[ln], B // LANES + 1)
            v.tensor_reduce(lmax[:, :], logit[:, :, :], AX.X, ALU.max).then_inc(rstep, 1)
            v.wait_ge(rstep, 1)
            v.tensor_tensor(work[:, :, :], logit[:, :, :], lmax[:, :].unsqueeze(2).to_broadcast([128, NT, E]),
                            ALU.subtract).then_inc(rstep, 1)
            v.wait_ge(exped, 1)
            v.tensor_reduce(esum[:, :], work[:, :, :], AX.X, ALU.add).then_inc(rstep, 1)
            v.tensor_reduce(lmax[:, :], work[:, :, :], AX.X, ALU.max).then_inc(rstep, 1)
            v.wait_ge(rstep, 4)
            v.reciprocal(prob[:, :], esum[:, :]).then_inc(rstep, 1)
            v.tensor_tensor(cand[:, :, :], work[:, :, :], lmax[:, :].unsqueeze(2).to_broadcast([128, NT, E]), ALU.is_lt)\
                .then_inc(rstep, 1)
            v.wait_ge(rstep, 6)
            v.scalar_tensor_tensor(hot[:, :, :].rearrange("p t e -> p (t e)"), cand[:, :, :].rearrange("p t e -> p (t e)"),
                                   float(E), w("expert"), ALU.mult, ALU.add).then_inc(rstep, 1)
            v.wait_ge(rstep, 7)
            v.tensor_reduce(first[:, :], hot[:, :, :], AX.X, ALU.min).then_inc(rstep, 1)
            v.wait_ge(rstep, 8)
            v.tensor_tensor(cand[:, :, :], w("expert").rearrange("p (t e) -> p t e", e=E),
                            first[:, :].unsqueeze(2).to_broadcast([128, NT, E]), ALU.is_equal).then_inc(rstep, 1)
            v.wait_ge(rstep, 9)
            v.tensor_copy(hotb[:, :, :], cand[:, :, :]).then_inc(hot_done, 1)
            v.tensor_copy(below_b[:, :], w("below")).then_inc(hot_done, 1)
            v.wait_ge(r_filled, 1)
            v.tensor_tensor(work[:, :, :], rps[:, 0:NT * E].rearrange("p (t e) -> p t e", e=E), cand[:, :, :], ALU.mult)\
                .then_inc(rstep, 1)
            v.wait_ge(rstep, 10)
            v.tensor_reduce(rank[:, :], work[:, :, :], AX.X, ALU.add).then_inc(rstep, 1)
            v.wait_ge(rstep, 11)
            v.tensor_scalar(keep[:, :], rank[:, :], float(CAP), None, ALU.is_lt).then_inc(rstep, 1)
            v.scalar_tensor_tensor(slot[:, :], first[:, :], float(CAP), rank[:, :], ALU.mult, ALU.add).then_inc(rstep, 1)
            v.wait_ge(rstep, 13)
            v.tensor_tensor(weight[:, :], prob[:, :], keep[:, :], ALU.mult).then_inc(rstep, 1)
            v.tensor_tensor(slotf[:, :], slot[:, :], keep[:, :], ALU.mult).then_inc(rstep, 1)
            v.tensor_scalar(to_f[:, :], keep[:, :], -float(E * CAP), float(E * CAP), ALU.mult, ALU.add).then_inc(rstep, 1)
            v.wait_ge(rstep, 16)
            v.tensor_tensor(to_u[:, :], to_f[:, :], slotf[:, :], ALU.add).then_inc(indexed, 1)
            v.tensor_copy(from_u[:, :], slotf[:, :]).then_inc(indexed, 1)
            with v.Fori(0, E // 2) as m:
                for p in range(2):
                    e = 2 * m + p
                    v.wait_ge(ye_out[p], 16 * m + 16)
                    v.wait_ge(y_filled, e + 1 + NB)
                    v.tensor_scalar(ye[p][:, :, :], yps[p][:, 0:ST * D].rearrange("p (t d) -> p t d", t=ST), 1.0, None,
                                    ALU.mult).then_inc(ye_done, 1)
            for t in range(NT):
                if t == 0:
                    v.wait_ge(gathered, 16 * NT)
                v.scalar_tensor_tensor(x[:, t, :], yg[:, t, :], weight[:, t:t + 1], x[:, t, :], ALU.mult, ALU.add)\
                    .then_inc(added, 1)
    st.close()


def L0_ffn(nc, g, wts):
    name = "l0f"
    x, ident = g["x"], g["ident"]
    E, F, F2 = 8, 512, 256
    FC = F // 128
    st = Stage(nc, name)
    NORM0, NORM1, PLAIN2 = (0, 4), (1, 5), (2, 6)
    order = [("xT",), ("route",)]
    order += [("up", e, n) for e in NORM0 for n in range(2)]
    order += [("z", e, t) for e in NORM0 for t in range(QT)]
    order += [("up", e, n) for e in NORM1 for n in range(2)] + [("mid", e) for e in NORM1]
    order += [("up", e, n) for e in PLAIN2 for n in range(2)]
    order += [("z", e, t) for e in NORM1 for t in range(QT)]
    order += [("flat", e, n) for e in PLAIN2 for n in range(2)]
    order += [("up", e, n) for e in (3, 7) for n in range(2)] + [("wT",), ("bias",)]
    order += [("zT", e, t) for e in NORM0 for t in range(QT)]
    DOWN = (3, 7, 2, 6, 0, 4, 1, 5)
    order += [("down", e) for e in DOWN[:6]]
    order += [("zT", e, t) for e in NORM1 for t in range(QT)]
    order += [("down", e) for e in DOWN[6:]]
    at = {label: k for k, label in enumerate(order)}
    R = Ring(st, "r", 8, len(order))

    w, loaded = wts.of, wts.loaded
    nrm = Norm(st, x)
    nrm2 = Norm(st, x, of=nrm)
    xnT = st.sb("xnT", [128, S])
    hT = st.sb("hT", [128, E, FC, S])
    flat = st.sb("flat", [128, 2, FC, S])
    mid = st.sb("mid", [128, 2, 2, S])
    z = st.sb("z", [128, 2, 4, F])
    zstats = st.sb("zstats", [128, 4, 6])
    zmv = st.sb("zmv", [128, 4, 2])
    zveps = st.sb("zveps", [128, 4])
    zrstd = st.sb("zrstd", [128, 4])
    zhalf = st.sb("zhalf", [128, 4])
    e_base = st.sb("e_base", [128, QT * E])
    lg = st.sb("lg", [128, QT, E])
    lmax = st.sb("lmax", [128, QT])
    ex = st.sb("ex", [128, QT, E])
    more = st.sb("more", [128, QT, E, E])
    same = st.sb("same", [128, QT, E, E])
    place = st.sb("place", [128, QT, E])
    wsum = st.sb("wsum", [128, QT])
    wrec = st.sb("wrec", [128, QT])
    wt = st.sb("wt", [128, QT, E])
    wT = st.sb("wT", [E, S])
    acc = st.sb("acc", [128, QT, D])

    consts = st.sem("consts")
    rt, powed, wt_done = st.sem("rt"), st.sem("powed"), st.sem("wt_done")
    zaggr, zveps_done, zrstd_done = st.sem("zaggr"), st.sem("zveps_done"), st.sem("zrstd_done")
    zn_done, zg_done, zb_done, zact_done = (st.sem(n) for n in ("zn_done", "zg_done", "zb_done", "zact_done"))
    acc_done, x_done = st.sem("acc_done"), st.sem("x_done")
    RS = 11

    def w_of(key, i, n):
        return w(key)[:, i * n:(i + 1) * n]

    def tile(e, t):
        return (0, QT * NORM0.index(e) + t) if e in NORM0 else (1, QT * NORM1.index(e) + t)

    with nc.Block(f"{name}_block") as block:
        @block.sync
        def _(sp):
            R.credit(sp)

        @block.gpsimd
        def _(pool):
            nrm.pool_setup(pool)
            nrm2.pool_setup(pool)
            pool.memset(zhalf[:, :], -0.5).then_inc(consts, 1)
            pool.memset(e_base[:, :], float(np.e)).then_inc(consts, 1)
            pool.wait_ge(consts, 2)
            pool.wait_ge(loaded, 16)
            nrm.pool(pool, 0)
            nrm2.pool(pool, 0)

            def batch(b, ahead):
                pool.wait_ge(rt, RS * b + 2)
                pool.tensor_tensor(ex[:, :, :].rearrange("p t e -> p (t e)"), e_base[:, :],
                                   lg[:, :, :].rearrange("p t e -> p (t e)"), ALU.pow).then_inc(powed, 1)
                for gr, experts in enumerate((NORM0, NORM1)):
                    pool.wait_ge(zveps_done, 2 * b + gr + 1)
                    pool.tensor_tensor(zrstd[:, :], zveps[:, :], zhalf[:, :], ALU.pow).then_inc(zrstd_done, 1)
                    for i in range(4):
                        n = 8 * b + 4 * gr + i + 1
                        zz = z[:, gr, i, :]
                        pool.wait_ge(zn_done, n)
                        pool.tensor_tensor(zz, zz, w_of(f"ln{gr}_g", i // QT, F), ALU.mult).then_inc(zg_done, 1)
                        pool.wait_ge(zg_done, n)
                        pool.tensor_tensor(zz, zz, w_of(f"ln{gr}_b", i // QT, F), ALU.add).then_inc(zb_done, 1)
                if ahead:
                    nrm.pool(pool, b + 1)
                    nrm2.pool(pool, b + 1)

            with pool.Fori(0, B - 1) as b:
                batch(b, True)
            batch(B - 1, False)

        @block.tensor
        def _(pe):
            pe.wait_ge(loaded, 16)
            with pe.Fori(0, B) as b:
                for k, label in enumerate(order):
                    kind, e = label[0], label[1] if len(label) > 1 else None
                    bank = R.bank(k)
                    if kind == "xT":
                        nrm2.wait(pe, b)
                        R.wait_free(pe, b, k)
                        for t in range(QT):
                            mm = pe.transpose(bank[:, t * 128:t * 128 + 128], nrm2.xn[:, t, :], ident[:, :])
                    if kind == "route":
                        R.wait_for(pe, b, [at["xT",]], k) if k >= R.n else R.wait_emptied(pe, b, at["xT",])
                        R.wait_free(pe, b, k)
                        for t in range(QT):
                            mm = pe.matmul(bank[:, t * E:t * E + E], xnT[:, t * 128:t * 128 + 128], w("router"),
                                           start=True, stop=True)
                    if kind == "up":
                        R.wait_free(pe, b, k)
                        for j in range(2):
                            c = FC * e + 2 * label[2] + j
                            mm = pe.matmul(bank[:, j * S:(j + 1) * S], w_of("up", c, 128), xnT[:, :], start=True, stop=True)
                    if kind == "z":
                        gr, i = tile(e, label[2])
                        t = label[2]
                        if gr == 0:
                            R.wait_for(pe, b, [at["up", e, n] for n in range(2)], k)
                            for c in range(FC):
                                mm = pe.matmul(bank[:, :], hT[:, e, c, t * 128:t * 128 + 128],
                                               w_of("spec0", FC * (i // QT) + c, F), start=(c == 0), stop=(c == FC - 1))
                        else:
                            R.wait_for(pe, b, [at["mid", e]], k)
                            for c in range(2):
                                mm = pe.matmul(bank[:, :], mid[:, i // QT, c, t * 128:t * 128 + 128],
                                               w_of("spec1b", 2 * (i // QT) + c, F), start=(c == 0), stop=(c == 1))
                    if kind == "mid":
                        R.wait_for(pe, b, [at["up", e, n] for n in range(2)], k)
                        for j in range(2):
                            for c in range(FC):
                                wc = w_of("spec1a", FC * NORM1.index(e) + c, F2)[:, j * 128:j * 128 + 128]
                                mm = pe.matmul(bank[:, j * S:(j + 1) * S], wc, hT[:, e, c, :], start=(c == 0),
                                               stop=(c == FC - 1))
                    if kind == "flat":
                        R.wait_for(pe, b, [at["up", e, n] for n in range(2)], k)
                        for j in range(2):
                            o = 2 * label[2] + j
                            for c in range(FC):
                                wc = w_of("spec2", FC * PLAIN2.index(e) + c, F)[:, o * 128:o * 128 + 128]
                                mm = pe.matmul(bank[:, j * S:(j + 1) * S], wc, hT[:, e, c, :], start=(c == 0),
                                               stop=(c == FC - 1))
                    if kind == "wT":
                        pe.wait_ge(wt_done, b + 1)
                        R.wait_free(pe, b, k)
                        for t in range(QT):
                            mm = pe.transpose(bank[0:E, t * 128:t * 128 + 128], wt[:, t, :], ident[:, :])
                    if kind == "bias":
                        R.wait_for(pe, b, [at["wT",]], k)
                        for t in range(QT):
                            mm = pe.matmul(bank[:, t * D:t * D + D], wT[:, t * 128:t * 128 + 128], w("down_b")[0:E, :],
                                           start=True, stop=True)
                    if kind == "zT":
                        gr, i = tile(e, label[2])
                        pe.wait_ge(zb_done if gr else zact_done, (8 * b + 4 + i + 1) if gr else (4 * b + i + 1))
                        R.wait_free(pe, b, k)
                        for c in range(FC):
                            mm = pe.transpose(bank[:, c * 128:c * 128 + 128], z[:, gr, i, c * 128:c * 128 + 128],
                                              ident[:, :])
                    if kind == "down":
                        if e in PLAIN2:
                            src, need = flat[:, PLAIN2.index(e), :, :], [at["flat", e, n] for n in range(2)]
                        elif e in (3, 7):
                            src, need = hT[:, e, :, :], [at["up", e, n] for n in range(2)]
                        else:
                            src, need = hT[:, e, :, :], [at["zT", e, t] for t in range(QT)]
                        R.wait_for(pe, b, need, k)
                        for t in range(QT):
                            for c in range(FC):
                                mm = pe.matmul(bank[:, t * D:t * D + D], src[:, c, t * 128:t * 128 + 128],
                                               w_of("down", FC * e + c, D), start=(c == 0), stop=(c == FC - 1))
                    mm.then_inc(R.full(k), 1)

        @block.scalar
        def _(act):
            act.wait_ge(loaded, 16)
            with act.Fori(0, B) as b:
                for k, label in enumerate(order):
                    kind, e = label[0], label[1] if len(label) > 1 else None
                    bank = R.bank(k)
                    if kind == "xT":
                        R.wait_filled(act, b, k)
                        act.activation(xnT[:, :], bank[:, 0:S], ACT.Identity, scale=w("ln_g"), bias=w("ln_b"))\
                            .then_inc(R.free(k), 1)
                    if kind in ("up", "mid", "flat"):
                        R.wait_filled(act, b, k)
                        for j in range(2):
                            src = bank[:, j * S:(j + 1) * S]
                            if kind == "up":
                                c = 2 * label[2] + j
                                dst, bias = hT[:, e, c, :], w("up_b")[:, FC * e + c:FC * e + c + 1]
                            elif kind == "mid":
                                m = NORM1.index(e)
                                dst, bias = mid[:, m, j, :], w("spec1a_b")[:, 2 * m + j:2 * m + j + 1]
                            else:
                                c, m = 2 * label[2] + j, PLAIN2.index(e)
                                dst, bias = flat[:, m, c, :], w("spec2_b")[:, FC * m + c:FC * m + c + 1]
                            a = act.activation(dst, src, ACT.Gelu, bias=bias)
                        a.then_inc(R.free(k), 1)
                    if kind == "wT":
                        R.wait_filled(act, b, k)
                        act.activation(wT[:, :], bank[0:E, 0:S], ACT.Copy).then_inc(R.free(k), 1)
                        for i in range(4):
                            act.wait_ge(zb_done, 8 * b + i + 1)
                            act.activation(z[:, 0, i, :], z[:, 0, i, :], ACT.Gelu).then_inc(zact_done, 1)
                    if kind == "zT":
                        t = label[2]
                        R.wait_filled(act, b, k)
                        act.activation(hT[:, e, :, t * 128:t * 128 + 128], bank[:, :].rearrange("p (c q) -> p c q", c=FC),
                                       ACT.Copy).then_inc(R.free(k), 1)

        @block.vector
        def _(v):
            v.wait_ge(loaded, 16)
            nrm.vector(v, 0)
            nrm2.vector(v, 0)

            def batch(b, ahead):
                k = at["route",]
                R.wait_filled(v, b, k)
                rl = R.bank(k)[:, 0:QT * E].rearrange("p (t e) -> p t e", e=E)
                v.tensor_reduce(lmax[:, :], rl, AX.X, ALU.max).then_inc(rt, 1)
                v.wait_ge(rt, RS * b + 1)
                v.tensor_tensor(lg[:, :, :], rl, lmax[:, :].unsqueeze(2).to_broadcast([128, QT, E]), ALU.subtract)\
                    .then_inc(rt, 1)
                v.wait_ge(rt, RS * b + 2)
                v.sem_inc(R.free(k), 1)
                v.wait_ge(powed, b + 1)
                for t in range(QT):
                    them = ex[:, t, :].unsqueeze(1).to_broadcast([128, E, E])
                    me = ex[:, t, :].unsqueeze(2).to_broadcast([128, E, E])
                    v.tensor_tensor(more[:, t, :, :], them, me, ALU.is_gt)
                    v.tensor_tensor(same[:, t, :, :], them, me, ALU.is_equal).then_inc(rt, 1)
                v.wait_ge(rt, RS * b + 4)
                for t in range(QT):
                    v.tensor_tensor(same[:, t, :, :], same[:, t, :, :], w("earlier").rearrange("p (j i) -> p j i", i=E),
                                    ALU.mult).then_inc(rt, 1)
                v.wait_ge(rt, RS * b + 6)
                v.tensor_tensor(more[:, :, :, :].rearrange("p t j i -> p (t j i)"),
                                more[:, :, :, :].rearrange("p t j i -> p (t j i)"),
                                same[:, :, :, :].rearrange("p t j i -> p (t j i)"), ALU.add).then_inc(rt, 1)
                v.wait_ge(rt, RS * b + 7)
                v.tensor_reduce(place[:, :, :].rearrange("p t j -> p (t j)"),
                                more[:, :, :, :].rearrange("p t j i -> p (t j) i"), AX.X, ALU.add).then_inc(rt, 1)
                v.wait_ge(rt, RS * b + 8)
                v.scalar_tensor_tensor(place[:, :, :], place[:, :, :], 2.0, ex[:, :, :], ALU.is_lt, ALU.mult)\
                    .then_inc(rt, 1)
                v.wait_ge(rt, RS * b + 9)
                v.tensor_reduce(wsum[:, :], place[:, :, :], AX.X, ALU.add).then_inc(rt, 1)
                v.wait_ge(rt, RS * b + 10)
                v.reciprocal(wrec[:, :], wsum[:, :]).then_inc(rt, 1)
                v.wait_ge(rt, RS * b + 11)
                v.tensor_tensor(wt[:, :, :], place[:, :, :], wrec[:, :].unsqueeze(2).to_broadcast([128, QT, E]), ALU.mult)\
                    .then_inc(wt_done, 1)
                for gr, experts in enumerate((NORM0, NORM1)):
                    for i in range(4):
                        k = at["z", experts[i // QT], i % QT]
                        R.wait_filled(v, b, k)
                        v.tensor_tensor(z[:, gr, i, :], R.bank(k)[:, :], w_of(f"zbias{gr}", i // QT, F), ALU.add)\
                            .then_inc(R.free(k), 1)
                    for i in range(4):
                        R.wait_emptied(v, b, at["z", experts[i // QT], i % QT])
                        v.bn_stats(zstats[:, i, :], z[:, gr, i, :])
                    v.drain()
                    for i in range(4):
                        v.bn_aggr(zmv[:, i, :], zstats[:, i, :]).then_inc(zaggr, 1)
                    v.wait_ge(zaggr, 8 * b + 4 * gr + 4)
                    v.tensor_scalar(zveps[:, :], zmv[:, :, 1], EPS, None, ALU.add).then_inc(zveps_done, 1)
                    v.wait_ge(zrstd_done, 2 * b + gr + 1)
                    for i in range(4):
                        v.tensor_scalar(z[:, gr, i, :], z[:, gr, i, :], zmv[:, i, 0:1], zrstd[:, i:i + 1],
                                        ALU.subtract, ALU.mult).then_inc(zn_done, 1)
                k = at["bias",]
                R.wait_filled(v, b, k)
                v.tensor_tensor(acc[:, :, :], R.bank(k)[:, 0:QT * D].rearrange("p (t d) -> p t d", t=QT), nrm.xn[:, :, :],
                                ALU.add).then_inc(R.free(k), 1)
                R.wait_emptied(v, b, k)
                if ahead:
                    nrm.vector(v, b + 1)
                    nrm2.vector(v, b + 1)
                for n, e in enumerate(DOWN):
                    k = at["down", e]
                    R.wait_filled(v, b, k)
                    for t in range(QT):
                        if n > 0:
                            v.wait_ge(acc_done, QT * (E * b + n - 1) + t + 1)
                        v.scalar_tensor_tensor(acc[:, t, :], R.bank(k)[:, t * D:t * D + D], wt[:, t, e:e + 1], acc[:, t, :],
                                               ALU.mult, ALU.add).then_inc(acc_done, 1)
                    v.wait_ge(acc_done, QT * (E * b + n + 1))
                    v.sem_inc(R.free(k), 1)
                v.tensor_tensor(x[:, bass.ds(QT * b, QT), :], x[:, bass.ds(QT * b, QT), :], acc[:, :, :], ALU.add)\
                    .then_inc(x_done, 1)

            with v.Fori(0, B - 1) as b:
                batch(b, True)
            batch(B - 1, False)
    st.close()


def heads_on(rows, head_rows, width):
    return (np.arange(rows)[:, None] // head_rows == np.arange(width)[None, :]).astype(np.float32)


def turned(wt, d):
    n = wt.shape[1] // d
    a = wt.reshape(wt.shape[0], n, 2, d // 2)
    return np.ascontiguousarray(a[:, :, ::-1, :]).reshape(wt.shape[0], n * d)


def rope_tables(d):
    half = d // 2
    inv = (1.0 / 10000.0 ** (np.arange(half, dtype=np.float32) / half)).astype(np.float32)
    ang = np.arange(S, dtype=np.float32)[None, :] * inv[:, None]
    f = np.arange(128) % d
    sign = np.where(f < half, -1.0, 1.0)[:, None]
    return np.cos(ang)[f % half].astype(np.float32), (np.sin(ang)[f % half] * sign).astype(np.float32)


def spread_o(wo, d, groups):
    mw = 128 * groups // H
    a = np.zeros((128, groups, D), np.float32)
    for h in range(H):
        gr, j = divmod(h, H // groups)
        a[mw * j:mw * j + d, gr, :] = wo[h * d:(h + 1) * d]
    return a.reshape(128, groups * D)


def ones_on():
    a = np.zeros((128, 2, 32), np.float32)
    for gr in range(2):
        for j in range(2):
            a[SC * j:SC * j + SC, gr, 16 * gr + 8 * j:16 * gr + 8 * j + 8] = 1
    return a.reshape(128, 64)


def pack(parts):
    at, n = {}, 0
    for key, a in parts.items():
        at[key] = (n, a.shape[1])
        n += a.shape[1]
    return np.concatenate([np.asarray(a, np.float32) for a in parts.values()], 1), at


def pack_L3_attn(i):
    wk = np.tile(i["L3_attn_wk"], (1, 4))
    wv = np.tile(i["L3_attn_wv"], (1, 4))
    cos, sin = rope_tables(8)
    return pack({"q": i["L3_attn_wq"], "qr": turned(i["L3_attn_wq"], 8), "k": wk, "kr": turned(wk, 8), "v": wv,
                 "o": i["L3_attn_wo"], "cos": cos, "sin": sin, "kmask": heads_on(128, 8, 16)})


def pack_L0_attn(i):
    h, r = np.arange(256) // 16, np.arange(256) % 16
    rows = 8 * h + r % 8
    inv = (10000.0 ** -(np.arange(8, dtype=np.float32) / 8)).astype(np.float32)
    ang = (np.arange(S, dtype=np.float32)[None, :] * inv[:, None]).astype(np.float32)[r[:128] % 8]
    is_cos = (r[:128] < 8)[:, None]
    return pack({"q": i["L0_attn_wq"].T[:, rows], "k": i["L0_attn_wk"].T[:, rows], "v": i["L0_attn_wv"].T,
                 "o": i["L0_attn_wo"].T, "cos": np.where(is_cos, np.cos(ang), np.sin(ang)),
                 "turn": np.where(is_cos, -np.sin(ang), np.cos(ang)),
                 "bias": i["L0_attn_pope_bias"].reshape(-1)[rows].reshape(2, 128).T, "kmask": heads_on(128, 16, 8)})


def pack_L2_attn(i):
    wk = np.concatenate([i["L2_attn_Wk"].T[:, 64 * g:64 * g + 64] for g in (0, 0, 1, 1, 2, 2, 3, 3)], 1)
    cos, sin = rope_tables(64)
    return pack({"q": i["L2_attn_Wq"].T, "qr": turned(i["L2_attn_Wq"].T, 64), "k": wk, "kr": turned(wk, 64),
                 "v": i["L2_attn_Wv"].T, "g": np.concatenate([i["L2_attn_Wg_slc"].T, i["L2_attn_Wg_swa"].T], 1),
                 "o": spread_o(i["L2_attn_Wo"].T, 64, 8), "cos": cos, "sin": sin, "kmask": heads_on(128, 64, 2)})


def pairs_o(wo):
    return wo.reshape(2, 4, 16, D).transpose(1, 0, 2, 3).reshape(128, D)


def rows_of(a):
    return np.broadcast_to(a[None, :], (128, a.shape[0]))


def below(a):
    return np.concatenate([a, np.zeros((128 - a.shape[0], a.shape[1]), np.float32)], 0)


def pack_L1_xattn(i):
    kv, kvb = i["L1_xattn_kv_w"].T, i["L1_xattn_kv_b"]
    return pack({"q": i["L1_xattn_q_w"].T, "qb": i["L1_xattn_q_b"][:, None], "k": kv[:, :D], "kb": kvb[:D, None],
                 "v": kv[:, D:], "vb": rows_of(kvb[D:]), "o": pairs_o(i["L1_xattn_proj_w"].T),
                 "ob": rows_of(i["L1_xattn_proj_b"]), "kmask": heads_on(128, 8, 16), "ones": ones_on()})


def pack_L2_xattn(i):
    p = "L2_xattn_"
    return pack({"q": i[p + "Wq"].T, "qb": i[p + "bq"][:, None], "k": i[p + "Wk"].T, "kb": i[p + "bk"][:, None],
                 "v": i[p + "Wv"].T, "vb": rows_of(i[p + "bv"]), "o": pairs_o(i[p + "Wo"].T),
                 "ob": rows_of(i[p + "bo"]), "kmask": heads_on(128, 8, 16), "ones": ones_on(),
                 "w1": rows_of(i[p + "w1"].T.reshape(-1)), "b1": below(i[p + "b1"][:, None]),
                 "w2": below(i[p + "w2"].T), "b2": below(i[p + "b2"][:, None]),
                 "w3": below(np.broadcast_to(i[p + "w3"].T, (64, 128))), "b3": rows_of(i[p + "b3"])})


def pack_L0_xattn(i):
    p = "L0_xattn_"
    a, at = pack({"q": i[p + "W_q"].T, "qb": i[p + "b_q"][:, None], "k": i[p + "W_k"].T, "kb": i[p + "b_k"][:, None],
                  "v": i[p + "W_v"].T, "vb": rows_of(i[p + "b_v"])})
    return {"L0_xattn": a, "mask_L0": i["mask_SxS2_bk1"]}, at


def pack_L1_attn(i):
    p = "L1_attn_"
    return pack({"A": i[p + "A_log"], "B": i[p + "B_p"], "C": i[p + "C_p"], "D": i[p + "D_p"][:, None],
                 "dt": i[p + "W_dt"].T, "bdt": i[p + "b_dt"][:, None]})


def chunks(a):
    n = a.shape[0] // 128
    return a.reshape(n, 128, -1).transpose(1, 0, 2).reshape(128, -1)


def pack_L1_ffn(i):
    return pack({"gate": i["L1_ffn_w_gate"].T, "up": i["L1_ffn_w_up"].T, "down": chunks(i["L1_ffn_w_down"].T)})


def pack_L2_ffn(i):
    p = "L2_ffn_"
    before = np.concatenate([np.arange(S)[None, :] < 128 * t + np.arange(128)[:, None] for t in range(QT)], 1)
    return pack({"gate": np.broadcast_to(i[p + "Wg"], (128, 128)), "q": i[p + "Wq"], "k": i[p + "Wk"],
                 "v": i[p + "Wv"], "o": i[p + "Wo"], "kmask": heads_on(128, 8, 16),
                 "ones": np.tile(np.repeat([1, 0], [8, 32]), (128, 4)),
                 "before": before, "iota": rows_of(np.arange(S // 2))})


def pack_L3_xattn(i):
    p = "L3_xattn_"
    return pack({"q": i[p + "Wq"], "k": i[p + "Wkv"][:, :1024], "v": i[p + "Wkv"][:, 1024:], "o": chunks(i[p + "Wo"]),
                 "ob": rows_of(i[p + "bo"]), "g1": i[p + "g1"][:, None], "b1": i[p + "b1"][:, None],
                 "g2": i[p + "g2"][:, None], "b2": i[p + "b2"][:, None]})


def pack_L3_ffn(i):
    a, at = pack({"r": i["L3_ffn_Wr"], "expert": rows_of(np.tile(np.arange(8), NT)),
                  "below": np.arange(128)[:, None] < np.arange(128)[None, :]})
    return {"L3_ffn": a, "L3_ffn_W1": i["L3_ffn_W1"], "L3_ffn_W2": i["L3_ffn_W2"]}, at


def pack_L0_ffn(i):
    p = "L0_ffn_"
    E = 8
    of = lambda a: np.concatenate(list(a), 1)
    cols = lambda a: a.reshape(-1, 128).T
    return pack({
        "up": of(i[p + "up_W"]), "down": of(chunks(a) for a in i[p + "down_W"]),
        "spec0": of(chunks(a) for a in i[p + "spec0_W"]), "spec1a": of(chunks(a) for a in i[p + "spec1a_W"]),
        "spec1b": of(chunks(a) for a in i[p + "spec1b_W"]), "spec2": of(chunks(a) for a in i[p + "spec2_W"]),
        "up_b": cols(i[p + "up_b"]), "spec1a_b": cols(i[p + "spec1a_b"]), "spec2_b": cols(i[p + "spec2_b"]),
        "zbias0": rows_of(i[p + "spec0_b"].reshape(-1)), "zbias1": rows_of(i[p + "spec1b_b"].reshape(-1)),
        "ln0_g": rows_of(i[p + "ln0_g"].reshape(-1)), "ln0_b": rows_of(i[p + "ln0_b"].reshape(-1)),
        "ln1_g": rows_of(i[p + "ln1_g"].reshape(-1)), "ln1_b": rows_of(i[p + "ln1_b"].reshape(-1)),
        "ln_g": i[p + "ln_g"][:, None], "ln_b": i[p + "ln_b"][:, None], "router": i[p + "router_w"],
        "down_b": below(i[p + "down_b"]),
        "earlier": rows_of((np.arange(E)[None, :] < np.arange(E)[:, None]).reshape(-1))})


SPEC_L3 = dict(d=8, groups=4, causal=True, qchunks=1, kchunks=1, heads_of_kchunk=16, kvheads=16, gates=0, rope=True)
SPEC_L0 = dict(d=8, groups=4, causal=False, qchunks=2, kchunks=2, heads_of_kchunk=8, kvheads=16, gates=0, rope=False)
SPEC_L2 = dict(d=64, groups=8, causal=True, qchunks=8, kchunks=4, heads_of_kchunk=2, kvheads=4, gates=1, rope=True)
STAGES = {
    "L0_attn": (lambda nc, g, w: self_attention(nc, g, "l0a", w, SPEC_L0), pack_L0_attn),
    "L0_xattn": (L0_xattn, pack_L0_xattn),
    "L0_ffn": (L0_ffn, pack_L0_ffn),
    "L1_attn": (L1_attn, pack_L1_attn),
    "L1_xattn": (lambda nc, g, w: cross_attention(nc, g, "l1x", w, "plain"), pack_L1_xattn),
    "L1_ffn": (L1_ffn, pack_L1_ffn),
    "L2_attn": (lambda nc, g, w: self_attention(nc, g, "l2a", w, SPEC_L2), pack_L2_attn),
    "L2_xattn": (L2_xattn, pack_L2_xattn),
    "L2_ffn": (L2_ffn, pack_L2_ffn),
    "L3_attn": (lambda nc, g, w: self_attention(nc, g, "l3a", w, SPEC_L3), pack_L3_attn),
    "L3_xattn": (L3_xattn, pack_L3_xattn),
    "L3_ffn": (L3_ffn, pack_L3_ffn),
}
TOGETHER = (("L0_attn",), ("L0_xattn", "L0_ffn"),
            ("L1_attn", "L1_xattn", "L1_ffn", "L2_attn", "L2_xattn", "L2_ffn", "L3_attn", "L3_xattn", "L3_ffn"))


def program(nc, stages, dram, ats, x_in, out):
    with ExitStack() as ctx:
        g = {}

        def kept(name, shape, dt=F32):
            g[name] = ctx.enter_context(nc.sbuf_tensor(f"sb_{name}", shape, dt))
            return g[name]

        x = kept("x", [128, NT + QT * MAX_LANES, D])
        ident = kept("ident", [128, 128])
        identb = kept("identb", [128, 128], BF16)
        onesb = kept("onesb", [128, 128], BF16)
        tri = kept("tri", [128, 128], BF16)
        pad = kept("pad", [128, B, SC], BF16)
        hide = kept("hide", [128, B, SC], BF16)
        mask8 = kept("mask8", [128, QT, SC], U8)
        ctxT = kept("ctxT", [128, B, SC])
        minus_mean = kept("minus_mean", [128, 1])
        st = Stage(nc, "in")
        trif = st.sb("trif", [128, 128])
        raw = st.sb("raw", [128, B * SC // 128, D])
        masks = st.sb("masks", [128, 2, B, SC], U8)
        ps = st.ps("ps")
        mask_in = st.sem("mask_in")
        landed, cast, turned_in, out_of = st.sem("landed"), st.sem("cast"), st.sem("turned"), st.sem("out_of")
        with nc.Block("in_block") as block:
            @block.sync
            def _(sp):
                sp.dma_start(x[:, 0:NT, :], x_in.rearrange("(t p) d -> p t d", p=128)).then_inc(landed, 16)
                sp.dma_start(ident[:, :], dram["ident"]).then_inc(landed, 16)
                sp.dma_start(trif[:, :], dram["tri"]).then_inc(landed, 16)
                sp.dma_start(raw[:, :, :], dram["ctx"].rearrange("(t p) d -> p t d", p=128)).then_inc(landed, 16)
                if "mask_L0" in dram:
                    sp.dma_start(mask8[:, :, :], dram["mask_L0"].rearrange("(t p) k -> p t k", p=128))\
                        .then_inc(mask_in, 16)
                for n, key in enumerate(("mask_pad", "mask_keep")):
                    sp.dma_start(masks[:, n, :, :], dram[key].partition_broadcast(128)).then_inc(landed, 16)

            @block.tensor
            def _(pe):
                pe.wait_ge(landed, 96)
                for t in range(B * SC // 128):
                    mm = pe.transpose(ps[:, t * 128:t * 128 + 128], raw[:, t, :], ident[:, :])
                mm.then_inc(turned_in, 1)

            @block.vector
            def _(v):
                if "mask_L0" in dram:
                    v.wait_ge(mask_in, 16)
                v.memset(x[:, NT:, :], 0.0)
                v.memset(onesb[:, :], 1.0).then_inc(cast, 1)
                v.memset(minus_mean[:, :], -1.0 / SC).then_inc(cast, 1)
                v.wait_ge(landed, 96)
                v.tensor_copy(identb[:, :], ident[:, :]).then_inc(cast, 1)
                v.tensor_copy(tri[:, :], trif[:, :]).then_inc(cast, 1)
                v.tensor_scalar(pad[:, :, :], masks[:, 0, :, :], MASKED, None, ALU.mult).then_inc(cast, 1)
                v.tensor_scalar(hide[:, :, :], masks[:, 1, :, :], -MASKED, MASKED, ALU.mult, ALU.add)\
                    .then_inc(cast, 1)
                v.wait_ge(turned_in, 1)
                v.tensor_copy(ctxT[:, :, :].rearrange("p b k -> p (b k)"), ps[:, :]).then_inc(out_of, 1)
        st.close()
        g["dram"] = dram
        for group in TOGETHER:
            group = [s for s in group if s in stages]
            if not group:
                continue
            weights = {s: Weights(nc, s, dram[s], ats[s]) for s in reversed(group)}
            with nc.Block(f"fetch_{group[0]}") as block:
                @block.sync
                def _(sp):
                    for s in group:
                        weights[s].fetch(sp)
            for s in group:
                STAGES[s][0](nc, g, weights[s])
                weights[s].close()
        st = Stage(nc, "out")
        stored = st.sem("stored")
        with nc.Block("out_block") as block:
            @block.sync
            def _(sp):
                sp.dma_start(out.rearrange("(t p) d -> p t d", p=128), g["x"][:, 0:NT, :]).then_inc(stored, 16)
                sp.wait_ge(stored, 16)
        st.close()


def laid_out(inputs, stages):
    arrays = {
        "ident": np.eye(128, dtype=np.float32),
        "tri": np.where(np.arange(128)[None, :] > np.arange(128)[:, None], MASKED, 0).astype(np.float32),
        "ctx": np.ascontiguousarray(inputs["ctx_1024"].reshape(B * SC, D)),
        "mask_pad": inputs["mask_BxS2_bk0"],
        "mask_keep": inputs["mask_BxS2_bf1"],
        "x_in": np.ascontiguousarray(inputs["x"].reshape(B * S, D)),
    }
    ats = {}
    for s in stages:
        a, ats[s] = STAGES[s][1](inputs)
        arrays.update(a if isinstance(a, dict) else {s: a})
    return arrays, ats


def build(nc, arrays, ats, stages):
    dram = {n: nc.dram_tensor(n, list(a.shape), mybir.dt.from_np(a.dtype), kind="ExternalInput").ap()
            for n, a in arrays.items()}
    out = nc.dram_tensor("out", [B * S, D], F32, kind="ExternalOutput").ap()
    program(nc, stages, dram, ats, dram["x_in"], out)


def kernel(**inputs):
    import concourse.bacc as bacc
    from concourse.bass_utils import run_bass_kernel_spmd

    arrays, ats = laid_out({k: np.asarray(v) for k, v in inputs.items()}, list(STAGES))
    nc = bacc.Bacc("TRN2", target_bir_lowering=False, num_devices=1)
    build(nc, arrays, ats, list(STAGES))
    r = run_bass_kernel_spmd(nc, [arrays], core_ids=[0])
    return r.results[0]["out"].reshape(B, S, D)
```
